# Optimizing a Trainium2 kernel written in Bass

```python
import numpy as np
import jax
import jax.numpy as jnp

def _softmax(x, axis=-1):
    return jax.nn.softmax(x, axis=axis)

def _gelu(x):
    return jax.nn.gelu(x, approximate=True)

def _silu(x):
    return jax.nn.silu(x)

def _sigmoid(x):
    return jax.nn.sigmoid(x)

def _layernorm(x, axis=-1, eps=1e-05):
    m = jnp.mean(x, axis=axis, keepdims=True)
    v = jnp.var(x, axis=axis, keepdims=True)
    return (x - m) / jnp.sqrt(v + eps)

def _scatter_add(tgt, idx, src, axis=0):
    return tgt.at[idx].add(src)

def _segment_sum(src, seg, n):
    return jax.ops.segment_sum(src, seg, n)
kernel_name = 'mk_gnn_resnorm_d2_gnn_r8_9f5202'

def setup_inputs(seed: int=0):
    np.random.seed(seed)
    _w = jnp.asarray

    def _rec_inputs():
        import jax
        import jax.numpy as jnp
        _gk = jax.random.key(seed)
        x = -0.0003713 + 1 * jax.random.normal(jax.random.fold_in(_gk, 1), (6250, 128), jnp.float32)
        src = jax.random.randint(jax.random.fold_in(_gk, 2), (200000,), 0, 6250, jnp.int32)
        dst = jnp.minimum((6250 * jax.random.uniform(jax.random.fold_in(_gk, 3), (200000,)) ** 2.0).astype(jnp.int32), 49999)
        _o = jnp.argsort(dst, stable=True)
        src = src[_o]
        dst = dst[_o]
        edge_attr_128 = jax.random.uniform(jax.random.fold_in(_gk, 12), (200000, 128), jnp.float32, 0.0, 1)
        edge_weight = jax.random.uniform(jax.random.fold_in(_gk, 13), (200000,), jnp.float32, 0.0, 4.99999)
        return (x, src, dst, edge_attr_128, edge_weight)
    x, src, dst, edge_attr_128, edge_weight = _rec_inputs()

    def _L0_gnn_setup():
        import jax, jax.numpy as jnp
        import numpy as np
        N_NODES = 12500
        N_RAND_EDGES = 200000
        D = 128

        def _graph_conv(x, W, b, src, dst, norm_src, norm_dst, n_nodes, act):
            h = x @ W
            m = h[src] * norm_src[:, None]
            agg = jax.ops.segment_sum(m, dst, num_segments=n_nodes)
            out = agg * norm_dst[:, None] + b
            return jax.nn.relu(out) if act else out
        key = jax.random.key(seed)
        k_feat, k_src, k_dst, k_w1, k_w2, k_w3 = jax.random.split(key, 6)
        feats = jax.random.normal(k_feat, (N_NODES, D), dtype=jnp.float32)
        src_r = jax.random.randint(k_src, (N_RAND_EDGES,), 0, N_NODES, dtype=jnp.int64)
        dst_r = jax.random.randint(k_dst, (N_RAND_EDGES,), 0, N_NODES, dtype=jnp.int64)
        loops = jnp.arange(N_NODES, dtype=jnp.int64)
        src = jnp.concatenate([src_r, loops])
        dst = jnp.concatenate([dst_r, loops])
        scale = 1.0 / np.sqrt(D)
        W1 = jax.random.normal(k_w1, (D, D), dtype=jnp.float32) * scale
        W2 = jax.random.normal(k_w2, (D, D), dtype=jnp.float32) * scale
        W3 = jax.random.normal(k_w3, (D, D), dtype=jnp.float32) * scale
        b1 = jnp.zeros((D,), dtype=jnp.float32)
        b2 = jnp.zeros((D,), dtype=jnp.float32)
        b3 = jnp.zeros((D,), dtype=jnp.float32)
        return {'feats': feats, 'W1': W1, 'b1': b1, 'W2': W2, 'b2': b2, 'W3': W3, 'b3': b3, 'src': src, 'dst': dst}
    _L0_gnn_all = _L0_gnn_setup()
    _L0_gnn_in = {k: v for k, v in _L0_gnn_all.items() if k in ('W1', 'b1', 'W2', 'b2', 'W3', 'b3')}
    del _L0_gnn_all

    def _L1_gnn_setup():
        import jax, jax.numpy as jnp
        import numpy as np
        IN_FEATS = 128
        OUT_FEATS = 128
        N_NODES = 2500
        N_EDGES = 80000
        R_MIN, R_MAX = (0.0, 5.0)
        LN2 = 0.6931471805599453

        def ssp(x):
            return jax.nn.softplus(x) - LN2
        key = jax.random.key(seed)
        ks = jax.random.split(key, 12)
        h = jax.random.normal(ks[0], (N_NODES, IN_FEATS), dtype=jnp.float32)
        edge_feat = jax.random.uniform(ks[1], (N_EDGES, IN_FEATS), dtype=jnp.float32)
        dist = jax.random.uniform(ks[2], (N_EDGES,), dtype=jnp.float32) * R_MAX
        src = jax.random.randint(ks[3], (N_EDGES,), 0, N_NODES)
        dst = jax.random.randint(ks[4], (N_EDGES,), 0, N_NODES)
        s = 0.1
        W1 = jax.random.normal(ks[5], (IN_FEATS, IN_FEATS), dtype=jnp.float32) * s
        b1 = jnp.zeros((IN_FEATS,), dtype=jnp.float32)
        W2 = jax.random.normal(ks[6], (IN_FEATS, IN_FEATS), dtype=jnp.float32) * s
        b2 = jnp.zeros((IN_FEATS,), dtype=jnp.float32)
        W3 = jax.random.normal(ks[7], (IN_FEATS, OUT_FEATS), dtype=jnp.float32) * s
        b3 = jnp.zeros((OUT_FEATS,), dtype=jnp.float32)
        return {'h': h, 'edge_feat': edge_feat, 'dist': dist, 'src': src, 'dst': dst, 'W1': W1, 'b1': b1, 'W2': W2, 'b2': b2, 'W3': W3, 'b3': b3}
    _L1_gnn_all = _L1_gnn_setup()
    _L1_gnn_in = {k: v for k, v in _L1_gnn_all.items() if k in ('W1', 'b1', 'W2', 'b2', 'W3', 'b3')}
    del _L1_gnn_all
    return {'x': x, 'src': src, 'dst': dst, 'edge_attr_128': edge_attr_128, 'edge_weight': edge_weight, 'L0_gnn_W1': _L0_gnn_in['W1'], 'L0_gnn_b1': _L0_gnn_in['b1'], 'L0_gnn_W2': _L0_gnn_in['W2'], 'L0_gnn_b2': _L0_gnn_in['b2'], 'L0_gnn_W3': _L0_gnn_in['W3'], 'L0_gnn_b3': _L0_gnn_in['b3'], 'L1_gnn_W1': _L1_gnn_in['W1'], 'L1_gnn_b1': _L1_gnn_in['b1'], 'L1_gnn_W2': _L1_gnn_in['W2'], 'L1_gnn_b2': _L1_gnn_in['b2'], 'L1_gnn_W3': _L1_gnn_in['W3'], 'L1_gnn_b3': _L1_gnn_in['b3']}

def reference(x, src, dst, edge_attr_128, edge_weight, L0_gnn_W1, L0_gnn_b1, L0_gnn_W2, L0_gnn_b2, L0_gnn_W3, L0_gnn_b3, L1_gnn_W1, L1_gnn_b1, L1_gnn_W2, L1_gnn_b2, L1_gnn_W3, L1_gnn_b3):
    import jax
    import jax.numpy as jnp

    def _L0_gnn_ref(feats, W1, b1, W2, b2, W3, b3, src, dst):
        import jax, jax.numpy as jnp
        import numpy as np
        N_NODES = 12500
        N_RAND_EDGES = 200000
        D = 128

        def _graph_conv(x, W, b, src, dst, norm_src, norm_dst, n_nodes, act):
            h = x @ W
            m = h[src] * norm_src[:, None]
            agg = jax.ops.segment_sum(m, dst, num_segments=n_nodes)
            out = agg * norm_dst[:, None] + b
            return jax.nn.relu(out) if act else out
        n = feats.shape[0]
        ones = jnp.ones(src.shape[0], dtype=feats.dtype)
        deg_out = jnp.clip(jax.ops.segment_sum(ones, src, num_segments=n), 1.0)
        deg_in = jnp.clip(jax.ops.segment_sum(ones, dst, num_segments=n), 1.0)
        norm_src = jax.lax.rsqrt(deg_out)[src]
        norm_dst = jax.lax.rsqrt(deg_in)
        h = _graph_conv(feats, W1, b1, src, dst, norm_src, norm_dst, n, act=True)
        h = _graph_conv(h, W2, b2, src, dst, norm_src, norm_dst, n, act=True)
        h = _graph_conv(h, W3, b3, src, dst, norm_src, norm_dst, n, act=False)
        return h

    def _L1_gnn_ref(h, edge_feat, dist, src, dst, W1, b1, W2, b2, W3, b3):
        import jax, jax.numpy as jnp
        import numpy as np
        IN_FEATS = 128
        OUT_FEATS = 128
        N_NODES = 2500
        N_EDGES = 80000
        R_MIN, R_MAX = (0.0, 5.0)
        LN2 = 0.6931471805599453

        def ssp(x):
            return jax.nn.softplus(x) - LN2
        n_nodes = h.shape[0]
        centers = jnp.linspace(R_MIN, R_MAX, IN_FEATS, dtype=jnp.float32)
        delta = (R_MAX - R_MIN) / (IN_FEATS - 1)
        coeff = -0.5 / (delta * delta)
        bf = jnp.exp(coeff * (dist[:, None] - centers[None, :]) ** 2)
        bf = ssp(bf @ W1 + b1)
        bf = ssp(bf @ W2 + b2)
        cut = jnp.where(dist < R_MAX, 0.5 * (jnp.cos(jnp.pi * dist / R_MAX) + 1.0), 0.0)
        msg = h[src] * edge_feat * bf * cut[:, None]
        agg = jax.ops.segment_prod(msg, dst, num_segments=n_nodes)
        out = ssp(agg @ W3 + b3)
        return out
    x = _layernorm(x + _L0_gnn_ref(x, L0_gnn_W1, L0_gnn_b1, L0_gnn_W2, L0_gnn_b2, L0_gnn_W3, L0_gnn_b3, src, dst), axis=-1)
    x = _layernorm(x + _L1_gnn_ref(x, edge_attr_128, edge_weight, src, dst, L1_gnn_W1, L1_gnn_b1, L1_gnn_W2, L1_gnn_b2, L1_gnn_W3, L1_gnn_b3), axis=-1)
    return x

_drawn_inputs = setup_inputs


def setup_inputs(seed=0):
    import zlib

    import numpy as np

    out = dict(_drawn_inputs(seed))
    spreads = {'L0_gnn_b1': (0.0, 0.277),
     'L0_gnn_b2': (0.0, 0.1),
     'L0_gnn_b3': (0.0, 0.1),
     'L1_gnn_b1': (0.0, 0.1),
     'L1_gnn_b2': (0.0, 0.1),
     'L1_gnn_b3': (0.0, 0.1)}
    factors = {'edge_weight': 8.0, 'L0_gnn_W1': 7.991}
    for name, (base, spread) in spreads.items():
        noise = np.random.default_rng([zlib.crc32(name.encode()), seed]).standard_normal(out[name].shape)
        drawn = base * np.exp(spread * noise) if base else spread * noise
        out[name] = jnp.asarray(drawn.astype(out[name].dtype))
    for name, factor in factors.items():
        out[name] = (out[name] * factor).astype(out[name].dtype)
    return out
```

```python
import math

import numpy as np
import concourse.bass as bass
from concourse import mybir
from contextlib import ExitStack

F32 = mybir.dt.float32
BF16 = mybir.dt.bfloat16
I32 = mybir.dt.int32
ALU = mybir.AluOpType
ACT = mybir.ActivationFunctionType

P = 128
N = 6250
E = 200000
D = 128
NT = -(-N // P)
NP = NT * P
NW = NT + 1
CH = -(-E // P)
C4 = 4
BLK = P * C4
NB = -(-E // BLK)
EP = NB * BLK
U = 12
H = U // 2
ITS = -(-(CH + NT) // U)
STEPS = ITS * U
ST = -(-STEPS // P)
FULL = E // BLK
TAIL = E - FULL * BLK
PADNODE = 8191
RT = NT + 1
HG = 17
HB = EP // P // HG
CUTOFF = 5.0
LN2 = 0.6931471805599453
SOFT_MAX = 18.0
EPS = 1e-5
DELTA = CUTOFF / (D - 1)
AHEAD = 3
COEFF = -0.5 / (DELTA * DELTA)


def gnn(nc, x, src, dst, edge_attr, edge_weight, w1, b1, w2, b2, w3, b3, v1, c1, v2, c2, v3, c3, out):
    scratch = lambda name, shape, dt: nc.dram_tensor(name, shape, dt, kind="Internal").ap()
    src_d = scratch("src_padded", (EP,), I32)
    dst_d = scratch("dst_padded", (EP,), I32)
    prev_d = scratch("dst_of_previous_edge", (EP,), I32)
    wt_d = scratch("weight_padded", (EP,), F32)
    win_d = scratch("step_windows", (ST * P,), I32)
    row_d = scratch("row_starts", (RT * P,), F32)
    h_d = scratch("h_rows", (NP, D), F32)
    x1_d = scratch("x1_rows", (NP, D), F32)
    g_d = scratch("edge_filter", (EP, D), F32)
    run_d = scratch("running_products", (EP + 1, D), F32)
    ONES_ROW = EP
    src_rows = src_d.rearrange("(c e) -> c e", e=P)
    dst_rows = dst_d.rearrange("(c e) -> c e", e=P)

    outer = ExitStack()
    with outer:
        sb_in = lambda stack: (lambda name, shape, dt=F32: stack.enter_context(nc.sbuf_tensor(name, shape, dt)))
        sb = sb_in(outer)
        sem = lambda name: outer.enter_context(nc.semaphore(name))

        ident = sb("ident", [P, P])
        iota_f = sb("iota_f", [P, P])
        pcol = sb("pcol", [P, 1])
        steps_src = sb("steps_src", [P, ST * P], I32)
        steps_dst = sb("steps_dst", [P, ST * P])
        windows = sb("windows", [1, ST * P], I32)
        edge_src = sb("edge_src", [P, NB + AHEAD, C4], I32)
        edge_cut = sb("edge_cut", [P, NB, C4])
        edge_same = sb("edge_same", [P, NB, C4])
        edge_first = sb("edge_first", [P, NB, C4])
        last_row = sb("last_row", [P, NT], I32)
        norm_src = sb("norm_src", [P, NT])
        norm_dst = sb("norm_dst", [P, NP])
        banks = [outer.enter_context(nc.psum_tensor(f"bank{i}", [P, 512], F32)) for i in range(8)]

        with ExitStack() as ph:
            sbt = sb_in(ph)
            pad_i = sbt("pad_i", [1, BLK], I32)
            lead_i = sbt("lead_i", [1, 1], I32)
            pad_w = sbt("pad_w", [1, BLK])
            iota_i = sbt("iota_i", [P, P], I32)
            pcol_i = sbt("pcol_i", [P, 1], I32)
            ones_row = sbt("ones_row", [1, D])
            s_pads, s_iota, s_copied, s_const = sem("s_pads"), sem("s_iota"), sem("s_copied"), sem("s_const")
            with nc.Block() as block:
                @block.gpsimd
                def _(pool):
                    nc.gpsimd.memset(pad_i[:], PADNODE)
                    nc.gpsimd.memset(lead_i[:], -1)
                    nc.gpsimd.memset(ones_row[:], 1.0)
                    nc.gpsimd.memset(pad_w[:], 0.0).then_inc(s_pads, 1)
                    nc.gpsimd.iota(iota_i[:], [[1, P]], base=0, channel_multiplier=0)
                    nc.gpsimd.iota(pcol_i[:], [[1, 1]], base=0, channel_multiplier=1).then_inc(s_iota, 1)

                @block.vector
                def _(dve):
                    dve.wait_ge(s_iota, 1)
                    nc.vector.tensor_copy(iota_f[:], iota_i[:])
                    nc.vector.tensor_copy(pcol[:], pcol_i[:]).then_inc(s_const, 1)
                    dve.wait_ge(s_const, 1)
                    nc.vector.tensor_scalar(ident[:], iota_f[:], pcol[:, 0:1], None, ALU.is_equal)

                @block.sync
                def _(sp):
                    sp.dma_start(src_d[0:E].rearrange("(a b) -> a b", a=16),
                                 src.rearrange("(a b) -> a b", a=16)).then_inc(s_copied, 16)
                    for ap in (dst_d[0:E], prev_d[1:E + 1]):
                        sp.dma_start(ap.rearrange("(a b) -> a b", a=16),
                                     dst.rearrange("(a b) -> a b", a=16)).then_inc(s_copied, 16)
                    sp.dma_start(wt_d[0:E].rearrange("(a b) -> a b", a=16),
                                 edge_weight.rearrange("(a b) -> a b", a=16)).then_inc(s_copied, 16)
                    sp.wait_ge(s_pads, 1)
                    row = lambda ap: ap.rearrange("(a b) -> a b", a=1)
                    sp.dma_start(row(src_d[E:EP]), pad_i[:, 0:EP - E]).then_inc(s_copied, 16)
                    sp.dma_start(row(dst_d[E:EP]), pad_i[:, 0:EP - E]).then_inc(s_copied, 16)
                    sp.dma_start(row(prev_d[E + 1:EP]), pad_i[:, 0:EP - E - 1]).then_inc(s_copied, 16)
                    sp.dma_start(row(prev_d[0:1]), lead_i[:]).then_inc(s_copied, 16)
                    sp.dma_start(row(wt_d[E:EP]), pad_w[:, 0:EP - E]).then_inc(s_copied, 16)
                    sp.dma_start(run_d[ONES_ROW:ONES_ROW + 1, :], ones_row[:]).then_inc(s_copied, 16)
                    sp.wait_ge(s_copied, 10 * 16)

        with ExitStack() as ph:
            sbt = sb_in(ph)
            CR = EP // P
            first_i = sbt("first_i", [1, CR], I32)
            first_w = sbt("first_w", [1, CR], I32)
            chunk_no = sbt("chunk_no", [1, CR], I32)
            first_r = sbt("first_r", [1, CR])
            start_r = sbt("start_r", [1, CR])
            first_b = sbt("first_b", [P, CR])
            start_b = sbt("start_b", [P, CR])
            junk = sbt("junk", [P, CR])
            number_i = sbt("number_i", [P, RT], I32)
            number = sbt("number", [P, RT])
            chunk_f = sbt("chunk_f", [P, ST])
            chunk_i = sbt("chunk_i", [P, ST], I32)
            win_f = sbt("win_f", [P, ST])
            win_i = sbt("win_i", [P, ST], I32)
            base_f = sbt("base_f", [P, ST])
            rowc_f = sbt("rowc_f", [P, RT])
            rowc_i = sbt("rowc_i", [P, RT], I32)
            inrow = sbt("inrow", [P, RT])
            start_f = sbt("start_f", [P, RT])
            end_f = sbt("end_f", [P, NT])
            has_f = sbt("has_f", [P, NT])
            alt_f = sbt("alt_f", [P, NT])
            srows = sbt("srows", [P, ST, P], I32)
            drows = sbt("drows", [P, ST, P], I32)
            nrows = sbt("nrows", [P, 2, P], I32)
            s_first, s_ff, s_start, s_bc, s_num, s_numf = (sem(n) for n in
                ("s_first", "s_ff", "s_start", "s_bc", "s_num", "s_numf"))
            s_cnt, s_chunk, s_srows, s_rel, s_tp, s_tpc = (sem(n) for n in
                ("s_cnt", "s_chunk", "s_srows", "s_rel", "s_tp", "s_tpc"))
            s_win, s_wind, s_winl, s_link = (sem(n) for n in ("s_win", "s_wind", "s_winl", "s_link"))
            s_rowc, s_rowused = sem("s_rowc"), sem("s_rowused")
            s_nrows = [sem(f"s_nrows{i}") for i in range(2)]
            s_rs, s_rsd, s_rb, s_deg, s_sq = (sem(n) for n in ("s_rs", "s_rsd", "s_rb", "s_deg", "s_sq"))
            with nc.Block() as block:
                @block.sync
                def _(sp):
                    with nc.allow_non_contiguous_dma(reason="first dst of every chunk"):
                        sp.dma_start(first_i[:], dst_rows[:, 0:1].rearrange("c o -> o c")).then_inc(s_first, 16)
                    sp.wait_ge(s_win, 1)
                    with nc.allow_non_contiguous_dma(reason="small table"):
                        sp.dma_start(win_d.rearrange("(t p) -> p t", p=P), win_i[:]).then_inc(s_wind, 16)
                    sp.wait_ge(s_wind, 16)
                    sp.dma_start(windows[:], win_d.rearrange("(a b) -> a b", a=1)).then_inc(s_winl, 16)
                    sp.wait_ge(s_rs, 1)
                    with nc.allow_non_contiguous_dma(reason="small table"):
                        sp.dma_start(row_d.rearrange("(t p) -> p t", p=P), start_f[:]).then_inc(s_rsd, 16)
                    sp.wait_ge(s_rsd, 16)
                    rows = row_d.rearrange("(a b) -> a b", a=1)
                    sp.dma_start(norm_dst[:, :], rows[:, 1:NP + 1].to_broadcast([P, NP])).then_inc(s_rb, 16)
                    with nc.allow_non_contiguous_dma(reason="small table"):
                        sp.dma_start(end_f[:], row_d[1:NP + 1].rearrange("(t p) -> p t", p=P)).then_inc(s_rb, 16)
                    sp.wait_ge(s_winl, 16)
                    sp.wait_ge(s_rb, 32)

                @block.gpsimd
                def _(pool):
                    nc.gpsimd.iota(chunk_no[:], [[1, CR]], base=0, channel_multiplier=0)
                    nc.gpsimd.iota(number_i[:], [[P, RT]], base=0, channel_multiplier=1).then_inc(s_num, 1)
                    pool.wait_ge(s_start, 1)
                    nc.gpsimd.partition_broadcast(start_b[:], start_r[:])
                    nc.gpsimd.partition_broadcast(first_b[:], first_r[:]).then_inc(s_bc, 1)
                    pool.wait_ge(s_chunk, 1)
                    for t in range(ST):
                        for rows, table in ((srows, src_rows), (drows, dst_rows)):
                            pool.indirect_dma_start(out=rows[:, t, :], out_offset=None, in_=table,
                                                    in_offset=bass.IndirectOffsetOnAxis(ap=chunk_i[:, t:t + 1], axis=0)
                                                    ).then_inc(s_srows, 16)
                    pool.wait_ge(s_rowc, 1)
                    for t in range(RT):
                        if t >= 2:
                            pool.wait_ge(s_rowused, t - 1)
                        pool.indirect_dma_start(out=nrows[:, t % 2, :], out_offset=None, in_=dst_rows,
                                                in_offset=bass.IndirectOffsetOnAxis(ap=rowc_i[:, t:t + 1], axis=0)
                                                ).then_inc(s_nrows[t % 2], 16)

                @block.vector
                def _(dve):
                    links = [0]

                    def link(ins):
                        links[0] += 1
                        ins.then_inc(s_link, 1)
                        dve.wait_ge(s_link, links[0])

                    dve.wait_ge(s_num, 1)
                    dve.wait_ge(s_first, 16)
                    link(nc.vector.tensor_scalar(first_w[:], first_i[:], 7, None, ALU.arith_shift_right))
                    nc.vector.tensor_copy(first_r[:], first_i[:])
                    nc.vector.tensor_copy(number[:], number_i[:])
                    nc.vector.tensor_tensor(start_r[:], first_w[:], chunk_no[:], ALU.add).then_inc(s_start, 1)
                    dve.wait_ge(s_bc, 1)
                    dve.wait_ge(s_start, 1)
                    for t in range(ST):
                        link(nc.vector.tensor_scalar(junk[:, 0:CH - 1], start_b[:, 1:CH], number[:, t:t + 1], 0.0,
                                                     ALU.is_le, ALU.add, accum_out=chunk_f[:, t:t + 1]))
                    nc.vector.tensor_copy(chunk_i[:], chunk_f[:]).then_inc(s_chunk, 1)
                    link(nc.vector.tensor_tensor(win_f[:], number[:, 0:ST], chunk_f[:], ALU.subtract))
                    link(nc.vector.tensor_scalar(win_f[:], win_f[:], float(NW - 1), None, ALU.min))
                    nc.vector.tensor_copy(win_i[:], win_f[:]).then_inc(s_win, 1)
                    link(nc.vector.tensor_scalar(base_f[:], win_f[:], float(-P), None, ALU.mult))
                    for t in range(RT):
                        link(nc.vector.tensor_scalar(junk[:, 0:CH], first_b[:, 0:CH], number[:, t:t + 1], 0.0,
                                                     ALU.is_lt, ALU.add, accum_out=rowc_f[:, t:t + 1]))
                    link(nc.vector.tensor_scalar(rowc_f[:], rowc_f[:], -1.0, 0.0, ALU.add, ALU.max))
                    nc.vector.tensor_copy(rowc_i[:], rowc_f[:]).then_inc(s_rowc, 1)
                    dve.wait_ge(s_srows, 2 * ST * 16)
                    sf, df = srows[:].bitcast(F32), drows[:].bitcast(F32)
                    link(nc.vector.tensor_scalar(sf, srows[:], float(N - 1), None, ALU.min))
                    for t in range(ST):
                        last = nc.vector.tensor_scalar(df[:, t, :], drows[:, t, :], base_f[:, t:t + 1], None, ALU.add)
                    last.then_inc(s_rel, 1)
                    for g in range(2 * ST):
                        t, dstside = g // 2, g % 2
                        dve.wait_ge(s_tp, g + 1)
                        table = steps_dst if dstside else steps_src
                        nc.vector.tensor_copy(table[:, t * P:(t + 1) * P], banks[g % 8][:, 0:P]).then_inc(s_tpc, 1)
                    dve.wait_ge(s_tpc, 2 * ST)
                    nc.vector.tensor_copy(steps_src[:, STEPS:STEPS + H], steps_src[:, 0:H])
                    for t in range(RT):
                        dve.wait_ge(s_nrows[t % 2], 16 * (t // 2 + 1))
                        ins = nc.vector.tensor_scalar(junk[:, 0:P], nrows[:, t % 2, :], number[:, t:t + 1], 0.0,
                                                      ALU.is_lt, ALU.add, accum_out=inrow[:, t:t + 1])
                        ins.then_inc(s_rowused, 1)
                        dve.wait_ge(s_rowused, t + 1)
                    nc.vector.scalar_tensor_tensor(start_f[:], rowc_f[:], float(P), inrow[:], ALU.mult,
                                                   ALU.add).then_inc(s_rs, 1)
                    dve.wait_ge(s_rs, 1)
                    dve.wait_ge(s_rb, 32)
                    link(nc.vector.tensor_tensor(has_f[:], end_f[:], start_f[:, 0:NT], ALU.is_gt))
                    link(nc.vector.tensor_scalar(alt_f[:], has_f[:], float(-ONES_ROW), float(ONES_ROW),
                                                 ALU.mult, ALU.add))
                    link(nc.vector.scalar_tensor_tensor(end_f[:], end_f[:], -1.0, has_f[:], ALU.add, ALU.mult))
                    nc.vector.tensor_tensor(last_row[:], end_f[:], alt_f[:], ALU.add)
                    link(nc.vector.tensor_copy(junk[:, 0:1], norm_dst[:, NP - 1:NP]))
                    pieces = 8
                    w = NP // pieces
                    for j in reversed(range(pieces)):
                        a, b = j * w, (j + 1) * w
                        if j:
                            link(nc.vector.tensor_tensor(junk[:, 0:w], norm_dst[:, a:b], norm_dst[:, a - 1:b - 1],
                                                         ALU.subtract))
                        else:
                            link(nc.vector.tensor_tensor(junk[:, 1:w], norm_dst[:, 1:b], norm_dst[:, 0:b - 1],
                                                         ALU.subtract))
                            link(nc.vector.tensor_copy(junk[:, 0:1], norm_dst[:, 0:1]))
                        link(nc.vector.tensor_scalar(junk[:, 0:w], junk[:, 0:w], 1.0, None, ALU.max))
                        link(nc.vector.reciprocal(norm_dst[:, a:b], junk[:, 0:w]))
                    nc.vector.memset(junk[:, 0:1], 0.0).then_inc(s_deg, 1)

                @block.scalar
                def _(act):
                    act.wait_ge(s_deg, 1)
                    nc.scalar.activation(norm_dst[:], norm_dst[:], ACT.Sqrt)

                @block.tensor
                def _(pe):
                    pe.wait_ge(s_rel, 1)
                    for g in range(2 * ST):
                        rows = drows if g % 2 else srows
                        if g >= 8:
                            pe.wait_ge(s_tpc, g - 7)
                        nc.tensor.transpose(banks[g % 8][:, 0:P], rows[:, g // 2, :].bitcast(F32),
                                            ident[:]).then_inc(s_tp, 1)

        with ExitStack() as ph:
            sbt = sb_in(ph)
            TB = -(-NB // P)
            b_src = sbt("b_src", [P, TB, BLK], I32)
            b_dst = sbt("b_dst", [P, TB, BLK], I32)
            b_prev = sbt("b_prev", [P, TB, BLK], I32)
            b_wt = sbt("b_wt", [P, TB, BLK])
            b_ang = sbt("b_ang", [P, TB, BLK])
            b_in = sbt("b_in", [P, TB, BLK])
            half_pi = sbt("half_pi", [P, 1])
            s_b, s_l2, s_rdy, s_ang, s_sin, s_t2, s_t2c = (sem(n) for n in
                ("s_b", "s_l2", "s_rdy", "s_ang", "s_sin", "s_t2", "s_t2c"))
            rows_of = lambda t: min(P, NB - t * P)
            with nc.Block() as block:
                @block.sync
                def _(sp):
                    views = ((b_src, src_d), (b_dst, dst_d), (b_prev, prev_d),
                             (b_wt, wt_d))
                    for t in range(TB):
                        r = rows_of(t)
                        for tile, flat in views:
                            sp.dma_start(tile[0:r, t, :], flat[t * P * BLK:(t * P + r) * BLK].rearrange(
                                "(b e) -> b e", e=BLK)).then_inc(s_b, 16)
                    sp.wait_ge(s_b, 4 * TB * 16)

                tabs = ("src", "same", "cut")

                @block.vector
                def _(dve):
                    links = [0]

                    def link(ins):
                        links[0] += 1
                        ins.then_inc(s_l2, 1)
                        dve.wait_ge(s_l2, links[0])

                    nc.vector.memset(half_pi[:], math.pi / 2)
                    nc.vector.memset(edge_src[:, NB:NB + AHEAD, :], 0)
                    dve.wait_ge(s_b, 4 * TB * 16)
                    for t in range(TB):
                        r = rows_of(t)
                        nc.vector.tensor_scalar(b_ang[0:r, t, :], b_wt[0:r, t, :], CUTOFF, None, ALU.min)
                        nc.vector.tensor_scalar(b_in[0:r, t, :], b_wt[0:r, t, :], CUTOFF, None, ALU.is_lt)
                        link(nc.vector.tensor_tensor(b_dst[0:r, t, :].bitcast(F32), b_dst[0:r, t, :],
                                                     b_prev[0:r, t, :], ALU.is_equal))
                        link(nc.vector.tensor_copy(b_src[0:r, t, :].bitcast(F32), b_src[0:r, t, :]))
                    nc.vector.memset(b_prev[0:1, 0, 0:1], 0).then_inc(s_ang, 1)
                    dve.wait_ge(s_sin, TB)
                    for t in range(TB):
                        r = rows_of(t)
                        link(nc.vector.tensor_scalar(b_ang[0:r, t, :], b_ang[0:r, t, :], 0.5, 0.5, ALU.mult, ALU.add))
                        last = nc.vector.tensor_tensor(b_ang[0:r, t, :], b_ang[0:r, t, :], b_in[0:r, t, :], ALU.mult)
                    last.then_inc(s_rdy, 1)
                    for g in range(3 * TB):
                        t, r = g // 3, rows_of(g // 3)
                        dve.wait_ge(s_t2, g + 1)
                        table = (edge_src, edge_same, edge_cut)[g % 3]
                        nc.vector.tensor_copy(table[:, t * P:t * P + r, :].rearrange("p b c -> p c b"),
                                              banks[g % 8][:].rearrange("p (c b) -> p c b", c=C4)[:, :, 0:r]
                                              ).then_inc(s_t2c, 1)
                    dve.wait_ge(s_t2c, 3 * TB)
                    nc.vector.tensor_scalar(edge_first[:], edge_same[:], -1.0, 1.0, ALU.mult, ALU.add)

                @block.scalar
                def _(act):
                    act.wait_ge(s_ang, 1)
                    for t in range(TB):
                        r = rows_of(t)
                        nc.scalar.activation(b_ang[0:r, t, :], b_ang[0:r, t, :], ACT.Sin, bias=half_pi[0:r, :],
                                             scale=-math.pi / CUTOFF).then_inc(s_sin, 1)

                @block.tensor
                def _(pe):
                    pe.wait_ge(s_rdy, 1)
                    for g in range(3 * TB):
                        t, r = g // 3, rows_of(g // 3)
                        if g >= 8:
                            pe.wait_ge(s_t2c, g - 7)
                        tile = (b_src[:].bitcast(F32), b_dst[:].bitcast(F32), b_ang[:])[g % 3]
                        for c in range(C4):
                            last = nc.tensor.transpose(banks[g % 8][:, c * P:c * P + r],
                                                       tile[0:r, t, :].rearrange("b (e c) -> b c e", c=C4)[:, c, :],
                                                       ident[0:r, 0:r])
                        last.then_inc(s_t2, 1)

        with ExitStack() as ph:
            sbt = sb_in(ph)
            CR = EP // P
            part_i = sbt("part_i", [P, CR], I32)
            low = sbt("low", [P, CR], BF16)
            high = sbt("high", [P, CR], BF16)
            iota_b = sbt("iota_b", [P, P], BF16)
            zero_b = sbt("zero_b", [P, P], BF16)
            hot_low = sbt("hot_low", [P, 2, HG, P], BF16)
            hot_high = sbt("hot_high", [P, 2, HG, NT], BF16)
            counts = banks[0][:, 0:NT]
            s_l3, s_parts, s_low, s_hist, s_sqrt = (sem(n) for n in
                ("s_l3", "s_parts", "s_hot_bins", "s_hist", "s_sqrt"))
            srcs = edge_src[:, 0:NB, :].rearrange("p b c -> p (b c)")
            with nc.Block() as block:
                @block.vector
                def _(dve):
                    links = [0]

                    def link(ins):
                        links[0] += 1
                        ins.then_inc(s_l3, 1)
                        dve.wait_ge(s_l3, links[0])

                    link(nc.vector.tensor_scalar(part_i[:], srcs, P - 1, None, ALU.bitwise_and))
                    link(nc.vector.tensor_copy(low[:], part_i[:]))
                    link(nc.vector.tensor_scalar(part_i[:], srcs, 7, None, ALU.arith_shift_right))
                    nc.vector.tensor_copy(iota_b[:], iota_f[:])
                    nc.vector.memset(zero_b[:], 0.0)
                    link(nc.vector.tensor_copy(high[:], part_i[:]))
                    nc.vector.tensor_scalar(srcs, srcs, float(N - 1), None, ALU.min).then_inc(s_parts, 1)
                    with dve.Fori(0, HB // 2) as i:
                        for j in range(2):
                            dve.wait_ge(s_hist, i * 2 + (j + 1))
                            nc.vector.tensor_tensor(
                                hot_low[:, j], low[:, bass.ds((i * 2 + j) * HG, HG)].unsqueeze(2).to_broadcast([P, HG, P]),
                                iota_b[:].unsqueeze(1).to_broadcast([P, HG, P]), ALU.is_equal)
                            nc.vector.tensor_tensor(
                                hot_high[:, j], high[:, bass.ds((i * 2 + j) * HG, HG)].unsqueeze(2).to_broadcast([P, HG, NT]),
                                iota_b[:, 0:NT].unsqueeze(1).to_broadcast([P, HG, NT]), ALU.is_equal).then_inc(s_low, 1)
                    dve.wait_ge(s_hist, 2 + HB + 1)
                    link(nc.vector.tensor_scalar(norm_src[:], counts, 1.0, None, ALU.max))
                    nc.vector.reciprocal(norm_src[:], norm_src[:]).then_inc(s_sqrt, 1)

                @block.tensor
                def _(pe):
                    pe.wait_ge(s_parts, 1)
                    nc.tensor.matmul(counts, zero_b[:], zero_b[:, 0:NT], start=True, stop=False).then_inc(s_hist, 2)
                    with pe.Fori(0, HB // 2) as i:
                        for j in range(2):
                            pe.wait_ge(s_low, i * 2 + (j + 1))
                            for g in range(HG):
                                last = nc.tensor.matmul(counts, hot_low[:, j, g, :], hot_high[:, j, g, :],
                                                        start=False, stop=False)
                            last.then_inc(s_hist, 1)
                    nc.tensor.matmul(counts, zero_b[:], zero_b[:, 0:NT], start=False, stop=True).then_inc(s_hist, 1)

                @block.scalar
                def _(act):
                    act.wait_ge(s_sqrt, 1)
                    nc.scalar.activation(norm_src[:], norm_src[:], ACT.Sqrt)

        x_sb = sb("x_sb", [P, NT, D])
        with ExitStack() as ph:
            sbt = sb_in(ph)
            agg = sbt("agg", [P, NW * P])
            xT = sbt("xT", [P, NP])
            ws = [sbt(f"w{k}", [D, D]) for k in range(3)]
            bs = [sbt(f"b{k}", [D, 1]) for k in range(3)]
            hs = x_sb
            idx = sbt("idx", [P, U], I32)
            msg = sbt("msg", [P, U, D])
            hot = sbt("hot", [P, U, P])
            v1_sb, v2_sb = sbt("v1_sb", [D, D]), sbt("v2_sb", [D, D])
            c1_sb = sbt("c1_sb", [D, 1])
            c1_less = sbt("c1_less", [D, 1])
            c2_row = sbt("c2_row", [1, C4, D])
            ones_r = sbt("ones_r", [1, P])
            center = sbt("center", [P, 1])
            halves = sbt("halves", [P, 1])
            dist = sbt("dist", [P, BLK])
            sq = sbt("sq", [P, BLK])
            basis = sbt("basis", [P, BLK])
            t1, e1, s1 = sbt("t1", [P, BLK]), sbt("e1", [P, BLK]), sbt("s1", [P, BLK])
            t2, e2 = sbt("t2", [P, BLK]), sbt("e2", [P, BLK])
            y2 = sbt("y2", [P, C4, D])
            ef = sbt("ef", [P, C4, D])
            g_out = sbt("g_out", [P, C4, D])
            ps1, ps2 = banks[2], banks[3]
            slots = banks[0:2] + banks[4:8]

            s_x, s_w, s_cst, s_xt, s_xtc = (sem(n) for n in ("s_x", "s_w", "s_cst", "s_xt", "s_xtc"))
            s_hp, s_hc, s_hst = sem("s_h_in_psum"), sem("s_h_copied"), sem("s_h_stored")
            s_zero, s_scaled, s_relu = sem("s_agg_zeroed"), sem("s_agg_scaled"), sem("s_x_ready")
            s_idx, s_half = sem("s_idx_ready"), sem("s_half_begun")
            s_gat = [sem(f"s_gathered{u}") for u in range(U)]
            s_hot, s_mm, s_acc = sem("s_hot_ready"), sem("s_summed"), sem("s_accumulated")
            s_dist, s_sqr, s_bas, s_z1, s_t1, s_e1, s_l1, s_s1 = (sem(n) for n in (
                "s_dist_in", "s_squared", "s_basis", "s_z1", "s_t1", "s_e1", "s_l1", "s_s1"))
            s_z2, s_t2_, s_e2, s_l2_, s_y2, s_ef, s_g, s_gst = (sem(n) for n in (
                "s_z2", "s_t2_", "s_e2", "s_l2_", "s_y2", "s_ef_in", "s_g_ready", "s_g_stored"))
            s_ft, s_ln, s_bn, s_rv, s_sd, s_x1, s_x1d = (sem(n) for n in (
                "s_back", "s_resid", "s_moments", "s_recip", "s_rstd", "s_x1", "s_x1d"))
            mom = sbt("mom", [P, NT, 2])
            stat = sbt("stat", [P, NT, 6])
            rstd = sbt("rstd", [P, NT])

            HGRP = 4
            groups = [(a, min(a + HGRP, NT)) for a in range(0, NT, HGRP)]
            NG = len(groups)
            filters = [ITS, ITS, FULL - 2 * ITS]
            XCH = 7
            XW = NP // XCH

            wt_row = wt_d.rearrange("(a b) -> a b", a=1)
            g_rows = g_d.rearrange("(b p c) d -> p b c d", c=C4, p=P)
            ef_rows = edge_attr[0:FULL * BLK, :].rearrange("(b p c) d -> p b c d", c=C4, p=P)
            h_rows = h_d.rearrange("(t p) d -> p t d", p=P)
            x1_rows = x1_d.rearrange("(t p) d -> p t d", p=P)

            with nc.Block() as block:
                @block.sync
                def _(sp):
                    lastp = N - (NT - 1) * P
                    sp.wait_ge(s_cst, 1)
                    sp.dma_start(x_sb[:, 0:NT - 1, :], x[0:(NT - 1) * P, :].rearrange("(t p) d -> p t d", p=P)
                                 ).then_inc(s_x, 16)
                    sp.dma_start(x_sb[0:lastp, NT - 1, :], x[(NT - 1) * P:N, :]).then_inc(s_x, 16)
                    col = lambda b: b.rearrange("(a b) -> a b", b=1)
                    row = lambda b: b.rearrange("(a b) -> a b", a=1)
                    for tile, ap in zip(ws + [v1_sb, v2_sb], (w1, w2, w3, v1, v2)):
                        sp.dma_start(tile[:], ap).then_inc(s_w, 16)
                    for tile, ap in zip(bs + [c1_sb], (b1, b2, b3, c1)):
                        sp.dma_start(tile[:], col(ap)).then_inc(s_w, 16)
                    for c in range(C4):
                        sp.dma_start(c2_row[:, c, :], row(c2)).then_inc(s_w, 16)
                    sp.dma_start(dist[:], wt_row[:, 0:BLK].to_broadcast([P, BLK])).then_inc(s_dist, 16)
                    sp.dma_start(ef[:], ef_rows[:, 0]).then_inc(s_ef, 16)

                    with sp.Fori(0, FULL - 1) as b:
                        sp.wait_ge(s_sqr, b + 1)
                        sp.dma_start(dist[:], wt_row[:, bass.ds((b + 1) * BLK, BLK)].to_broadcast([P, BLK])
                                     ).then_inc(s_dist, 16)
                        sp.wait_ge(s_g, b + 1)
                        sp.dma_start(g_rows[:, bass.ds(b, 1)], g_out[:].unsqueeze(1)).then_inc(s_gst, 16)
                        sp.dma_start(ef[:].unsqueeze(1), ef_rows[:, bass.ds(b + 1, 1)]).then_inc(s_ef, 16)
                    sp.wait_ge(s_sqr, FULL)
                    sp.dma_start(dist[:], wt_row[:, FULL * BLK:EP].to_broadcast([P, BLK])).then_inc(s_dist, 16)
                    sp.wait_ge(s_g, FULL)
                    sp.dma_start(g_rows[:, FULL - 1], g_out[:]).then_inc(s_gst, 16)
                    sp.wait_ge(s_g, FULL + 1)
                    sp.dma_start(ef[0:TAIL // C4], edge_attr[FULL * BLK:E, :].rearrange("(p c) d -> p c d", c=C4)
                                 ).then_inc(s_ef, 16)
                    sp.wait_ge(s_g, FULL + 2)
                    sp.dma_start(g_rows[:, FULL], g_out[:]).then_inc(s_gst, 16)
                    sp.wait_ge(s_gst, 16 * (FULL + 2))

                @block.gpsimd
                def _(pool):
                    for k in range(3):
                        pool.wait_ge(s_hst, 16 * XCH * (k + 1))
                        with pool.Fori(0, ITS) as it:
                            for u in range(U):
                                if u % H == 0:
                                    pool.wait_ge(s_idx, it * 2 + (2 * ITS * k + u // H + 1))
                                    pool.sem_inc(s_half, 1)
                                pool.indirect_dma_start(
                                    out=msg[:, u, :], out_offset=None, in_=h_d,
                                    in_offset=bass.IndirectOffsetOnAxis(ap=idx[:, u:u + 1], axis=0)
                                ).then_inc(s_gat[u], 16)

                @block.scalar
                def _(act):
                    def copy_idx(step, half, done):
                        act.wait_ge(s_mm, done)
                        nc.scalar.copy(idx[:, half * H:(half + 1) * H],
                                       steps_src[:, bass.ds(step, H)]).then_inc(s_idx, 1)

                    def basis_of(b):
                        act.wait_ge(s_dist, b * 16 + 16)
                        nc.scalar.activation(sq[:], dist[:], ACT.Square, bias=center[:]).then_inc(s_sqr, 1)
                        act.wait_ge(s_sqr, b + 1)
                        nc.scalar.activation(basis[:], sq[:], ACT.Exp, scale=COEFF).then_inc(s_bas, 1)

                    def soft(b, t, e, s_in, s_exp, s_out):
                        act.wait_ge(s_in, b + 1)
                        nc.scalar.activation(e[:], t[:], ACT.Exp).then_inc(s_exp, 1)
                        act.wait_ge(s_exp, b + 1)
                        nc.scalar.activation(t[:], e[:], ACT.Ln, bias=halves[:], scale=0.5).then_inc(s_out, 1)

                    act.wait_ge(s_cst, 1)
                    act.wait_ge(s_mm, U)
                    nc.scalar.copy(idx[:, 0:H], steps_src[:, 0:H]).then_inc(s_idx, 1)
                    for k in range(3):
                        for j in range(XCH):
                            a, b = j * NT // XCH, (j + 1) * NT // XCH
                            act.wait_ge(s_hc, NG * k + -(-b // HGRP))
                            act.dma_start(h_rows[:, a:b, :], hs[:, a:b, :]).then_inc(s_hst, 16)

                        if k == 2:
                            act.wait_ge(s_hst, 16 * XCH * 3)
                            act.dma_start(x_sb[:, 0:NT - 1, :], x[0:(NT - 1) * P, :].rearrange(
                                "(t p) d -> p t d", p=P)).then_inc(s_x, 16)
                            act.dma_start(x_sb[0:N - (NT - 1) * P, NT - 1, :], x[(NT - 1) * P:N, :]).then_inc(s_x, 16)

                        def iteration(it, filtered):
                            copy_idx(it * U + H, 1, it * U + (STEPS * k + U))
                            if filtered:
                                b = it + ITS * k
                                basis_of(b)
                                soft(b, t1, e1, s_t1, s_e1, s_l1)
                            copy_idx(it * U + U, 0, it * U + (STEPS * k + U + H))
                            if filtered:
                                soft(b, t2, e2, s_t2_, s_e2, s_l2_)

                        nc.scalar.preload_act_table_set("natural_log_exp_and_others")
                        with act.Fori(0, filters[k]) as it:
                            iteration(it, True)
                        if filters[k] < ITS:
                            with act.Fori(filters[k], ITS) as it:
                                iteration(it, False)
                        for j in range(XCH):
                            act.wait_ge(s_scaled, XCH * k + j + 1)
                            nc.scalar.activation(xT[:, j * XW:(j + 1) * XW], agg[:, j * XW:(j + 1) * XW],
                                                 ACT.Relu if k < 2 else ACT.Identity, bias=bs[k][:]
                                                 ).then_inc(s_relu, 1)
                    basis_of(FULL)
                    soft(FULL, t1, e1, s_t1, s_e1, s_l1)
                    soft(FULL, t2, e2, s_t2_, s_e2, s_l2_)
                    act.wait_ge(s_rv, 1)
                    nc.scalar.activation(rstd[:], rstd[:], ACT.Sqrt).then_inc(s_sd, 1)
                    for j in range(XCH):
                        act.wait_ge(s_x1, j + 1)
                        act.dma_start(x1_rows[:, 7 * j:7 * j + 7, :], x_sb[:, 7 * j:7 * j + 7, :]).then_inc(s_x1d, 16)
                    act.wait_ge(s_x1d, 16 * XCH)

                @block.tensor
                def _(pe):
                    def z1(b):
                        pe.wait_ge(s_bas, b + 1)
                        nc.tensor.matmul(ps1[:], v1_sb[:], basis[:], start=True, stop=True).then_inc(s_z1, 1)

                    def z2(b):
                        pe.wait_ge(s_s1, b + 1)
                        nc.tensor.matmul(ps2[:], ones_r[:], c2_row[:].rearrange("p c d -> p (c d)"),
                                         start=True, stop=False)
                        s1_c = s1[:].rearrange("f (e c) -> f c e", c=C4)
                        for c in range(C4):
                            last = nc.tensor.matmul(ps2[:, c * D:(c + 1) * D], s1_c[:, c, :], v2_sb[:],
                                                    start=False, stop=(c == C4 - 1))
                        last.then_inc(s_z2, 1)

                    pe.wait_ge(s_cst, 1)
                    pe.wait_ge(s_x, 32)
                    pe.wait_ge(s_w, 16 * 13)
                    pe.sem_inc(s_mm, U)
                    for g, (a, b) in enumerate(groups):
                        if g >= 2:
                            pe.wait_ge(s_xtc, g - 1)
                        for t in range(a, b):
                            last = nc.tensor.transpose(banks[4 + g % 2][:, (t - a) * P:(t - a + 1) * P], x_sb[:, t, :],
                                                       ident[:])
                        last.then_inc(s_xt, 1)
                    pe.wait_ge(s_xtc, NG)
                    for k in range(3):
                        if k:
                            pe.wait_ge(s_relu, XCH * k)
                        for g, (a, b) in enumerate(groups):
                            if g >= 2:
                                pe.wait_ge(s_hc, NG * k + g - 1)
                            for t in range(a, b):
                                last = nc.tensor.matmul(banks[4 + g % 2][:, (t - a) * D:(t - a + 1) * D],
                                                        xT[:, t * P:(t + 1) * P], ws[k][:], start=True, stop=True)
                            last.then_inc(s_hp, 1)

                        def iteration(it, filtered):
                            for u in range(U):
                                pe.wait_ge(s_gat[u], it * 16 + 16 * (ITS * k + 1))
                                if u % H == 0:
                                    pe.wait_ge(s_hot, it * 2 + (2 * ITS * k + u // H + 1))
                                pe.wait_ge(s_acc, it * U + (STEPS * k + u + 1))
                                nc.tensor.matmul(slots[u % H][:, 0:P], msg[:, u, :],
                                                 hot[:, u, :], start=True, stop=True).then_inc(s_mm, 1)
                                if filtered and u == 0:
                                    z1(it + ITS * k)
                                if filtered and u == 5:
                                    z2(it + ITS * k)

                        with pe.Fori(0, filters[k]) as it:
                            iteration(it, True)
                        if filters[k] < ITS:
                            with pe.Fori(filters[k], ITS) as it:
                                iteration(it, False)
                    z1(FULL)
                    z2(FULL)
                    pe.wait_ge(s_relu, XCH * 3)
                    for g, (a, b) in enumerate(groups):
                        if g >= 2:
                            pe.wait_ge(s_ln, g - 1)
                        for t in range(a, b):
                            last = nc.tensor.transpose(banks[4 + g % 2][:, (t - a) * P:(t - a + 1) * P],
                                                       xT[:, t * P:(t + 1) * P], ident[:])
                        last.then_inc(s_ft, 1)

                @block.vector
                def _(dve):
                    nc.vector.memset(x_sb[:, NT - 1, :], 0.0)
                    nc.vector.memset(halves[:], 0.5)
                    nc.vector.memset(ones_r[:], 1.0)
                    nc.vector.tensor_scalar(center[:], pcol[:], -DELTA, None, ALU.mult).then_inc(s_cst, 1)
                    dve.sem_inc(s_acc, H)
                    dve.sem_inc(s_gst, 16)
                    dve.wait_ge(s_w, 16 * 13)
                    nc.vector.tensor_scalar(c1_less[:], c1_sb[:], -LN2, None, ALU.add)
                    for g, (a, b) in enumerate(groups):
                        dve.wait_ge(s_xt, g + 1)
                        nc.vector.tensor_copy(xT[:, a * P:b * P], banks[4 + g % 2][:, 0:(b - a) * P]).then_inc(s_xtc, 1)

                    def min1(b):
                        dve.wait_ge(s_z1, b + 1)
                        nc.vector.tensor_scalar(t1[:], ps1[:], c1_sb[:], SOFT_MAX, ALU.add, ALU.min).then_inc(s_t1, 1)

                    def max1(b):
                        dve.wait_ge(s_l1, b + 1)
                        nc.vector.scalar_tensor_tensor(s1[:], ps1[:], c1_less[:], t1[:], ALU.add,
                                                       ALU.max).then_inc(s_s1, 1)

                    def min2(b):
                        dve.wait_ge(s_z2, b + 1)
                        nc.vector.tensor_scalar(t2[:], ps2[:], SOFT_MAX, None, ALU.min).then_inc(s_t2_, 1)

                    def max2(b):
                        dve.wait_ge(s_l2_, b + 1)
                        nc.vector.scalar_tensor_tensor(y2[:].rearrange("p c d -> p (c d)"), ps2[:], -LN2, t2[:],
                                                       ALU.add, ALU.max).then_inc(s_y2, 1)

                    def weigh(b, loads, stores):
                        dve.wait_ge(s_y2, b + 1)
                        dve.wait_ge(s_ef, loads)
                        dve.wait_ge(s_gst, stores)
                        for c in range(C4):
                            cut = edge_cut[:].rearrange("p b c -> p (b c)")[:, bass.ds(b * C4 + c, 1)]
                            last = nc.vector.scalar_tensor_tensor(g_out[:, c, :], y2[:, c, :], cut, ef[:, c, :],
                                                                  ALU.mult, ALU.mult)
                        last.then_inc(s_g, 1)

                    for k in range(3):
                        if k:
                            dve.wait_ge(s_relu, XCH * k)
                            dve.wait_ge(s_hst, 16 * XCH * k)
                        nc.vector.memset(agg[:], 0.0).then_inc(s_zero, 1)
                        dve.wait_ge(s_zero, k + 1)
                        for g, (a, b) in enumerate(groups):
                            dve.wait_ge(s_hp, NG * k + g + 1)
                            nc.vector.tensor_tensor(
                                hs[:, a:b, :], banks[4 + g % 2][:, 0:(b - a) * D].rearrange("p (t d) -> p t d", d=D),
                                norm_src[:, a:b].unsqueeze(2).to_broadcast([P, b - a, D]), ALU.mult).then_inc(s_hc, 1)

                        def iteration(it, filtered):
                            blk = it + ITS * k
                            for half in range(2):
                                dve.wait_ge(s_mm, it * U + (STEPS * k + (half + 1) * H))
                                nc.vector.tensor_tensor(
                                    hot[:, half * H:(half + 1) * H, :],
                                    steps_dst[:, bass.ds(it * U + half * H, H)].unsqueeze(2).to_broadcast([P, H, P]),
                                    iota_f[:].unsqueeze(1).to_broadcast([P, H, P]), ALU.is_equal).then_inc(s_hot, 1)
                            wins = nc.values_load_multi_w_load_instructions(
                                windows[0:1, bass.ds(it * U, U)], engines=[mybir.EngineType.DVE],
                                min_val=0, max_val=NW - 1)[1]
                            for u in range(U):
                                dve.wait_ge(s_mm, it * U + (STEPS * k + U + u + 1))
                                dve.wait_ge(s_acc, it * U + (STEPS * k + H + u))
                                into = agg[:, bass.ds(wins[u] * P, P)]
                                nc.vector.tensor_tensor(into, into, slots[u % H][:, 0:P], ALU.add).then_inc(s_acc, 1)
                                if filtered:
                                    if u == 1:
                                        min1(blk)
                                    if u == 4:
                                        max1(blk)
                                    if u == 6:
                                        min2(blk)
                                    if u == 9:
                                        max2(blk)
                                        weigh(blk, blk * 16 + 16, blk * 16 + 16)

                        with dve.Fori(0, filters[k]) as it:
                            iteration(it, True)
                        if filters[k] < ITS:
                            with dve.Fori(filters[k], ITS) as it:
                                iteration(it, False)
                        dve.wait_ge(s_acc, STEPS * (k + 1) + H)
                        for j in range(XCH):
                            part = agg[:, j * XW:(j + 1) * XW]
                            nc.vector.tensor_tensor(part, part, norm_dst[:, j * XW:(j + 1) * XW],
                                                    ALU.mult).then_inc(s_scaled, 1)
                    dve.wait_ge(s_gst, 16 * (FULL + 1))
                    nc.vector.memset(ef[:], 0.0).then_inc(s_g, 1)
                    min1(FULL)
                    max1(FULL)
                    min2(FULL)
                    max2(FULL)
                    dve.wait_ge(s_y2, FULL + 1)
                    dve.wait_ge(s_ef, 16 * (FULL + 1))
                    for c in range(C4):
                        last = nc.vector.scalar_tensor_tensor(g_out[:, c, :], y2[:, c, :], edge_cut[:, FULL, c:c + 1],
                                                              ef[:, c, :], ALU.mult, ALU.mult)
                    last.then_inc(s_g, 1)
                    dve.wait_ge(s_x, 64)
                    for g, (a, b) in enumerate(groups):
                        dve.wait_ge(s_ft, g + 1)
                        nc.vector.tensor_tensor(x_sb[:, a:b, :], x_sb[:, a:b, :],
                                                banks[4 + g % 2][:, 0:(b - a) * D].rearrange("p (t d) -> p t d", d=D),
                                                ALU.add).then_inc(s_ln, 1)
                    dve.wait_ge(s_ln, NG)
                    for t in range(NT):
                        last = nc.vector.bn_stats(stat[:, t, :], x_sb[:, t, :])
                    last.then_inc(s_bn, 1)
                    dve.wait_ge(s_bn, 1)
                    for t in range(NT):
                        last = nc.vector.bn_aggr(mom[:, t, :], stat[:, t, :])
                    last.then_inc(s_bn, 1)
                    dve.wait_ge(s_bn, 2)
                    nc.vector.tensor_scalar(rstd[:], mom[:, :, 1], EPS, None, ALU.add).then_inc(s_bn, 1)
                    dve.wait_ge(s_bn, 3)
                    nc.vector.reciprocal(rstd[:], rstd[:]).then_inc(s_rv, 1)
                    dve.wait_ge(s_sd, 1)
                    for t in range(NT):
                        last = nc.vector.tensor_scalar(x_sb[:, t, :], x_sb[:, t, :], mom[:, t, 0:1], rstd[:, t:t + 1],
                                                       ALU.subtract, ALU.mult)
                        if t % 7 == 6:
                            last.then_inc(s_x1, 1)

        with ExitStack() as ph:
            sbt = sb_in(ph)
            R = AHEAD
            idx = sbt("idx4", [P, R, C4], I32)
            hgat = sbt("hgat", [P, R, C4, D])
            filt = sbt("filt", [P, R, C4, D])
            u_same = sbt("u_same", [P, R, C4, D])
            u_first = sbt("u_first", [P, R, C4, D])
            first_sb = sbt("first_sb", [P, R, BLK])
            run = sbt("run", [P, R, BLK])
            run_out = sbt("run_out", [P, R, C4, D])
            psame, pfirst = banks[0:R], banks[R:2 * R]
            prun = pfirst
            s_i, s_u, s_ts, s_fc, s_sc, s_tr, s_ro = (sem(n) for n in (
                "s_index4", "s_factors", "s_factors_T", "s_first_copied", "s_scanned", "s_run_T", "s_run_out"))
            s_turn = sem("s_gathers_begun")
            s_fi = [sem(f"s_filt_in{r}") for r in range(R)]
            s_gt = [[sem(f"s_hgat{r}_{c}") for c in range(C4)] for r in range(R)]
            s_rst = [sem(f"s_run_stored{r}") for r in range(R)]
            g_rows = g_d.rearrange("(b p c) d -> p b c d", c=C4, p=P)
            run_rows = run_d[0:EP, :].rearrange("(b p c) d -> p b c d", c=C4, p=P)
            LOOPS = (NB - 1) // R
            assert LOOPS * R == NB - 1 and R % 2
            with nc.Block() as block:
                @block.sync
                def _(sp):
                    def load(b, r):
                        sp.wait_ge(s_u, b + 1)
                        sp.dma_start(filt[:, r].unsqueeze(1), g_rows[:, bass.ds(b, 1)]).then_inc(s_fi[r], 16)

                    with sp.Fori(0, LOOPS) as i:
                        for r in range(R):
                            load(i * R + r, r)
                    load(NB - 1, 0)

                @block.gpsimd
                def _(pool):
                    def gather(b, r):
                        pool.wait_ge(s_i, b + 1)
                        pool.sem_inc(s_turn, 1)
                        for c in range(C4):
                            pool.indirect_dma_start(out=hgat[:, r, c, :], out_offset=None, in_=x1_d,
                                                    in_offset=bass.IndirectOffsetOnAxis(ap=idx[:, r, c:c + 1], axis=0)
                                                    ).then_inc(s_gt[r][c], 16)

                    with pool.Fori(0, LOOPS) as i:
                        for r in range(R):
                            gather(i * R + r, r)
                    gather(NB - 1, 0)

                @block.scalar
                def _(act):
                    def copy_idx(b, r):
                        act.wait_ge(s_u, b + 1)
                        nc.scalar.copy(idx[:, r:r + 1, :], edge_src[:, bass.ds(b, 1), :]).then_inc(s_i, 1)

                    def copy_first(b, r):
                        act.wait_ge(s_ts, b + (R + 1))
                        act.wait_ge(s_sc, b + 1)
                        nc.scalar.copy(first_sb[:, r, :], pfirst[r][:]).then_inc(s_fc, 1)

                    def store_run(b, r, stored):
                        act.wait_ge(s_tr, b + (R + 1))
                        act.wait_ge(s_rst[r], stored)
                        nc.scalar.copy(run_out[:, r].rearrange("p c d -> p (c d)"), prun[r][:]).then_inc(s_ro, 1)
                        act.wait_ge(s_ro, b + (R + 1))
                        act.dma_start(run_rows[:, bass.ds(b, 1)], run_out[:, r].unsqueeze(1)).then_inc(s_rst[r], 16)

                    act.sem_inc(s_ro, R)
                    for r in range(R):
                        act.sem_inc(s_rst[r], 16)
                        copy_idx(r, r)
                    copy_first(0, 0)
                    with act.Fori(0, LOOPS) as i:
                        for r in range(R):
                            b = i * R + r
                            copy_idx(b + R, r)
                            copy_first(b + 1, (r + 1) % R)
                            store_run(b, r, i * 16 + 16)
                    store_run(NB - 1, 0, LOOPS * 16 + 16)
                    act.wait_ge(s_rst[0], LOOPS * 16 + 32)
                    for r in range(1, R):
                        act.wait_ge(s_rst[r], LOOPS * 16 + 16)

                @block.tensor
                def _(pe):
                    def turn(b, r):
                        pe.wait_ge(s_u, b + (R + 1))
                        pe.wait_ge(s_ro, b + 1)
                        for bank, fac in ((pfirst[r], u_first), (psame[r], u_same)):
                            view = bank[:].rearrange("p (e c) -> p c e", c=C4)
                            for c in range(C4):
                                last = nc.tensor.transpose(view[:, c, :], fac[:, r, c, :], ident[:])
                        last.then_inc(s_ts, 1)

                    def back(b, r):
                        pe.wait_ge(s_sc, b + (R + 1))
                        view = run[:, r, :].rearrange("p (e c) -> p c e", c=C4)
                        bank = prun[r]
                        for c in range(C4):
                            last = nc.tensor.transpose(bank[:, c * P:(c + 1) * P], view[:, c, :], ident[:])
                        last.then_inc(s_tr, 1)

                    pe.sem_inc(s_ts, R)
                    pe.sem_inc(s_tr, R)
                    turn(0, 0)
                    with pe.Fori(0, LOOPS) as i:
                        for r in range(R):
                            b = i * R + r
                            turn(b + 1, (r + 1) % R)
                            back(b, r)
                    back(NB - 1, 0)

                @block.vector
                def _(dve):
                    same = edge_same[:].rearrange("p b c -> p (b c)")
                    first = edge_first[:].rearrange("p b c -> p (b c)")

                    def factors(b, r, nth):
                        for c in range(C4):
                            dve.wait_ge(s_gt[r][c], nth)
                        dve.wait_ge(s_fi[r], nth)
                        dve.wait_ge(s_ts, b + 1)
                        for out_, mask in ((u_same, same), (u_first, first)):
                            for c in range(C4):
                                last = nc.vector.scalar_tensor_tensor(
                                    out_[:, r, c, :], hgat[:, r, c, :], mask[:, bass.ds(b * C4 + c, 1)],
                                    filt[:, r, c, :], ALU.mult, ALU.mult)
                        last.then_inc(s_u, 1)

                    def scan(b, r):
                        dve.wait_ge(s_fc, b + 1)
                        dve.wait_ge(s_tr, b + 1)
                        dve.wait_ge(s_sc, b + R)
                        nc.vector.tensor_tensor_scan(run[:, r, :], psame[r][:], first_sb[:, r, :],
                                                     run[:, (r - 1) % R, BLK - 1:BLK], ALU.mult, ALU.add
                                                     ).then_inc(s_sc, 1)

                    nc.vector.memset(run[:, R - 1, BLK - 1:BLK], 0.0).then_inc(s_sc, R)
                    dve.sem_inc(s_u, R)
                    factors(0, 0, 16)
                    with dve.Fori(0, LOOPS) as i:
                        for r in range(R):
                            b = i * R + r
                            factors(b + 1, (r + 1) % R, i * 16 + (32 if r == R - 1 else 16))
                            scan(b, r)
                    scan(NB - 1, 0)

        with ExitStack() as ph:
            sbt = sb_in(ph)
            prod = sbt("prod", [P, NT, D])
            prodT = sbt("prodT", [P, 2, HGRP * P])
            v3_sb = sbt("v3_sb", [D, D])
            c3_row = sbt("c3_row", [1, D])
            ones_r = sbt("ones_r5", [1, P])
            halves = sbt("halves5", [P, 1])
            zmin = sbt("zmin", [P, NT, D])
            zall = sbt("zall", [P, NT, D])
            mom = sbt("mom5", [P, NT, 2])
            stat = sbt("stat5", [P, NT, 6])
            rstd = sbt("rstd5", [P, NT])
            s_w5, s_pg, s_pt, s_ptc, s_z, s_zc, s_ex, s_lg, s_l5, s_q5, s_r5, s_y, s_out = (sem(n) for n in (
                "s_w5", "s_prod_in", "s_prodT", "s_prodT_copied", "s_z3", "s_z3_copied", "s_exp3", "s_log3",
                "s_l5", "s_recip5", "s_rstd5", "s_out_ready", "s_out_stored"))
            with nc.Block() as block:
                @block.sync
                def _(sp):
                    sp.dma_start(v3_sb[:], v3).then_inc(s_w5, 16)
                    sp.dma_start(c3_row[:], c3.rearrange("(a b) -> a b", a=1)).then_inc(s_w5, 16)
                    for j in range(7):
                        sp.wait_ge(s_y, j + 1)
                        a, b = 7 * j, 7 * j + 7
                        full = min(b, NT - 1)
                        sp.dma_start(out[a * P:full * P, :].rearrange("(t p) d -> p t d", p=P),
                                     x_sb[:, a:full, :]).then_inc(s_out, 16)
                    sp.dma_start(out[(NT - 1) * P:N, :], x_sb[0:N - (NT - 1) * P, NT - 1, :]).then_inc(s_out, 16)
                    sp.wait_ge(s_out, 16 * 8)

                @block.gpsimd
                def _(pool):
                    nc.gpsimd.memset(ones_r[:], 1.0)
                    nc.gpsimd.memset(halves[:], 0.5).then_inc(s_w5, 1)
                    for t in range(NT):
                        pool.indirect_dma_start(out=prod[:, t, :], out_offset=None, in_=run_d,
                                                in_offset=bass.IndirectOffsetOnAxis(ap=last_row[:, t:t + 1], axis=0)
                                                ).then_inc(s_pg, 16)

                @block.tensor
                def _(pe):
                    pe.wait_ge(s_w5, 33)
                    pe.wait_ge(s_pg, 16 * NT)
                    for g, (a, b) in enumerate(groups):
                        if g >= 2:
                            pe.wait_ge(s_ptc, g - 1)
                        for t in range(a, b):
                            last = nc.tensor.transpose(banks[g % 2][:, (t - a) * P:(t - a + 1) * P], prod[:, t, :],
                                                       ident[:])
                        last.then_inc(s_pt, 1)
                        pe.wait_ge(s_ptc, g + 1)
                        if g >= 2:
                            pe.wait_ge(s_zc, g - 1)
                        for t in range(a, b):
                            z = banks[2 + g % 2][:, (t - a) * D:(t - a + 1) * D]
                            nc.tensor.matmul(z, ones_r[:], c3_row[:], start=True, stop=False)
                            last = nc.tensor.matmul(z, prodT[:, g % 2, (t - a) * P:(t - a + 1) * P], v3_sb[:],
                                                    start=False, stop=True)
                        last.then_inc(s_z, 1)

                @block.scalar
                def _(act):
                    act.wait_ge(s_zc, NG)
                    for j in range(7):
                        part = zmin[:, 7 * j:7 * j + 7, :]
                        nc.scalar.activation(part, part, ACT.Exp).then_inc(s_ex, 1)
                        act.wait_ge(s_ex, j + 1)
                        nc.scalar.activation(part, part, ACT.Ln, bias=halves[:], scale=0.5).then_inc(s_lg, 1)
                    act.wait_ge(s_q5, 1)
                    nc.scalar.activation(rstd[:], rstd[:], ACT.Sqrt).then_inc(s_r5, 1)

                @block.vector
                def _(dve):
                    for g, (a, b) in enumerate(groups):
                        dve.wait_ge(s_pt, g + 1)
                        if g >= 2:
                            dve.wait_ge(s_z, g - 1)
                        nc.vector.tensor_copy(prodT[:, g % 2, 0:(b - a) * P], banks[g % 2][:, 0:(b - a) * P]
                                              ).then_inc(s_ptc, 1)
                        dve.wait_ge(s_z, g + 1)
                        z = banks[2 + g % 2][:, 0:(b - a) * D].rearrange("p (t d) -> p t d", d=D)
                        nc.vector.tensor_scalar(zmin[:, a:b, :], z, SOFT_MAX, None, ALU.min)
                        nc.vector.tensor_scalar(zall[:, a:b, :], z, -LN2, None, ALU.add).then_inc(s_zc, 1)
                    dve.wait_ge(s_zc, NG)
                    for j in range(7):
                        dve.wait_ge(s_lg, j + 1)
                        sl = slice(7 * j, 7 * j + 7)
                        nc.vector.tensor_tensor(zall[:, sl, :], zall[:, sl, :], zmin[:, sl, :], ALU.max).then_inc(s_l5, 1)
                        dve.wait_ge(s_l5, 2 * j + 1)
                        nc.vector.tensor_tensor(x_sb[:, sl, :], x_sb[:, sl, :], zall[:, sl, :], ALU.add).then_inc(s_l5, 1)
                        dve.wait_ge(s_l5, 2 * j + 2)
                        for t in range(7 * j, 7 * j + 7):
                            last = nc.vector.bn_stats(stat[:, t, :], x_sb[:, t, :])
                    last.then_inc(s_l5, 1)
                    dve.wait_ge(s_l5, 15)
                    for t in range(NT):
                        last = nc.vector.bn_aggr(mom[:, t, :], stat[:, t, :])
                    last.then_inc(s_l5, 1)
                    dve.wait_ge(s_l5, 16)
                    nc.vector.tensor_scalar(rstd[:], mom[:, :, 1], EPS, None, ALU.add).then_inc(s_l5, 1)
                    dve.wait_ge(s_l5, 17)
                    nc.vector.reciprocal(rstd[:], rstd[:]).then_inc(s_q5, 1)
                    dve.wait_ge(s_r5, 1)
                    for t in range(NT):
                        last = nc.vector.tensor_scalar(x_sb[:, t, :], x_sb[:, t, :], mom[:, t, 0:1], rstd[:, t:t + 1],
                                                       ALU.subtract, ALU.mult)
                        if t % 7 == 6:
                            last.then_inc(s_y, 1)


_INS = ["x", "src", "dst", "edge_attr_128", "edge_weight",
        "L0_gnn_W1", "L0_gnn_b1", "L0_gnn_W2", "L0_gnn_b2", "L0_gnn_W3", "L0_gnn_b3",
        "L1_gnn_W1", "L1_gnn_b1", "L1_gnn_W2", "L1_gnn_b2", "L1_gnn_W3", "L1_gnn_b3"]


def kernel(**inputs):
    import concourse.bacc as bacc
    from concourse.bass_utils import run_bass_kernel_spmd

    nc = bacc.Bacc("TRN2", target_bir_lowering=False, num_devices=1)
    arrays, args = {}, []
    for name in _INS:
        a = np.ascontiguousarray(inputs[name])
        arrays[f"in_{name}"] = a
        args.append(nc.dram_tensor(f"in_{name}", a.shape, mybir.dt.from_np(a.dtype), kind="ExternalInput").ap())
    res = nc.dram_tensor("out_x", (N, D), F32, kind="ExternalOutput").ap()
    gnn(nc, *args, res)
    r = run_bass_kernel_spmd(nc, [arrays], core_ids=[0])
    return r.results[0]["out_x"]
```

```python
import math

import numpy as np
import concourse.bass as bass
from concourse import mybir
from contextlib import ExitStack

F32 = mybir.dt.float32
BF16 = mybir.dt.bfloat16
I32 = mybir.dt.int32
ALU = mybir.AluOpType
ACT = mybir.ActivationFunctionType

P = 128
N = 6250
E = 200000
D = 128
NT = -(-N // P)
NP = NT * P
NW = NT + 1
J = 2
CE = J * P
CH = -(-E // CE)
C4 = 4
BLK = P * C4
NB = -(-E // BLK)
EP = NB * BLK
U = 24
H = 4
G = U // H
SU = U // J
ITS = -(-(CH + NT) // SU)
STEPS = ITS * SU
GATHERS = ITS * U
ST = -(-STEPS // P)
FULL = E // BLK
FB = 2
TAIL = E - FULL * BLK
PADNODE = 8191
RT = NT + 1
HG = 17
HB = EP // P // HG
CUTOFF = 5.0
LN2 = 0.6931471805599453
SLOTS = 6
SOFT_MAX = 18.0
EPS = 1e-5
DELTA = CUTOFF / (D - 1)
AHEAD = 3
COEFF = -0.5 / (DELTA * DELTA)


def gnn(nc, x, src, dst, edge_attr, edge_weight, w1, b1, w2, b2, w3, b3, v1, c1, v2, c2, v3, c3, out):
    scratch = lambda name, shape, dt: nc.dram_tensor(name, shape, dt, kind="Internal").ap()
    src_d = scratch("src_padded", (EP,), I32)
    dst_d = scratch("dst_padded", (EP,), I32)
    prev_d = scratch("dst_of_previous_edge", (EP,), I32)
    wt_d = scratch("weight_padded", (EP,), F32)
    win_d = scratch("step_windows", (ST * P,), I32)
    row_d = scratch("row_starts", (RT * P,), F32)
    norm_d = scratch("norm_of_nodes", (NP,), F32)
    h_d = scratch("h_rows", (NP, D), F32)
    x1_d = scratch("x1_rows", (NP, D), F32)
    g_d = scratch("edge_filter", (EP, D), F32)
    run_d = scratch("running_products", (EP + 1, D), F32)
    ONES_ROW = EP
    src_rows = src_d.rearrange("(c e) -> c e", e=CE)
    dst_rows = dst_d.rearrange("(c e) -> c e", e=CE)

    outer = ExitStack()
    with outer:
        sb_in = lambda stack: (lambda name, shape, dt=F32: stack.enter_context(nc.sbuf_tensor(name, shape, dt)))
        sb = sb_in(outer)
        sem = lambda name: outer.enter_context(nc.semaphore(name))

        ident = sb("ident", [P, P])
        iota_f = sb("iota_f", [P, P])
        pcol = sb("pcol", [P, 1])
        steps_src = sb("steps_src", [P, ST * P * J], I32)
        steps_dst = sb("steps_dst", [P, ST * P * J])
        windows = sb("windows", [1, ST * P], I32)
        edge_src = sb("edge_src", [P, NB + AHEAD, C4], I32)
        edge_cut = sb("edge_cut", [P, NB, C4])
        edge_same = sb("edge_same", [P, NB, C4])
        edge_first = sb("edge_first", [P, NB, C4])
        last_row = sb("last_row", [P, NT], I32)
        norm_src = sb("norm_src", [P, NT])
        norm_dst = sb("norm_dst", [P, NP])
        banks = [outer.enter_context(nc.psum_tensor(f"bank{i}", [P, 512], F32)) for i in range(8)]

        with ExitStack() as ph:
            sbt = sb_in(ph)
            pad_i = sbt("pad_i", [1, BLK], I32)
            lead_i = sbt("lead_i", [1, 1], I32)
            pad_w = sbt("pad_w", [1, BLK])
            iota_i = sbt("iota_i", [P, P], I32)
            pcol_i = sbt("pcol_i", [P, 1], I32)
            ones_row = sbt("ones_row", [1, D])
            s_pads, s_iota, s_copied, s_const = sem("s_pads"), sem("s_iota"), sem("s_copied"), sem("s_const")
            with nc.Block() as block:
                @block.gpsimd
                def _(pool):
                    nc.gpsimd.memset(pad_i[:], PADNODE)
                    nc.gpsimd.memset(lead_i[:], -1)
                    nc.gpsimd.memset(ones_row[:], 1.0)
                    nc.gpsimd.memset(pad_w[:], 0.0).then_inc(s_pads, 1)
                    nc.gpsimd.iota(iota_i[:], [[1, P]], base=0, channel_multiplier=0)
                    nc.gpsimd.iota(pcol_i[:], [[1, 1]], base=0, channel_multiplier=1).then_inc(s_iota, 1)

                @block.vector
                def _(dve):
                    dve.wait_ge(s_iota, 1)
                    nc.vector.tensor_copy(iota_f[:], iota_i[:])
                    nc.vector.tensor_copy(pcol[:], pcol_i[:]).then_inc(s_const, 1)
                    dve.wait_ge(s_const, 1)
                    nc.vector.tensor_scalar(ident[:], iota_f[:], pcol[:, 0:1], None, ALU.is_equal)

                @block.sync
                def _(sp):
                    sp.dma_start(src_d[0:E].rearrange("(a b) -> a b", a=16),
                                 src.rearrange("(a b) -> a b", a=16)).then_inc(s_copied, 16)
                    for ap in (dst_d[0:E], prev_d[1:E + 1]):
                        sp.dma_start(ap.rearrange("(a b) -> a b", a=16),
                                     dst.rearrange("(a b) -> a b", a=16)).then_inc(s_copied, 16)
                    sp.dma_start(wt_d[0:E].rearrange("(a b) -> a b", a=16),
                                 edge_weight.rearrange("(a b) -> a b", a=16)).then_inc(s_copied, 16)
                    sp.wait_ge(s_pads, 1)
                    row = lambda ap: ap.rearrange("(a b) -> a b", a=1)
                    sp.dma_start(row(src_d[E:EP]), pad_i[:, 0:EP - E]).then_inc(s_copied, 16)
                    sp.dma_start(row(dst_d[E:EP]), pad_i[:, 0:EP - E]).then_inc(s_copied, 16)
                    sp.dma_start(row(prev_d[E + 1:EP]), pad_i[:, 0:EP - E - 1]).then_inc(s_copied, 16)
                    sp.dma_start(row(prev_d[0:1]), lead_i[:]).then_inc(s_copied, 16)
                    sp.dma_start(row(wt_d[E:EP]), pad_w[:, 0:EP - E]).then_inc(s_copied, 16)
                    sp.dma_start(run_d[ONES_ROW:ONES_ROW + 1, :], ones_row[:]).then_inc(s_copied, 16)
                    sp.wait_ge(s_copied, 10 * 16)

        with ExitStack() as ph:
            sbt = sb_in(ph)
            TB = -(-NB // P)
            b_src = sbt("b_src", [P, TB, BLK], I32)
            b_dst = sbt("b_dst", [P, TB, BLK], I32)
            b_prev = sbt("b_prev", [P, TB, BLK], I32)
            b_wt = sbt("b_wt", [P, TB, BLK])
            b_ang = sbt("b_ang", [P, TB, BLK])
            b_in = sbt("b_in", [P, TB, BLK])
            half_pi = sbt("half_pi", [P, 1])
            s_b, s_l2, s_rdy, s_ang, s_sin, s_t2, s_t2c = (sem(n) for n in
                ("s_b", "s_l2", "s_rdy", "s_ang", "s_sin", "s_t2", "s_t2c"))
            rows_of = lambda t: min(P, NB - t * P)
            with nc.Block() as block:
                @block.sync
                def _(sp):
                    views = ((b_src, src_d), (b_dst, dst_d), (b_prev, prev_d),
                             (b_wt, wt_d))
                    for t in range(TB):
                        r = rows_of(t)
                        for tile, flat in views:
                            sp.dma_start(tile[0:r, t, :], flat[t * P * BLK:(t * P + r) * BLK].rearrange(
                                "(b e) -> b e", e=BLK)).then_inc(s_b, 16)
                    sp.wait_ge(s_b, 4 * TB * 16)

                tabs = ("src", "same", "cut")

                @block.vector
                def _(dve):
                    links = [0]

                    def link(ins):
                        links[0] += 1
                        ins.then_inc(s_l2, 1)
                        dve.wait_ge(s_l2, links[0])

                    nc.vector.memset(half_pi[:], math.pi / 2)
                    nc.vector.memset(edge_src[:, NB:NB + AHEAD, :], 0)
                    dve.wait_ge(s_b, 4 * TB * 16)
                    for t in range(TB):
                        r = rows_of(t)
                        nc.vector.tensor_scalar(b_ang[0:r, t, :], b_wt[0:r, t, :], CUTOFF, None, ALU.min)
                        nc.vector.tensor_scalar(b_in[0:r, t, :], b_wt[0:r, t, :], CUTOFF, None, ALU.is_lt)
                        link(nc.vector.tensor_tensor(b_dst[0:r, t, :].bitcast(F32), b_dst[0:r, t, :],
                                                     b_prev[0:r, t, :], ALU.is_equal))
                        link(nc.vector.tensor_copy(b_src[0:r, t, :].bitcast(F32), b_src[0:r, t, :]))
                    nc.vector.memset(b_prev[0:1, 0, 0:1], 0).then_inc(s_ang, 1)
                    dve.wait_ge(s_sin, TB)
                    for t in range(TB):
                        r = rows_of(t)
                        link(nc.vector.tensor_scalar(b_ang[0:r, t, :], b_ang[0:r, t, :], 0.5, 0.5, ALU.mult, ALU.add))
                        last = nc.vector.tensor_tensor(b_ang[0:r, t, :], b_ang[0:r, t, :], b_in[0:r, t, :], ALU.mult)
                    last.then_inc(s_rdy, 1)
                    for g in range(3 * TB):
                        t, r = g // 3, rows_of(g // 3)
                        dve.wait_ge(s_t2, g + 1)
                        table = (edge_src, edge_same, edge_cut)[g % 3]
                        nc.vector.tensor_copy(table[:, t * P:t * P + r, :].rearrange("p b c -> p c b"),
                                              banks[g % 8][:].rearrange("p (c b) -> p c b", c=C4)[:, :, 0:r]
                                              ).then_inc(s_t2c, 1)
                    dve.wait_ge(s_t2c, 3 * TB)
                    nc.vector.tensor_scalar(edge_first[:], edge_same[:], -1.0, 1.0, ALU.mult, ALU.add)

                @block.scalar
                def _(act):
                    act.wait_ge(s_ang, 1)
                    for t in range(TB):
                        r = rows_of(t)
                        nc.scalar.activation(b_ang[0:r, t, :], b_ang[0:r, t, :], ACT.Sin, bias=half_pi[0:r, :],
                                             scale=-math.pi / CUTOFF).then_inc(s_sin, 1)

                @block.tensor
                def _(pe):
                    pe.wait_ge(s_rdy, 1)
                    for g in range(3 * TB):
                        t, r = g // 3, rows_of(g // 3)
                        if g >= 8:
                            pe.wait_ge(s_t2c, g - 7)
                        tile = (b_src[:].bitcast(F32), b_dst[:].bitcast(F32), b_ang[:])[g % 3]
                        for c in range(C4):
                            last = nc.tensor.transpose(banks[g % 8][:, c * P:c * P + r],
                                                       tile[0:r, t, :].rearrange("b (e c) -> b c e", c=C4)[:, c, :],
                                                       ident[0:r, 0:r])
                        last.then_inc(s_t2, 1)

        with ExitStack() as ph:
            sbt = sb_in(ph)
            CR = EP // CE
            first_i = sbt("first_i", [1, CR], I32)
            first_w = sbt("first_w", [1, CR], I32)
            chunk_no = sbt("chunk_no", [1, CR], I32)
            first_r = sbt("first_r", [1, CR])
            start_r = sbt("start_r", [1, CR])
            first_b = sbt("first_b", [P, CR])
            start_b = sbt("start_b", [P, CR])
            junk = sbt("junk", [P, CR])
            number_i = sbt("number_i", [P, RT], I32)
            number = sbt("number", [P, RT])
            chunk_f = sbt("chunk_f", [P, ST])
            chunk_i = sbt("chunk_i", [P, ST], I32)
            win_f = sbt("win_f", [P, ST])
            win_i = sbt("win_i", [P, ST], I32)
            base_f = sbt("base_f", [P, ST])
            rowc_f = sbt("rowc_f", [P, RT])
            rowc_i = sbt("rowc_i", [P, RT], I32)
            inrow = sbt("inrow", [P, RT])
            start_f = sbt("start_f", [P, RT])
            end_f = sbt("end_f", [P, NT])
            has_f = sbt("has_f", [P, NT])
            alt_f = sbt("alt_f", [P, NT])
            norm_p = sbt("norm_p", [P, NT])
            srows = sbt("srows", [P, ST, CE], I32)
            drows = sbt("drows", [P, ST, CE], I32)
            nrows = sbt("nrows", [P, RT, CE], I32)
            bins = EP // P
            part_i = sbt("part_i", [P, bins], I32)
            low = sbt("low", [P, bins], BF16)
            high = sbt("high", [P, bins], BF16)
            iota_b = sbt("iota_b", [P, P], BF16)
            zero_b = sbt("zero_b", [P, P], BF16)
            hot_low = sbt("hot_low", [P, 2, HG, P], BF16)
            hot_high = sbt("hot_high", [P, 2, HG, NT], BF16)
            counts = banks[7][:, 0:NT]
            TPB = 7
            s_first, s_start, s_bc, s_num = (sem(n) for n in ("s_first", "s_start", "s_bc", "s_num"))
            s_chunk, s_srows, s_rel, s_tp, s_tpc = (sem(n) for n in ("s_chunk", "s_srows", "s_rel", "s_tp", "s_tpc"))
            s_win, s_wind, s_winl, s_link = (sem(n) for n in ("s_win", "s_wind", "s_winl", "s_link"))
            s_rowc, s_nrows, s_rs, s_rsd, s_rb = (sem(n) for n in ("s_rowc", "s_nrows", "s_rs", "s_rsd", "s_rb"))
            s_parts, s_bins, s_hist, s_recip, s_root, s_nd = (sem(n) for n in (
                "s_parts", "s_hot_bins", "s_hist", "s_degree_recip", "s_root", "s_norm_stored"))
            srcs = edge_src[:, 0:NB, :].rearrange("p b c -> p (b c)")
            with nc.Block() as block:
                @block.sync
                def _(sp):
                    with nc.allow_non_contiguous_dma(reason="first dst of every chunk"):
                        sp.dma_start(first_i[:], dst_rows[:, 0:1].rearrange("c o -> o c")).then_inc(s_first, 16)
                    sp.wait_ge(s_win, 1)
                    with nc.allow_non_contiguous_dma(reason="small table"):
                        sp.dma_start(win_d.rearrange("(t p) -> p t", p=P), win_i[:]).then_inc(s_wind, 16)
                    sp.wait_ge(s_wind, 16)
                    sp.dma_start(windows[:], win_d.rearrange("(a b) -> a b", a=1)).then_inc(s_winl, 16)
                    sp.wait_ge(s_rs, 1)
                    with nc.allow_non_contiguous_dma(reason="small table"):
                        sp.dma_start(row_d.rearrange("(t p) -> p t", p=P), start_f[:]).then_inc(s_rsd, 16)
                        sp.wait_ge(s_rsd, 16)
                        sp.dma_start(end_f[:], row_d[1:NP + 1].rearrange("(t p) -> p t", p=P)).then_inc(s_rb, 16)
                        sp.wait_ge(s_root, 1)
                        sp.dma_start(norm_d.rearrange("(t p) -> p t", p=P), norm_p[:]).then_inc(s_nd, 16)
                    sp.wait_ge(s_nd, 16)
                    sp.dma_start(norm_dst[:, :], norm_d.rearrange("(a b) -> a b", a=1).to_broadcast([P, NP])
                                 ).then_inc(s_rb, 16)
                    sp.wait_ge(s_winl, 16)
                    sp.wait_ge(s_rb, 32)

                @block.gpsimd
                def _(pool):
                    nc.gpsimd.iota(chunk_no[:], [[1, CR]], base=0, channel_multiplier=0)
                    nc.gpsimd.iota(number_i[:], [[P, RT]], base=0, channel_multiplier=1).then_inc(s_num, 1)
                    pool.wait_ge(s_start, 1)
                    nc.gpsimd.partition_broadcast(start_b[:], start_r[:])
                    nc.gpsimd.partition_broadcast(first_b[:], first_r[:]).then_inc(s_bc, 1)
                    pool.wait_ge(s_chunk, 1)
                    for t in range(ST):
                        for rows, table in ((srows, src_rows), (drows, dst_rows)):
                            pool.indirect_dma_start(out=rows[:, t, :], out_offset=None, in_=table,
                                                    in_offset=bass.IndirectOffsetOnAxis(ap=chunk_i[:, t:t + 1], axis=0)
                                                    ).then_inc(s_srows, 16)
                    pool.wait_ge(s_rowc, 1)
                    for t in range(RT):
                        pool.indirect_dma_start(out=nrows[:, t, :], out_offset=None, in_=dst_rows,
                                                in_offset=bass.IndirectOffsetOnAxis(ap=rowc_i[:, t:t + 1], axis=0)
                                                ).then_inc(s_nrows, 16)

                @block.vector
                def _(dve):
                    links = [0]

                    def link(ins):
                        links[0] += 1
                        ins.then_inc(s_link, 1)
                        dve.wait_ge(s_link, links[0])

                    dve.wait_ge(s_num, 1)
                    dve.wait_ge(s_first, 16)
                    link(nc.vector.tensor_scalar(first_w[:], first_i[:], 7, None, ALU.arith_shift_right))
                    nc.vector.tensor_copy(first_r[:], first_i[:])
                    nc.vector.tensor_copy(number[:], number_i[:])
                    nc.vector.tensor_tensor(start_r[:], first_w[:], chunk_no[:], ALU.add).then_inc(s_start, 1)
                    link(nc.vector.tensor_scalar(part_i[:], srcs, P - 1, None, ALU.bitwise_and))
                    link(nc.vector.tensor_copy(low[:], part_i[:]))
                    link(nc.vector.tensor_scalar(part_i[:], srcs, 7, None, ALU.arith_shift_right))
                    nc.vector.tensor_copy(iota_b[:], iota_f[:])
                    nc.vector.memset(zero_b[:], 0.0)
                    link(nc.vector.tensor_copy(high[:], part_i[:]))
                    nc.vector.tensor_scalar(srcs, srcs, float(N - 1), None, ALU.min).then_inc(s_parts, 1)
                    dve.wait_ge(s_bc, 1)
                    dve.wait_ge(s_start, 1)
                    for t in range(ST):
                        link(nc.vector.tensor_scalar(junk[:, 0:CH - 1], start_b[:, 1:CH], number[:, t:t + 1], 0.0,
                                                     ALU.is_le, ALU.add, accum_out=chunk_f[:, t:t + 1]))
                    nc.vector.tensor_copy(chunk_i[:], chunk_f[:]).then_inc(s_chunk, 1)
                    link(nc.vector.tensor_tensor(win_f[:], number[:, 0:ST], chunk_f[:], ALU.subtract))
                    link(nc.vector.tensor_scalar(win_f[:], win_f[:], float(NW - 1), None, ALU.min))
                    nc.vector.tensor_copy(win_i[:], win_f[:]).then_inc(s_win, 1)
                    link(nc.vector.tensor_scalar(base_f[:], win_f[:], float(-P), None, ALU.mult))
                    for t in range(RT):
                        link(nc.vector.tensor_scalar(junk[:, 0:CH], first_b[:, 0:CH], number[:, t:t + 1], 0.0,
                                                     ALU.is_lt, ALU.add, accum_out=rowc_f[:, t:t + 1]))
                    link(nc.vector.tensor_scalar(rowc_f[:], rowc_f[:], -1.0, 0.0, ALU.add, ALU.max))
                    nc.vector.tensor_copy(rowc_i[:], rowc_f[:]).then_inc(s_rowc, 1)
                    dve.wait_ge(s_srows, 2 * ST * 16)
                    sf, df = srows[:].bitcast(F32), drows[:].bitcast(F32)
                    link(nc.vector.tensor_scalar(sf, srows[:], float(N - 1), None, ALU.min))
                    for t in range(ST):
                        last = nc.vector.tensor_scalar(df[:, t, :], drows[:, t, :], base_f[:, t:t + 1], None, ALU.add)
                    last.then_inc(s_rel, 1)

                    def bin_hots(i, j):
                        dve.wait_ge(s_hist, i * 2 + (j + 1))
                        for hot_, part, n in ((hot_low, low, P), (hot_high, high, NT)):
                            last = nc.vector.tensor_tensor(
                                hot_[:, j], part[:, bass.ds((i * 2 + j) * HG, HG)].unsqueeze(2).to_broadcast([P, HG, n]),
                                iota_b[:, 0:n].unsqueeze(1).to_broadcast([P, HG, n]), ALU.is_equal)
                        last.then_inc(s_bins, 1)

                    with dve.Fori(0, HB // 4) as i:
                        for j in range(2):
                            bin_hots(i, j)
                    for g in range(2 * ST * J):
                        t, j, table = g // (2 * J), g // 2 % J, (steps_src, steps_dst)[g % 2]
                        dve.wait_ge(s_tp, g + 1)
                        nc.vector.tensor_copy(
                            table[:, t * P * J:(t + 1) * P * J].rearrange("p (s j) -> p j s", j=J)[:, j, :],
                            banks[g % TPB][:, 0:P]).then_inc(s_tpc, 1)
                    dve.wait_ge(s_tpc, 2 * ST * J)
                    nc.vector.tensor_copy(steps_src[:, GATHERS:GATHERS + H], steps_src[:, 0:H])
                    dve.wait_ge(s_nrows, 16 * RT)
                    for t in range(RT):
                        link(nc.vector.tensor_scalar(junk[:, 0:CE], nrows[:, t, :], number[:, t:t + 1], 0.0,
                                                     ALU.is_lt, ALU.add, accum_out=inrow[:, t:t + 1]))
                    nc.vector.scalar_tensor_tensor(start_f[:], rowc_f[:], float(CE), inrow[:], ALU.mult,
                                                   ALU.add).then_inc(s_rs, 1)
                    with dve.Fori(HB // 4, HB // 2) as i:
                        for j in range(2):
                            bin_hots(i, j)
                    dve.wait_ge(s_rs, 1)
                    dve.wait_ge(s_rb, 16)
                    link(nc.vector.tensor_tensor(norm_p[:], end_f[:], start_f[:, 0:NT], ALU.subtract))
                    link(nc.vector.tensor_scalar(norm_p[:], norm_p[:], 1.0, None, ALU.max))
                    link(nc.vector.reciprocal(norm_p[:], norm_p[:]))
                    dve.wait_ge(s_hist, 2 + HB + 1)
                    link(nc.vector.tensor_scalar(norm_src[:], counts, 1.0, None, ALU.max))
                    nc.vector.reciprocal(norm_src[:], norm_src[:]).then_inc(s_recip, 1)
                    link(nc.vector.tensor_tensor(has_f[:], end_f[:], start_f[:, 0:NT], ALU.is_gt))
                    link(nc.vector.tensor_scalar(alt_f[:], has_f[:], float(-ONES_ROW), float(ONES_ROW),
                                                 ALU.mult, ALU.add))
                    link(nc.vector.scalar_tensor_tensor(end_f[:], end_f[:], -1.0, has_f[:], ALU.add, ALU.mult))
                    nc.vector.tensor_tensor(last_row[:], end_f[:], alt_f[:], ALU.add)

                @block.scalar
                def _(act):
                    act.wait_ge(s_recip, 1)
                    nc.scalar.activation(norm_p[:], norm_p[:], ACT.Sqrt).then_inc(s_root, 1)
                    nc.scalar.activation(norm_src[:], norm_src[:], ACT.Sqrt)

                @block.tensor
                def _(pe):
                    def bin_sums(i, j):
                        pe.wait_ge(s_bins, i * 2 + (j + 1))
                        for g in range(HG):
                            last = nc.tensor.matmul(counts, hot_low[:, j, g, :], hot_high[:, j, g, :],
                                                    start=False, stop=False)
                        last.then_inc(s_hist, 1)

                    pe.wait_ge(s_parts, 1)
                    nc.tensor.matmul(counts, zero_b[:], zero_b[:, 0:NT], start=True, stop=False).then_inc(s_hist, 2)
                    pe.wait_ge(s_rel, 1)
                    with pe.Fori(0, HB // 4) as i:
                        for j in range(2):
                            bin_sums(i, j)
                    for g in range(2 * ST * J):
                        t, j, rows = g // (2 * J), g // 2 % J, (srows, drows)[g % 2]
                        if g >= TPB:
                            pe.wait_ge(s_tpc, g - TPB + 1)
                        nc.tensor.transpose(banks[g % TPB][:, 0:P], rows[:, t, j * P:(j + 1) * P].bitcast(F32),
                                            ident[:]).then_inc(s_tp, 1)
                    with pe.Fori(HB // 4, HB // 2) as i:
                        for j in range(2):
                            bin_sums(i, j)
                    nc.tensor.matmul(counts, zero_b[:], zero_b[:, 0:NT], start=False, stop=True).then_inc(s_hist, 1)

        x_sb = sb("x_sb", [P, NT, D])
        with ExitStack() as ph:
            sbt = sb_in(ph)
            agg = sbt("agg", [P, NW * P])
            xT = sbt("xT", [P, NP])
            ws = [sbt(f"w{k}", [D, D]) for k in range(3)]
            bs = [sbt(f"b{k}", [D, 1]) for k in range(3)]
            hs = x_sb
            idx = sbt("idx", [P, U], I32)
            msg = sbt("msg", [P, U, D])
            hot = sbt("hot", [P, U, P])
            v1_sb, v2_sb = sbt("v1_sb", [D, D]), sbt("v2_sb", [D, D])
            c1_sb = sbt("c1_sb", [D, 1])
            c1_less = sbt("c1_less", [D, 1])
            c2_row = sbt("c2_row", [3, C4, D])
            c2_parts = sbt("c2_parts", [3, C4, D], BF16)
            c2_rest = sbt("c2_rest", [3, C4, D])
            mask3 = sbt("mask3", [3, 3])
            c2_part = sbt("c2_part", [3, C4, D], BF16)
            s_parts3 = sem("s_c2_parts")
            ones_r = sbt("ones_r", [3, P], BF16)
            center = sbt("center", [P, 1])
            halves = sbt("halves", [P, 1])
            dist = sbt("dist", [P, BLK])
            sq = sbt("sq", [P, BLK])
            basis = sbt("basis", [P, BLK])
            t1, e1, s1 = sbt("t1", [P, BLK]), sbt("e1", [P, BLK]), sbt("s1", [P, BLK])
            t2, e2 = sbt("t2", [P, BLK]), sbt("e2", [P, BLK])
            y2 = sbt("y2", [P, C4, D])
            ef = sbt("ef", [P, C4, D])
            g_out = sbt("g_out", [P, C4, D])
            ps1, ps2 = banks[2], banks[3]
            slots = banks[0:2] + banks[4:8]

            s_x, s_w, s_cst, s_xt, s_xtc = (sem(n) for n in ("s_x", "s_w", "s_cst", "s_xt", "s_xtc"))
            s_hp, s_hc, s_hst = sem("s_h_in_psum"), sem("s_h_copied"), sem("s_h_stored")
            s_zero, s_scaled, s_relu = sem("s_agg_zeroed"), sem("s_agg_scaled"), sem("s_x_ready")
            s_idx, s_group = sem("s_idx_ready"), sem("s_group_begun")
            s_gat = [sem(f"s_gathered{u}") for u in range(U)]
            s_hot, s_mm, s_acc = sem("s_hot_ready"), sem("s_summed"), sem("s_accumulated")
            s_dist, s_sqr, s_bas, s_z1, s_t1, s_e1, s_l1, s_s1 = (sem(n) for n in (
                "s_dist_in", "s_squared", "s_basis", "s_z1", "s_t1", "s_e1", "s_l1", "s_s1"))
            s_z2, s_t2_, s_e2, s_l2_, s_y2, s_ef, s_g, s_gst = (sem(n) for n in (
                "s_z2", "s_t2_", "s_e2", "s_l2_", "s_y2", "s_ef_in", "s_g_ready", "s_g_stored"))
            s_ft, s_ln, s_bn, s_rv, s_sd, s_x1, s_x1d = (sem(n) for n in (
                "s_back", "s_resid", "s_moments", "s_recip", "s_rstd", "s_x1", "s_x1d"))
            mom = sbt("mom", [P, NT, 2])
            stat = sbt("stat", [P, NT, 6])
            rstd = sbt("rstd", [P, NT])

            HGRP = 4
            groups = [(a, min(a + HGRP, NT)) for a in range(0, NT, HGRP)]
            NG = len(groups)
            filters = [ITS, ITS, FULL // FB - 2 * ITS]
            assert FULL % FB == 0 and 0 < filters[2] <= ITS
            XCH = 7
            XW = NP // XCH

            wt_row = wt_d.rearrange("(a b) -> a b", a=1)
            g_rows = g_d.rearrange("(b p c) d -> p b c d", c=C4, p=P)
            ef_rows = edge_attr[0:FULL * BLK, :].rearrange("(b p c) d -> p b c d", c=C4, p=P)
            h_rows = h_d.rearrange("(t p) d -> p t d", p=P)
            x1_rows = x1_d.rearrange("(t p) d -> p t d", p=P)

            with nc.Block() as block:
                @block.sync
                def _(sp):
                    lastp = N - (NT - 1) * P
                    sp.wait_ge(s_cst, 1)
                    sp.dma_start(x_sb[:, 0:NT - 1, :], x[0:(NT - 1) * P, :].rearrange("(t p) d -> p t d", p=P)
                                 ).then_inc(s_x, 16)
                    sp.dma_start(x_sb[0:lastp, NT - 1, :], x[(NT - 1) * P:N, :]).then_inc(s_x, 16)
                    col = lambda b: b.rearrange("(a b) -> a b", b=1)
                    row = lambda b: b.rearrange("(a b) -> a b", a=1)
                    for tile, ap in zip(ws + [v1_sb, v2_sb], (w1, w2, w3, v1, v2)):
                        sp.dma_start(tile[:], ap).then_inc(s_w, 16)
                    for tile, ap in zip(bs + [c1_sb], (b1, b2, b3, c1)):
                        sp.dma_start(tile[:], col(ap)).then_inc(s_w, 16)
                    for c in range(C4):
                        sp.dma_start(c2_row[:, c, :], row(c2).to_broadcast([3, D])).then_inc(s_w, 16)
                    sp.dma_start(dist[:], wt_row[:, 0:BLK].to_broadcast([P, BLK])).then_inc(s_dist, 16)
                    sp.dma_start(ef[:], ef_rows[:, 0]).then_inc(s_ef, 16)

                    with sp.Fori(0, FULL - 1) as b:
                        sp.wait_ge(s_sqr, b + 1)
                        sp.dma_start(dist[:], wt_row[:, bass.ds((b + 1) * BLK, BLK)].to_broadcast([P, BLK])
                                     ).then_inc(s_dist, 16)
                        sp.wait_ge(s_g, b + 1)
                        sp.dma_start(g_rows[:, bass.ds(b, 1)], g_out[:].unsqueeze(1)).then_inc(s_gst, 16)
                        sp.dma_start(ef[:].unsqueeze(1), ef_rows[:, bass.ds(b + 1, 1)]).then_inc(s_ef, 16)
                    sp.wait_ge(s_sqr, FULL)
                    sp.dma_start(dist[:], wt_row[:, FULL * BLK:EP].to_broadcast([P, BLK])).then_inc(s_dist, 16)
                    sp.wait_ge(s_g, FULL)
                    sp.dma_start(g_rows[:, FULL - 1], g_out[:]).then_inc(s_gst, 16)
                    sp.wait_ge(s_g, FULL + 1)
                    sp.dma_start(ef[0:TAIL // C4], edge_attr[FULL * BLK:E, :].rearrange("(p c) d -> p c d", c=C4)
                                 ).then_inc(s_ef, 16)
                    sp.wait_ge(s_g, FULL + 2)
                    sp.dma_start(g_rows[:, FULL], g_out[:]).then_inc(s_gst, 16)
                    sp.wait_ge(s_gst, 16 * (FULL + 2))

                @block.gpsimd
                def _(pool):
                    nc.gpsimd.tensor_copy(idx[:, 0:H], steps_src[:, 0:H]).then_inc(s_idx, 1)
                    for k in range(3):
                        if k:
                            pool.wait_ge(s_relu, XCH * k)
                        nc.gpsimd.memset(agg[:], 0.0).then_inc(s_zero, 1)
                        pool.wait_ge(s_hst, 16 * XCH * (k + 1))
                        with pool.Fori(0, ITS) as it:
                            for g in range(G):
                                pool.wait_ge(s_idx, it * G + (G * ITS * k + g + 1))
                                pool.wait_ge(s_mm, it * U + (GATHERS * k + (g + 2) * H))
                                pool.sem_inc(s_group, 1)
                                nxt = (g + 1) % G * H
                                nc.gpsimd.tensor_copy(idx[:, nxt:nxt + H],
                                                      steps_src[:, bass.ds(it * U + (g + 1) * H, H)]).then_inc(s_idx, 1)
                                for u in range(g * H, (g + 1) * H):
                                    pool.indirect_dma_start(
                                        out=msg[:, u, :], out_offset=None, in_=h_d,
                                        in_offset=bass.IndirectOffsetOnAxis(ap=idx[:, u:u + 1], axis=0)
                                    ).then_inc(s_gat[u], 16)

                @block.scalar
                def _(act):
                    def basis_of(b):
                        act.wait_ge(s_dist, b * 16 + 16)
                        nc.scalar.activation(sq[:], dist[:], ACT.Square, bias=center[:]).then_inc(s_sqr, 1)
                        act.wait_ge(s_sqr, b + 1)
                        nc.scalar.activation(basis[:], sq[:], ACT.Exp, scale=COEFF).then_inc(s_bas, 1)

                    def soft(b, t, e, s_in, s_exp, s_out):
                        act.wait_ge(s_in, b + 1)
                        nc.scalar.activation(e[:], t[:], ACT.Exp).then_inc(s_exp, 1)
                        act.wait_ge(s_exp, b + 1)
                        nc.scalar.activation(t[:], e[:], ACT.Ln, bias=halves[:], scale=0.5).then_inc(s_out, 1)

                    act.wait_ge(s_cst, 1)
                    for k in range(3):
                        for j in range(XCH):
                            a, b = j * NT // XCH, (j + 1) * NT // XCH
                            act.wait_ge(s_hc, NG * k + -(-b // HGRP))
                            act.dma_start(h_rows[:, a:b, :], hs[:, a:b, :]).then_inc(s_hst, 16)

                        if k == 2:
                            act.wait_ge(s_hst, 16 * XCH * 3)
                            act.dma_start(x_sb[:, 0:NT - 1, :], x[0:(NT - 1) * P, :].rearrange(
                                "(t p) d -> p t d", p=P)).then_inc(s_x, 16)
                            act.dma_start(x_sb[0:N - (NT - 1) * P, NT - 1, :], x[(NT - 1) * P:N, :]).then_inc(s_x, 16)

                        nc.scalar.preload_act_table_set("natural_log_exp_and_others")
                        with act.Fori(0, filters[k]) as it:
                            for f in range(FB):
                                b = it * FB + (ITS * FB * k + f)
                                basis_of(b)
                                soft(b, t1, e1, s_t1, s_e1, s_l1)
                                soft(b, t2, e2, s_t2_, s_e2, s_l2_)
                        for j in range(XCH):
                            act.wait_ge(s_scaled, XCH * k + j + 1)
                            nc.scalar.activation(xT[:, j * XW:(j + 1) * XW], agg[:, j * XW:(j + 1) * XW],
                                                 ACT.Relu if k < 2 else ACT.Identity, bias=bs[k][:]
                                                 ).then_inc(s_relu, 1)
                    basis_of(FULL)
                    soft(FULL, t1, e1, s_t1, s_e1, s_l1)
                    soft(FULL, t2, e2, s_t2_, s_e2, s_l2_)
                    act.wait_ge(s_rv, 1)
                    nc.scalar.activation(rstd[:], rstd[:], ACT.Sqrt).then_inc(s_sd, 1)
                    for j in range(XCH):
                        act.wait_ge(s_x1, j + 1)
                        act.dma_start(x1_rows[:, 7 * j:7 * j + 7, :], x_sb[:, 7 * j:7 * j + 7, :]).then_inc(s_x1d, 16)
                    act.wait_ge(s_x1d, 16 * XCH)

                @block.tensor
                def _(pe):
                    def z1(b):
                        pe.wait_ge(s_bas, b + 1)
                        nc.tensor.matmul(ps1[:], v1_sb[:], basis[:], start=True, stop=True).then_inc(s_z1, 1)

                    def z2(b):
                        pe.wait_ge(s_s1, b + 1)
                        nc.tensor.matmul(ps2[:], ones_r[:], c2_parts[:].rearrange("p c d -> p (c d)"),
                                         start=True, stop=False)
                        s1_c = s1[:].rearrange("f (e c) -> f c e", c=C4)
                        for c in range(C4):
                            last = nc.tensor.matmul(ps2[:, c * D:(c + 1) * D], s1_c[:, c, :], v2_sb[:],
                                                    start=False, stop=(c == C4 - 1))
                        last.then_inc(s_z2, 1)

                    pe.wait_ge(s_cst, 1)
                    pe.wait_ge(s_x, 32)
                    pe.wait_ge(s_w, 16 * 13)
                    pe.sem_inc(s_mm, U)
                    for g, (a, b) in enumerate(groups):
                        if g >= 2:
                            pe.wait_ge(s_xtc, g - 1)
                        for t in range(a, b):
                            last = nc.tensor.transpose(banks[4 + g % 2][:, (t - a) * P:(t - a + 1) * P], x_sb[:, t, :],
                                                       ident[:])
                        last.then_inc(s_xt, 1)
                    pe.wait_ge(s_xtc, NG)
                    for k in range(3):
                        for g, (a, b) in enumerate(groups):
                            if k:
                                pe.wait_ge(s_relu, XCH * (k - 1) + -(-b * P // XW))
                            if g >= 2:
                                pe.wait_ge(s_hc, NG * k + g - 1)
                            for t in range(a, b):
                                last = nc.tensor.matmul(banks[4 + g % 2][:, (t - a) * D:(t - a + 1) * D],
                                                        xT[:, t * P:(t + 1) * P], ws[k][:], start=True, stop=True)
                            last.then_inc(s_hp, 1)

                        def iteration(it, filtered):
                            for u in range(U):
                                pe.wait_ge(s_gat[u], it * 16 + 16 * (ITS * k + 1))
                                if u % H == 0:
                                    pe.wait_ge(s_hot, it * G + (G * ITS * k + u // H + 1))
                                if u % J == 0:
                                    pe.wait_ge(s_acc, it * SU + (STEPS * k + u // J + 1))
                                nc.tensor.matmul(slots[u // J % SLOTS][:, 0:P], msg[:, u, :], hot[:, u, :],
                                                 start=(u % J == 0), stop=(u % J == J - 1)).then_inc(s_mm, 1)
                                if filtered and u % (U // FB) == J - 1:
                                    z1(it * FB + (ITS * FB * k + u // (U // FB)))
                                if filtered and u % (U // FB) == 4 * J - 1:
                                    z2(it * FB + (ITS * FB * k + u // (U // FB)))

                        with pe.Fori(0, filters[k]) as it:
                            iteration(it, True)
                        if filters[k] < ITS:
                            with pe.Fori(filters[k], ITS) as it:
                                iteration(it, False)
                    z1(FULL)
                    z2(FULL)
                    pe.wait_ge(s_relu, XCH * 3)
                    for g, (a, b) in enumerate(groups):
                        if g >= 2:
                            pe.wait_ge(s_ln, g - 1)
                        for t in range(a, b):
                            last = nc.tensor.transpose(banks[4 + g % 2][:, (t - a) * P:(t - a + 1) * P],
                                                       xT[:, t * P:(t + 1) * P], ident[:])
                        last.then_inc(s_ft, 1)

                @block.vector
                def _(dve):
                    nc.vector.memset(x_sb[:, NT - 1, :], 0.0)
                    nc.vector.memset(halves[:], 0.5)
                    nc.vector.memset(ones_r[:], 1.0)
                    nc.vector.tensor_scalar(center[:], pcol[:], -DELTA, None, ALU.mult).then_inc(s_cst, 1)
                    dve.sem_inc(s_acc, SLOTS)
                    dve.sem_inc(s_gst, 16)
                    dve.wait_ge(s_w, 16 * 13)
                    parts = [0]

                    def then(ins):
                        parts[0] += 1
                        ins.then_inc(s_parts3, 1)
                        dve.wait_ge(s_parts3, parts[0])

                    for i in range(3):
                        nc.vector.tensor_scalar(mask3[:, i:i + 1], pcol[0:3, 0:1], float(i), None, ALU.is_equal)
                        then(nc.vector.tensor_copy(c2_part[:], c2_row[:]))
                        then(nc.vector.tensor_tensor(c2_row[:], c2_row[:], c2_part[:], ALU.subtract))
                        if i == 0:
                            then(nc.vector.tensor_scalar(c2_rest[:], c2_part[:], mask3[:, 0:1], None, ALU.mult))
                        else:
                            then(nc.vector.scalar_tensor_tensor(c2_rest[:], c2_part[:], mask3[:, i:i + 1], c2_rest[:],
                                                                ALU.mult, ALU.add))
                    nc.vector.tensor_copy(c2_parts[:], c2_rest[:]).then_inc(s_parts3, 1)
                    nc.vector.tensor_scalar(c1_less[:], c1_sb[:], -LN2, None, ALU.add)
                    for g, (a, b) in enumerate(groups):
                        dve.wait_ge(s_xt, g + 1)
                        nc.vector.tensor_copy(xT[:, a * P:b * P], banks[4 + g % 2][:, 0:(b - a) * P]).then_inc(s_xtc, 1)

                    def min1(b):
                        dve.wait_ge(s_z1, b + 1)
                        nc.vector.tensor_scalar(t1[:], ps1[:], c1_sb[:], SOFT_MAX, ALU.add, ALU.min).then_inc(s_t1, 1)

                    def max1(b):
                        dve.wait_ge(s_l1, b + 1)
                        nc.vector.scalar_tensor_tensor(s1[:], ps1[:], c1_less[:], t1[:], ALU.add,
                                                       ALU.max).then_inc(s_s1, 1)

                    def min2(b):
                        dve.wait_ge(s_z2, b + 1)
                        nc.vector.tensor_scalar(t2[:], ps2[:], SOFT_MAX, None, ALU.min).then_inc(s_t2_, 1)

                    def max2(b):
                        dve.wait_ge(s_l2_, b + 1)
                        nc.vector.scalar_tensor_tensor(y2[:].rearrange("p c d -> p (c d)"), ps2[:], -LN2, t2[:],
                                                       ALU.add, ALU.max).then_inc(s_y2, 1)

                    def weigh_all(b):
                        dve.wait_ge(s_y2, b + 1)
                        dve.wait_ge(s_ef, b * 16 + 16)
                        dve.wait_ge(s_gst, b * 16 + 16)
                        for c in range(C4):
                            cut = edge_cut[:].rearrange("p b c -> p (b c)")[:, bass.ds(b * C4 + c, 1)]
                            last = nc.vector.scalar_tensor_tensor(g_out[:, c, :], y2[:, c, :], cut, ef[:, c, :],
                                                                  ALU.mult, ALU.mult)
                        last.then_inc(s_g, 1)

                    for k in range(3):
                        if k:
                            dve.wait_ge(s_hst, 16 * XCH * k)
                        for g, (a, b) in enumerate(groups):
                            dve.wait_ge(s_hp, NG * k + g + 1)
                            nc.vector.tensor_tensor(
                                hs[:, a:b, :], banks[4 + g % 2][:, 0:(b - a) * D].rearrange("p (t d) -> p t d", d=D),
                                norm_src[:, a:b].unsqueeze(2).to_broadcast([P, b - a, D]), ALU.mult).then_inc(s_hc, 1)

                        def one_hots(it, g):
                            dve.wait_ge(s_mm, it * U + (GATHERS * k + (g + 1) * H))
                            nc.vector.tensor_tensor(
                                hot[:, g * H:(g + 1) * H, :],
                                steps_dst[:, bass.ds(it * U + g * H, H)].unsqueeze(2).to_broadcast([P, H, P]),
                                iota_f[:].unsqueeze(1).to_broadcast([P, H, P]), ALU.is_equal).then_inc(s_hot, 1)

                        def iteration(it, filtered):
                            per = SU // FB
                            beside = {1: (min1,), 2: (max1,), 4: (min2,), 5: (max2, weigh_all)}
                            one_hots(it, 0)
                            wins = nc.values_load_multi_w_load_instructions(
                                windows[0:1, bass.ds(it * SU, SU)], engines=[mybir.EngineType.DVE],
                                min_val=0, max_val=NW - 1)[1]
                            for u in range(SU):
                                dve.wait_ge(s_mm, it * U + (GATHERS * k + U + (u + 1) * J))
                                dve.wait_ge(s_acc, it * SU + (STEPS * k + SLOTS + u))
                                into = agg[:, bass.ds(wins[u] * P, P)]
                                nc.vector.tensor_tensor(into, into, slots[u % SLOTS][:, 0:P], ALU.add
                                                        ).then_inc(s_acc, 1)
                                if u % (H // J) == 0 and u // (H // J) < G - 1:
                                    one_hots(it, u // (H // J) + 1)
                                if filtered:
                                    for work in beside.get(u % per, ()):
                                        work(it * FB + (ITS * FB * k + u // per))

                        dve.wait_ge(s_zero, k + 1)
                        with dve.Fori(0, filters[k]) as it:
                            iteration(it, True)
                        if filters[k] < ITS:
                            with dve.Fori(filters[k], ITS) as it:
                                iteration(it, False)
                        dve.wait_ge(s_acc, STEPS * (k + 1) + SLOTS)
                        for j in range(XCH):
                            part = agg[:, j * XW:(j + 1) * XW]
                            nc.vector.tensor_tensor(part, part, norm_dst[:, j * XW:(j + 1) * XW],
                                                    ALU.mult).then_inc(s_scaled, 1)
                    dve.wait_ge(s_gst, 16 * (FULL + 1))
                    nc.vector.memset(ef[:], 0.0).then_inc(s_g, 1)
                    min1(FULL)
                    max1(FULL)
                    min2(FULL)
                    max2(FULL)
                    dve.wait_ge(s_y2, FULL + 1)
                    dve.wait_ge(s_ef, 16 * (FULL + 1))
                    for c in range(C4):
                        last = nc.vector.scalar_tensor_tensor(g_out[:, c, :], y2[:, c, :], edge_cut[:, FULL, c:c + 1],
                                                              ef[:, c, :], ALU.mult, ALU.mult)
                    last.then_inc(s_g, 1)
                    dve.wait_ge(s_x, 64)
                    for g, (a, b) in enumerate(groups):
                        dve.wait_ge(s_ft, g + 1)
                        nc.vector.tensor_tensor(x_sb[:, a:b, :], x_sb[:, a:b, :],
                                                banks[4 + g % 2][:, 0:(b - a) * D].rearrange("p (t d) -> p t d", d=D),
                                                ALU.add).then_inc(s_ln, 1)
                    dve.wait_ge(s_ln, NG)
                    for t in range(NT):
                        last = nc.vector.bn_stats(stat[:, t, :], x_sb[:, t, :])
                    last.then_inc(s_bn, 1)
                    dve.wait_ge(s_bn, 1)
                    for t in range(NT):
                        last = nc.vector.bn_aggr(mom[:, t, :], stat[:, t, :])
                    last.then_inc(s_bn, 1)
                    dve.wait_ge(s_bn, 2)
                    nc.vector.tensor_scalar(rstd[:], mom[:, :, 1], EPS, None, ALU.add).then_inc(s_bn, 1)
                    dve.wait_ge(s_bn, 3)
                    nc.vector.reciprocal(rstd[:], rstd[:]).then_inc(s_rv, 1)
                    dve.wait_ge(s_sd, 1)
                    for t in range(NT):
                        last = nc.vector.tensor_scalar(x_sb[:, t, :], x_sb[:, t, :], mom[:, t, 0:1], rstd[:, t:t + 1],
                                                       ALU.subtract, ALU.mult)
                        if t % 7 == 6:
                            last.then_inc(s_x1, 1)

        with ExitStack() as ph:
            sbt = sb_in(ph)
            R = AHEAD
            idx = sbt("idx4", [P, R, C4], I32)
            hgat = sbt("hgat", [P, R, C4, D])
            filt = sbt("filt", [P, R, C4, D])
            u_same = sbt("u_same", [P, R, C4, D])
            u_first = sbt("u_first", [P, R, C4, D])
            first_sb = sbt("first_sb", [P, R, BLK])
            run = sbt("run", [P, R, BLK])
            run_out = sbt("run_out", [P, R, C4, D])
            psame, pfirst = banks[0:R], banks[R:2 * R]
            prun = pfirst
            s_i, s_u, s_ts, s_fc, s_sc, s_tr, s_ro = (sem(n) for n in (
                "s_index4", "s_factors", "s_factors_T", "s_first_copied", "s_scanned", "s_run_T", "s_run_out"))
            s_turn = sem("s_gathers_begun")
            s_fi = [sem(f"s_filt_in{r}") for r in range(R)]
            s_gt = [[sem(f"s_hgat{r}_{c}") for c in range(C4)] for r in range(R)]
            s_rst = [sem(f"s_run_stored{r}") for r in range(R)]
            g_rows = g_d.rearrange("(b p c) d -> p b c d", c=C4, p=P)
            run_rows = run_d[0:EP, :].rearrange("(b p c) d -> p b c d", c=C4, p=P)
            LOOPS = (NB - 1) // R
            assert LOOPS * R == NB - 1 and R % 2
            with nc.Block() as block:
                @block.sync
                def _(sp):
                    def load(b, r):
                        sp.wait_ge(s_u, b + 1)
                        sp.dma_start(filt[:, r].unsqueeze(1), g_rows[:, bass.ds(b, 1)]).then_inc(s_fi[r], 16)

                    with sp.Fori(0, LOOPS) as i:
                        for r in range(R):
                            load(i * R + r, r)
                    load(NB - 1, 0)

                @block.gpsimd
                def _(pool):
                    def gather(b, r):
                        pool.wait_ge(s_i, b + 1)
                        pool.sem_inc(s_turn, 1)
                        for c in range(C4):
                            pool.indirect_dma_start(out=hgat[:, r, c, :], out_offset=None, in_=x1_d,
                                                    in_offset=bass.IndirectOffsetOnAxis(ap=idx[:, r, c:c + 1], axis=0)
                                                    ).then_inc(s_gt[r][c], 16)

                    with pool.Fori(0, LOOPS) as i:
                        for r in range(R):
                            gather(i * R + r, r)
                    gather(NB - 1, 0)

                @block.scalar
                def _(act):
                    def copy_idx(b, r):
                        act.wait_ge(s_u, b + 1)
                        nc.scalar.copy(idx[:, r:r + 1, :], edge_src[:, bass.ds(b, 1), :]).then_inc(s_i, 1)

                    def copy_first(b, r):
                        act.wait_ge(s_ts, b + (R + 1))
                        act.wait_ge(s_sc, b + 1)
                        nc.scalar.copy(first_sb[:, r, :], pfirst[r][:]).then_inc(s_fc, 1)

                    def store_run(b, r, stored):
                        act.wait_ge(s_tr, b + (R + 1))
                        act.wait_ge(s_rst[r], stored)
                        nc.scalar.copy(run_out[:, r].rearrange("p c d -> p (c d)"), prun[r][:]).then_inc(s_ro, 1)
                        act.wait_ge(s_ro, b + (R + 1))
                        act.dma_start(run_rows[:, bass.ds(b, 1)], run_out[:, r].unsqueeze(1)).then_inc(s_rst[r], 16)

                    act.sem_inc(s_ro, R)
                    for r in range(R):
                        act.sem_inc(s_rst[r], 16)
                        copy_idx(r, r)
                    copy_first(0, 0)
                    with act.Fori(0, LOOPS) as i:
                        for r in range(R):
                            b = i * R + r
                            copy_idx(b + R, r)
                            copy_first(b + 1, (r + 1) % R)
                            store_run(b, r, i * 16 + 16)
                    store_run(NB - 1, 0, LOOPS * 16 + 16)
                    act.wait_ge(s_rst[0], LOOPS * 16 + 32)
                    for r in range(1, R):
                        act.wait_ge(s_rst[r], LOOPS * 16 + 16)

                @block.tensor
                def _(pe):
                    def turn(b, r):
                        pe.wait_ge(s_u, b + (R + 1))
                        pe.wait_ge(s_ro, b + 1)
                        for bank, fac in ((pfirst[r], u_first), (psame[r], u_same)):
                            view = bank[:].rearrange("p (e c) -> p c e", c=C4)
                            for c in range(C4):
                                last = nc.tensor.transpose(view[:, c, :], fac[:, r, c, :], ident[:])
                        last.then_inc(s_ts, 1)

                    def back(b, r):
                        pe.wait_ge(s_sc, b + (R + 1))
                        view = run[:, r, :].rearrange("p (e c) -> p c e", c=C4)
                        bank = prun[r]
                        for c in range(C4):
                            last = nc.tensor.transpose(bank[:, c * P:(c + 1) * P], view[:, c, :], ident[:])
                        last.then_inc(s_tr, 1)

                    pe.sem_inc(s_ts, R)
                    pe.sem_inc(s_tr, R)
                    turn(0, 0)
                    with pe.Fori(0, LOOPS) as i:
                        for r in range(R):
                            b = i * R + r
                            turn(b + 1, (r + 1) % R)
                            back(b, r)
                    back(NB - 1, 0)

                @block.vector
                def _(dve):
                    same = edge_same[:].rearrange("p b c -> p (b c)")
                    first = edge_first[:].rearrange("p b c -> p (b c)")

                    def factors(b, r, nth):
                        for c in range(C4):
                            dve.wait_ge(s_gt[r][c], nth)
                        dve.wait_ge(s_fi[r], nth)
                        dve.wait_ge(s_ts, b + 1)
                        for out_, mask in ((u_same, same), (u_first, first)):
                            for c in range(C4):
                                last = nc.vector.scalar_tensor_tensor(
                                    out_[:, r, c, :], hgat[:, r, c, :], mask[:, bass.ds(b * C4 + c, 1)],
                                    filt[:, r, c, :], ALU.mult, ALU.mult)
                        last.then_inc(s_u, 1)

                    def scan(b, r):
                        dve.wait_ge(s_fc, b + 1)
                        dve.wait_ge(s_tr, b + 1)
                        dve.wait_ge(s_sc, b + R)
                        nc.vector.tensor_tensor_scan(run[:, r, :], psame[r][:], first_sb[:, r, :],
                                                     run[:, (r - 1) % R, BLK - 1:BLK], ALU.mult, ALU.add
                                                     ).then_inc(s_sc, 1)

                    nc.vector.memset(run[:, R - 1, BLK - 1:BLK], 0.0).then_inc(s_sc, R)
                    dve.sem_inc(s_u, R)
                    factors(0, 0, 16)
                    with dve.Fori(0, LOOPS) as i:
                        for r in range(R):
                            b = i * R + r
                            factors(b + 1, (r + 1) % R, i * 16 + (32 if r == R - 1 else 16))
                            scan(b, r)
                    scan(NB - 1, 0)

        with ExitStack() as ph:
            sbt = sb_in(ph)
            prod = sbt("prod", [P, NT, D])
            prodT = sbt("prodT", [P, 2, HGRP * P])
            v3_sb = sbt("v3_sb", [D, D])
            c3_row = sbt("c3_row", [1, D])
            ones_r = sbt("ones_r5", [1, P])
            halves = sbt("halves5", [P, 1])
            zmin = sbt("zmin", [P, NT, D])
            zall = sbt("zall", [P, NT, D])
            mom = sbt("mom5", [P, NT, 2])
            stat = sbt("stat5", [P, NT, 6])
            rstd = sbt("rstd5", [P, NT])
            s_w5, s_pg, s_pt, s_ptc, s_z, s_zc, s_ex, s_lg, s_l5, s_q5, s_r5, s_y, s_out = (sem(n) for n in (
                "s_w5", "s_prod_in", "s_prodT", "s_prodT_copied", "s_z3", "s_z3_copied", "s_exp3", "s_log3",
                "s_l5", "s_recip5", "s_rstd5", "s_out_ready", "s_out_stored"))
            with nc.Block() as block:
                @block.sync
                def _(sp):
                    sp.dma_start(v3_sb[:], v3).then_inc(s_w5, 16)
                    sp.dma_start(c3_row[:], c3.rearrange("(a b) -> a b", a=1)).then_inc(s_w5, 16)
                    for j in range(7):
                        sp.wait_ge(s_y, j + 1)
                        a, b = 7 * j, 7 * j + 7
                        full = min(b, NT - 1)
                        sp.dma_start(out[a * P:full * P, :].rearrange("(t p) d -> p t d", p=P),
                                     x_sb[:, a:full, :]).then_inc(s_out, 16)
                    sp.dma_start(out[(NT - 1) * P:N, :], x_sb[0:N - (NT - 1) * P, NT - 1, :]).then_inc(s_out, 16)
                    sp.wait_ge(s_out, 16 * 8)

                @block.gpsimd
                def _(pool):
                    nc.gpsimd.memset(ones_r[:], 1.0)
                    nc.gpsimd.memset(halves[:], 0.5).then_inc(s_w5, 1)
                    for t in range(NT):
                        pool.indirect_dma_start(out=prod[:, t, :], out_offset=None, in_=run_d,
                                                in_offset=bass.IndirectOffsetOnAxis(ap=last_row[:, t:t + 1], axis=0)
                                                ).then_inc(s_pg, 16)

                @block.tensor
                def _(pe):
                    pe.wait_ge(s_w5, 33)
                    pe.wait_ge(s_pg, 16 * NT)
                    for g, (a, b) in enumerate(groups):
                        if g >= 2:
                            pe.wait_ge(s_ptc, g - 1)
                        for t in range(a, b):
                            last = nc.tensor.transpose(banks[g % 2][:, (t - a) * P:(t - a + 1) * P], prod[:, t, :],
                                                       ident[:])
                        last.then_inc(s_pt, 1)
                        pe.wait_ge(s_ptc, g + 1)
                        if g >= 2:
                            pe.wait_ge(s_zc, g - 1)
                        for t in range(a, b):
                            z = banks[2 + g % 2][:, (t - a) * D:(t - a + 1) * D]
                            nc.tensor.matmul(z, ones_r[:], c3_row[:], start=True, stop=False)
                            last = nc.tensor.matmul(z, prodT[:, g % 2, (t - a) * P:(t - a + 1) * P], v3_sb[:],
                                                    start=False, stop=True)
                        last.then_inc(s_z, 1)

                @block.scalar
                def _(act):
                    act.wait_ge(s_zc, NG)
                    for j in range(7):
                        part = zmin[:, 7 * j:7 * j + 7, :]
                        nc.scalar.activation(part, part, ACT.Exp).then_inc(s_ex, 1)
                        act.wait_ge(s_ex, j + 1)
                        nc.scalar.activation(part, part, ACT.Ln, bias=halves[:], scale=0.5).then_inc(s_lg, 1)
                    act.wait_ge(s_q5, 1)
                    nc.scalar.activation(rstd[:], rstd[:], ACT.Sqrt).then_inc(s_r5, 1)

                @block.vector
                def _(dve):
                    for g, (a, b) in enumerate(groups):
                        dve.wait_ge(s_pt, g + 1)
                        if g >= 2:
                            dve.wait_ge(s_z, g - 1)
                        nc.vector.tensor_copy(prodT[:, g % 2, 0:(b - a) * P], banks[g % 2][:, 0:(b - a) * P]
                                              ).then_inc(s_ptc, 1)
                        dve.wait_ge(s_z, g + 1)
                        z = banks[2 + g % 2][:, 0:(b - a) * D].rearrange("p (t d) -> p t d", d=D)
                        nc.vector.tensor_scalar(zmin[:, a:b, :], z, SOFT_MAX, None, ALU.min)
                        nc.vector.tensor_scalar(zall[:, a:b, :], z, -LN2, None, ALU.add).then_inc(s_zc, 1)
                    dve.wait_ge(s_zc, NG)
                    for j in range(7):
                        dve.wait_ge(s_lg, j + 1)
                        sl = slice(7 * j, 7 * j + 7)
                        nc.vector.tensor_tensor(zall[:, sl, :], zall[:, sl, :], zmin[:, sl, :], ALU.max).then_inc(s_l5, 1)
                        dve.wait_ge(s_l5, 2 * j + 1)
                        nc.vector.tensor_tensor(x_sb[:, sl, :], x_sb[:, sl, :], zall[:, sl, :], ALU.add).then_inc(s_l5, 1)
                        dve.wait_ge(s_l5, 2 * j + 2)
                        for t in range(7 * j, 7 * j + 7):
                            last = nc.vector.bn_stats(stat[:, t, :], x_sb[:, t, :])
                    last.then_inc(s_l5, 1)
                    dve.wait_ge(s_l5, 15)
                    for t in range(NT):
                        last = nc.vector.bn_aggr(mom[:, t, :], stat[:, t, :])
                    last.then_inc(s_l5, 1)
                    dve.wait_ge(s_l5, 16)
                    nc.vector.tensor_scalar(rstd[:], mom[:, :, 1], EPS, None, ALU.add).then_inc(s_l5, 1)
                    dve.wait_ge(s_l5, 17)
                    nc.vector.reciprocal(rstd[:], rstd[:]).then_inc(s_q5, 1)
                    dve.wait_ge(s_r5, 1)
                    for t in range(NT):
                        last = nc.vector.tensor_scalar(x_sb[:, t, :], x_sb[:, t, :], mom[:, t, 0:1], rstd[:, t:t + 1],
                                                       ALU.subtract, ALU.mult)
                        if t % 7 == 6:
                            last.then_inc(s_y, 1)


_INS = ["x", "src", "dst", "edge_attr_128", "edge_weight",
        "L0_gnn_W1", "L0_gnn_b1", "L0_gnn_W2", "L0_gnn_b2", "L0_gnn_W3", "L0_gnn_b3",
        "L1_gnn_W1", "L1_gnn_b1", "L1_gnn_W2", "L1_gnn_b2", "L1_gnn_W3", "L1_gnn_b3"]


def kernel(**inputs):
    import concourse.bacc as bacc
    from concourse.bass_utils import run_bass_kernel_spmd

    nc = bacc.Bacc("TRN2", target_bir_lowering=False, num_devices=1)
    arrays, args = {}, []
    for name in _INS:
        a = np.ascontiguousarray(inputs[name])
        arrays[f"in_{name}"] = a
        args.append(nc.dram_tensor(f"in_{name}", a.shape, mybir.dt.from_np(a.dtype), kind="ExternalInput").ap())
    res = nc.dram_tensor("out_x", (N, D), F32, kind="ExternalOutput").ap()
    gnn(nc, *args, res)
    r = run_bass_kernel_spmd(nc, [arrays], core_ids=[0])
    return r.results[0]["out_x"]
```

```python
import math

import numpy as np
import concourse.bass as bass
from concourse import mybir
from contextlib import ExitStack

F32 = mybir.dt.float32
BF16 = mybir.dt.bfloat16
I32 = mybir.dt.int32
ALU = mybir.AluOpType
ACT = mybir.ActivationFunctionType

P = 128
N = 6250
E = 200000
D = 128
NT = -(-N // P)
NP = NT * P
NW = NT + 1
J = 2
CE = J * P
CH = -(-E // CE)
C4 = 4
BLK = P * C4
NB = -(-E // BLK)
EP = NB * BLK
U = 24
H = 8
G = U // H
SU = U // J
ITS = -(-(CH + NT - 1) // SU)
STEPS = ITS * SU
GATHERS = ITS * U
ST = -(-STEPS // P)
FULL = E // BLK
FB = 2
TAIL = E - FULL * BLK
PADNODE = 8191
RT = NT + 1
HG = 17
HB = EP // P // HG
LOW = 64
HIGH = NP // LOW
CUTOFF = 5.0
LN2 = 0.6931471805599453
SLOTS = 6
SOFT_MAX = 18.0
EPS = 1e-5
DELTA = CUTOFF / (D - 1)
AHEAD = 3
COEFF = -0.5 / (DELTA * DELTA)


def gnn(nc, x, src, dst, edge_attr, edge_weight, w1, b1, w2, b2, w3, b3, v1, c1, v2, c2, v3, c3, out):
    scratch = lambda name, shape, dt: nc.dram_tensor(name, shape, dt, kind="Internal").ap()
    src_d = scratch("src_padded", (EP,), I32)
    dst_d = scratch("dst_padded", (EP,), I32)
    prev_d = scratch("dst_of_previous_edge", (EP,), I32)
    wt_d = scratch("weight_padded", (EP,), F32)
    win_d = scratch("step_windows", (ST * P,), I32)
    row_d = scratch("row_starts", (RT * P,), F32)
    norm_d = scratch("norm_of_nodes", (NP,), F32)
    h_d = scratch("h_rows", (NP, D), F32)
    x1_d = scratch("x1_rows", (NP, D), F32)
    g_d = scratch("edge_filter", (EP, D), F32)
    run_d = scratch("running_products", (EP + 1, D), F32)
    ONES_ROW = EP
    src_rows = src_d.rearrange("(c e) -> c e", e=CE)
    dst_rows = dst_d.rearrange("(c e) -> c e", e=CE)

    outer = ExitStack()
    with outer:
        sb_in = lambda stack: (lambda name, shape, dt=F32: stack.enter_context(nc.sbuf_tensor(name, shape, dt)))
        sb = sb_in(outer)
        sem = lambda name: outer.enter_context(nc.semaphore(name))

        ident = sb("ident", [P, P])
        iota_f = sb("iota_f", [P, P])
        pcol = sb("pcol", [P, 1])
        steps_src = sb("steps_src", [P, ST * P * J], I32)
        steps_dst = sb("steps_dst", [P, ST * P * J])
        windows = sb("windows", [1, ST * P], I32)
        edge_src = sb("edge_src", [P, NB + AHEAD, C4], I32)
        edge_same = sb("edge_same", [P, NB, C4])
        edge_first = sb("edge_first", [P, NB, C4])
        last_row = sb("last_row", [P, NT], I32)
        norm_src = sb("norm_src", [P, NT])
        norm_dst = sb("norm_dst", [P, NP])
        banks = [outer.enter_context(nc.psum_tensor(f"bank{i}", [P, 512], F32)) for i in range(8)]

        with ExitStack() as ph:
            sbt = sb_in(ph)
            pad_i = sbt("pad_i", [1, BLK], I32)
            lead_i = sbt("lead_i", [1, 1], I32)
            pad_w = sbt("pad_w", [1, BLK])
            iota_i = sbt("iota_i", [P, P], I32)
            pcol_i = sbt("pcol_i", [P, 1], I32)
            ones_row = sbt("ones_row", [1, D])
            s_pads, s_iota, s_copied, s_const = sem("s_pads"), sem("s_iota"), sem("s_copied"), sem("s_const")
            with nc.Block() as block:
                @block.gpsimd
                def _(pool):
                    nc.gpsimd.memset(pad_i[:], PADNODE)
                    nc.gpsimd.memset(lead_i[:], -1)
                    nc.gpsimd.memset(ones_row[:], 1.0)
                    nc.gpsimd.memset(pad_w[:], 0.0).then_inc(s_pads, 1)
                    nc.gpsimd.iota(iota_i[:], [[1, P]], base=0, channel_multiplier=0)
                    nc.gpsimd.iota(pcol_i[:], [[1, 1]], base=0, channel_multiplier=1).then_inc(s_iota, 1)

                @block.vector
                def _(dve):
                    dve.wait_ge(s_iota, 1)
                    nc.vector.tensor_copy(iota_f[:], iota_i[:])
                    nc.vector.tensor_copy(pcol[:], pcol_i[:]).then_inc(s_const, 1)
                    dve.wait_ge(s_const, 1)
                    nc.vector.tensor_scalar(ident[:], iota_f[:], pcol[:, 0:1], None, ALU.is_equal)

                @block.sync
                def _(sp):
                    sp.dma_start(src_d[0:E].rearrange("(a b) -> a b", a=16),
                                 src.rearrange("(a b) -> a b", a=16)).then_inc(s_copied, 16)
                    for ap in (dst_d[0:E], prev_d[1:E + 1]):
                        sp.dma_start(ap.rearrange("(a b) -> a b", a=16),
                                     dst.rearrange("(a b) -> a b", a=16)).then_inc(s_copied, 16)
                    sp.dma_start(wt_d[0:E].rearrange("(a b) -> a b", a=16),
                                 edge_weight.rearrange("(a b) -> a b", a=16)).then_inc(s_copied, 16)
                    sp.wait_ge(s_pads, 1)
                    row = lambda ap: ap.rearrange("(a b) -> a b", a=1)
                    sp.dma_start(row(src_d[E:EP]), pad_i[:, 0:EP - E]).then_inc(s_copied, 16)
                    sp.dma_start(row(dst_d[E:EP]), pad_i[:, 0:EP - E]).then_inc(s_copied, 16)
                    sp.dma_start(row(prev_d[E + 1:EP]), pad_i[:, 0:EP - E - 1]).then_inc(s_copied, 16)
                    sp.dma_start(row(prev_d[0:1]), lead_i[:]).then_inc(s_copied, 16)
                    sp.dma_start(row(wt_d[E:EP]), pad_w[:, 0:EP - E]).then_inc(s_copied, 16)
                    sp.dma_start(run_d[ONES_ROW:ONES_ROW + 1, :], ones_row[:]).then_inc(s_copied, 16)
                    sp.wait_ge(s_copied, 10 * 16)

        with ExitStack() as ph:
            sbt = sb_in(ph)
            TB = -(-NB // P)
            b_src = sbt("b_src", [P, TB, BLK], I32)
            b_dst = sbt("b_dst", [P, TB, BLK], I32)
            b_prev = sbt("b_prev", [P, TB, BLK], I32)
            b_wt = sbt("b_wt", [P, TB, BLK])
            b_ang = sbt("b_ang", [P, TB, BLK])
            b_in = sbt("b_in", [P, TB, BLK])
            half_pi = sbt("half_pi", [P, 1])
            edge_cut = sbt("edge_cut", [P, NB, C4])
            s_b, s_l2, s_rdy, s_ang, s_sin, s_t2, s_t2c = (sem(n) for n in
                ("s_b", "s_l2", "s_rdy", "s_ang", "s_sin", "s_t2", "s_t2c"))
            rows_of = lambda t: min(P, NB - t * P)
            with nc.Block() as block:
                @block.sync
                def _(sp):
                    views = ((b_src, src_d), (b_dst, dst_d), (b_prev, prev_d),
                             (b_wt, wt_d))
                    for t in range(TB):
                        r = rows_of(t)
                        for tile, flat in views:
                            sp.dma_start(tile[0:r, t, :], flat[t * P * BLK:(t * P + r) * BLK].rearrange(
                                "(b e) -> b e", e=BLK)).then_inc(s_b, 16)
                    sp.wait_ge(s_b, 4 * TB * 16)

                @block.vector
                def _(dve):
                    links = [0]

                    def link(ins):
                        links[0] += 1
                        ins.then_inc(s_l2, 1)
                        dve.wait_ge(s_l2, links[0])

                    nc.vector.memset(half_pi[:], math.pi / 2)
                    nc.vector.memset(edge_src[:, NB:NB + AHEAD, :], 0)
                    dve.wait_ge(s_b, 4 * TB * 16)
                    for t in range(TB):
                        r = rows_of(t)
                        nc.vector.tensor_scalar(b_ang[0:r, t, :], b_wt[0:r, t, :], CUTOFF, None, ALU.min)
                        nc.vector.tensor_scalar(b_in[0:r, t, :], b_wt[0:r, t, :], CUTOFF, None, ALU.is_lt)
                        link(nc.vector.tensor_tensor(b_dst[0:r, t, :].bitcast(F32), b_dst[0:r, t, :],
                                                     b_prev[0:r, t, :], ALU.is_equal))
                        link(nc.vector.tensor_copy(b_src[0:r, t, :].bitcast(F32), b_src[0:r, t, :]))
                    nc.vector.memset(b_prev[0:1, 0, 0:1], 0).then_inc(s_ang, 1)
                    dve.wait_ge(s_sin, TB)
                    for t in range(TB):
                        r = rows_of(t)
                        link(nc.vector.tensor_scalar(b_ang[0:r, t, :], b_ang[0:r, t, :], 0.5, 0.5, ALU.mult, ALU.add))
                        last = nc.vector.tensor_tensor(b_ang[0:r, t, :], b_ang[0:r, t, :], b_in[0:r, t, :], ALU.mult)
                    last.then_inc(s_rdy, 1)
                    for g in range(3 * TB):
                        t, r = g // 3, rows_of(g // 3)
                        dve.wait_ge(s_t2, g + 1)
                        table = (edge_src, edge_same, edge_cut)[g % 3]
                        nc.vector.tensor_copy(table[:, t * P:t * P + r, :].rearrange("p b c -> p c b"),
                                              banks[g % 8][:].rearrange("p (c b) -> p c b", c=C4)[:, :, 0:r]
                                              ).then_inc(s_t2c, 1)
                    dve.wait_ge(s_t2c, 3 * TB)
                    link(nc.vector.tensor_tensor(edge_same[:], edge_same[:], edge_cut[:], ALU.mult))
                    nc.vector.tensor_tensor(edge_first[:], edge_cut[:], edge_same[:], ALU.subtract)

                @block.scalar
                def _(act):
                    act.wait_ge(s_ang, 1)
                    for t in range(TB):
                        r = rows_of(t)
                        nc.scalar.activation(b_ang[0:r, t, :], b_ang[0:r, t, :], ACT.Sin, bias=half_pi[0:r, :],
                                             scale=-math.pi / CUTOFF).then_inc(s_sin, 1)

                @block.tensor
                def _(pe):
                    pe.wait_ge(s_rdy, 1)
                    for g in range(3 * TB):
                        t, r = g // 3, rows_of(g // 3)
                        if g >= 8:
                            pe.wait_ge(s_t2c, g - 7)
                        tile = (b_src[:].bitcast(F32), b_dst[:].bitcast(F32), b_ang[:])[g % 3]
                        for c in range(C4):
                            last = nc.tensor.transpose(banks[g % 8][:, c * P:c * P + r],
                                                       tile[0:r, t, :].rearrange("b (e c) -> b c e", c=C4)[:, c, :],
                                                       ident[0:r, 0:r])
                        last.then_inc(s_t2, 1)

        x_sb = sb("x_sb", [P, NT, D])
        with ExitStack() as ph:
            sbt = sb_in(ph)
            CR = EP // CE
            first_i = sbt("first_i", [1, CR], I32)
            first_w = sbt("first_w", [1, CR], I32)
            chunk_no = sbt("chunk_no", [1, CR], I32)
            first_r = sbt("first_r", [1, CR])
            start_r = sbt("start_r", [1, CR])
            first_b = sbt("first_b", [P, CR])
            start_b = sbt("start_b", [P, CR])
            junk = sbt("junk", [P, CR])
            number_i = sbt("number_i", [P, RT], I32)
            number = sbt("number", [P, RT])
            chunk_f = sbt("chunk_f", [P, ST])
            chunk_i = sbt("chunk_i", [P, ST], I32)
            win_f = sbt("win_f", [P, ST])
            win_i = sbt("win_i", [P, ST], I32)
            base_f = sbt("base_f", [P, ST])
            rowc_f = sbt("rowc_f", [P, RT])
            rowc_i = sbt("rowc_i", [P, RT], I32)
            inrow = sbt("inrow", [P, RT])
            start_f = sbt("start_f", [P, RT])
            end_f = sbt("end_f", [P, NT])
            has_f = sbt("has_f", [P, NT])
            alt_f = sbt("alt_f", [P, NT])
            norm_p = sbt("norm_p", [P, NT])
            srows = sbt("srows", [P, ST, CE], I32)
            drows = sbt("drows", [P, ST, CE], I32)
            nrows = sbt("nrows", [P, RT, CE], I32)
            bins = EP // P
            part_i = sbt("part_i", [P, bins], I32)
            low = sbt("low", [P, bins], BF16)
            high = sbt("high", [P, bins], BF16)
            iota_b = sbt("iota_b", [P, P], BF16)
            zero_b = sbt("zero_b", [P, P], BF16)
            hot_low = sbt("hot_low", [P, 2, HG, LOW], BF16)
            hot_high = sbt("hot_high", [P, 2, HG, HIGH], BF16)
            counts = banks[7][0:LOW, 0:HIGH]
            by_node = banks[0][:, 0:NT]
            counts_sb = sbt("counts_sb", [LOW, HIGH])
            upper = sbt("upper", [LOW, P])
            number_less = sbt("number_less", [P, RT])
            rowsum = sbt("rowsum", [P, RT])
            insum = sbt("insum", [P, RT])
            signs = sbt("signs", [P, CR])
            TPB = 7
            s_first, s_start, s_bc, s_num = (sem(n) for n in ("s_first", "s_start", "s_bc", "s_num"))
            s_chunk, s_srows, s_rel, s_tp, s_tpc = (sem(n) for n in ("s_chunk", "s_srows", "s_rel", "s_tp", "s_tpc"))
            s_win, s_wind, s_winl, s_link = (sem(n) for n in ("s_win", "s_wind", "s_winl", "s_link"))
            s_rowc, s_nrows, s_rs, s_rsd, s_rb = (sem(n) for n in ("s_rowc", "s_nrows", "s_rs", "s_rsd", "s_rb"))
            s_parts, s_bins, s_hist, s_recip, s_root, s_nd = (sem(n) for n in (
                "s_parts", "s_hot_bins", "s_hist", "s_degree_recip", "s_root", "s_norm_stored"))
            s_xpad, s_xin, s_rowsum, s_insum, s_cnt, s_nsrc, s_recip_in = (sem(n) for n in (
                "s_x_padded", "s_x_in", "s_rows_before", "s_edges_before",
                "s_counts_copied", "s_counts_by_node", "s_in_degree_recip"))
            srcs = edge_src[:, 0:NB, :].rearrange("p b c -> p (b c)")
            with nc.Block() as block:
                @block.sync
                def _(sp):
                    with nc.allow_non_contiguous_dma(reason="first dst of every chunk"):
                        sp.dma_start(first_i[:], dst_rows[:, 0:1].rearrange("c o -> o c")).then_inc(s_first, 16)
                    sp.wait_ge(s_xpad, 1)
                    sp.dma_start(x_sb[:, 0:NT - 1, :], x[0:(NT - 1) * P, :].rearrange("(t p) d -> p t d", p=P)
                                 ).then_inc(s_xin, 16)
                    sp.dma_start(x_sb[0:N - (NT - 1) * P, NT - 1, :], x[(NT - 1) * P:N, :]).then_inc(s_xin, 16)
                    sp.wait_ge(s_win, 1)
                    with nc.allow_non_contiguous_dma(reason="small table"):
                        sp.dma_start(win_d.rearrange("(t p) -> p t", p=P), win_i[:]).then_inc(s_wind, 16)
                    sp.wait_ge(s_wind, 16)
                    sp.dma_start(windows[:], win_d.rearrange("(a b) -> a b", a=1)).then_inc(s_winl, 16)
                    sp.wait_ge(s_rs, 1)
                    with nc.allow_non_contiguous_dma(reason="small table"):
                        sp.dma_start(row_d.rearrange("(t p) -> p t", p=P), start_f[:]).then_inc(s_rsd, 16)
                        sp.wait_ge(s_rsd, 16)
                        sp.dma_start(end_f[:], row_d[1:NP + 1].rearrange("(t p) -> p t", p=P)).then_inc(s_rb, 16)
                        sp.wait_ge(s_root, 1)
                        sp.dma_start(norm_d.rearrange("(t p) -> p t", p=P), norm_p[:]).then_inc(s_nd, 16)
                    sp.wait_ge(s_nd, 16)
                    sp.dma_start(norm_dst[:, :], norm_d.rearrange("(a b) -> a b", a=1).to_broadcast([P, NP])
                                 ).then_inc(s_rb, 16)
                    sp.wait_ge(s_winl, 16)
                    sp.wait_ge(s_rb, 32)
                    sp.wait_ge(s_xin, 32)

                @block.gpsimd
                def _(pool):
                    nc.gpsimd.iota(chunk_no[:], [[1, CR]], base=0, channel_multiplier=0)
                    nc.gpsimd.iota(number_i[:], [[P, RT]], base=0, channel_multiplier=1).then_inc(s_num, 1)
                    pool.wait_ge(s_start, 1)
                    nc.gpsimd.partition_broadcast(start_b[:], start_r[:])
                    nc.gpsimd.partition_broadcast(first_b[:], first_r[:]).then_inc(s_bc, 1)
                    pool.wait_ge(s_chunk, 1)
                    for t in range(ST):
                        for rows, table in ((srows, src_rows), (drows, dst_rows)):
                            pool.indirect_dma_start(out=rows[:, t, :], out_offset=None, in_=table,
                                                    in_offset=bass.IndirectOffsetOnAxis(ap=chunk_i[:, t:t + 1], axis=0)
                                                    ).then_inc(s_srows, 16)
                    pool.wait_ge(s_rowc, 1)
                    for t in range(RT):
                        pool.indirect_dma_start(out=nrows[:, t, :], out_offset=None, in_=dst_rows,
                                                in_offset=bass.IndirectOffsetOnAxis(ap=rowc_i[:, t:t + 1], axis=0)
                                                ).then_inc(s_nrows, 16)

                @block.vector
                def _(dve):
                    links = [0]

                    def link(ins):
                        links[0] += 1
                        ins.then_inc(s_link, 1)
                        dve.wait_ge(s_link, links[0])

                    link(nc.vector.tensor_scalar(number_less[:, 0:1], pcol[:], float(LOW), None, ALU.add))
                    link(nc.vector.tensor_scalar(upper[:], iota_f[0:LOW, :], number_less[0:LOW, 0:1], None,
                                                 ALU.is_equal))
                    dve.wait_ge(s_num, 1)
                    dve.wait_ge(s_first, 16)
                    nc.vector.memset(x_sb[:, NT - 1, :], 0.0).then_inc(s_xpad, 1)
                    link(nc.vector.tensor_scalar(first_w[:], first_i[:], 7, None, ALU.arith_shift_right))
                    nc.vector.tensor_copy(first_r[:], first_i[:])
                    nc.vector.tensor_copy(number[:], number_i[:])
                    nc.vector.tensor_scalar(number_less[:], number_i[:], -0.5, None, ALU.add)
                    nc.vector.tensor_tensor(start_r[:], first_w[:], chunk_no[:], ALU.add).then_inc(s_start, 1)
                    link(nc.vector.tensor_scalar(part_i[:], srcs, LOW - 1, None, ALU.bitwise_and))
                    link(nc.vector.tensor_copy(low[:], part_i[:]))
                    link(nc.vector.tensor_scalar(part_i[:], srcs, LOW.bit_length() - 1, None, ALU.arith_shift_right))
                    nc.vector.tensor_copy(iota_b[:], iota_f[:])
                    nc.vector.memset(zero_b[:], 0.0)
                    link(nc.vector.tensor_copy(high[:], part_i[:]))
                    nc.vector.tensor_scalar(srcs, srcs, float(N - 1), None, ALU.min).then_inc(s_parts, 1)
                    dve.wait_ge(s_bc, 1)
                    dve.wait_ge(s_start, 1)
                    for t in range(ST):
                        link(nc.vector.tensor_scalar(junk[:, 0:CH - 1], start_b[:, 1:CH], number[:, t:t + 1], 0.0,
                                                     ALU.is_le, ALU.add, accum_out=chunk_f[:, t:t + 1]))
                    nc.vector.tensor_copy(chunk_i[:], chunk_f[:]).then_inc(s_chunk, 1)
                    link(nc.vector.tensor_tensor(win_f[:], number[:, 0:ST], chunk_f[:], ALU.subtract))
                    link(nc.vector.tensor_scalar(win_f[:], win_f[:], float(NW - 1), None, ALU.min))
                    nc.vector.tensor_copy(win_i[:], win_f[:]).then_inc(s_win, 1)
                    link(nc.vector.tensor_scalar(base_f[:], win_f[:], float(-P), None, ALU.mult))
                    def bin_hots(i, j):
                        dve.wait_ge(s_hist, i * 2 + (j + 1))
                        for hot_, part, n in ((hot_low, low, LOW), (hot_high, high, HIGH)):
                            last = nc.vector.tensor_tensor(
                                hot_[:, j], part[:, bass.ds((i * 2 + j) * HG, HG)].unsqueeze(2).to_broadcast([P, HG, n]),
                                iota_b[:, 0:n].unsqueeze(1).to_broadcast([P, HG, n]), ALU.is_equal)
                        last.then_inc(s_bins, 1)

                    with dve.Fori(0, HB // 4) as i:
                        for j in range(2):
                            bin_hots(i, j)
                    dve.wait_ge(s_srows, 2 * ST * 16)
                    sf, df = srows[:].bitcast(F32), drows[:].bitcast(F32)
                    link(nc.vector.tensor_scalar(sf, srows[:], float(N - 1), None, ALU.min))
                    for t in range(ST):
                        last = nc.vector.tensor_scalar(df[:, t, :], drows[:, t, :], base_f[:, t:t + 1], None, ALU.add)
                    last.then_inc(s_rel, 1)
                    dve.wait_ge(s_rowsum, RT)
                    link(nc.vector.tensor_scalar(rowc_f[:], rowsum[:], 0.5, CH / 2 - 1.0, ALU.mult, ALU.add))
                    link(nc.vector.tensor_scalar(rowc_f[:], rowc_f[:], 0.0, None, ALU.max))
                    nc.vector.tensor_copy(rowc_i[:], rowc_f[:]).then_inc(s_rowc, 1)
                    for g in range(2 * ST * J):
                        t, j, table = g // (2 * J), g // 2 % J, (steps_src, steps_dst)[g % 2]
                        dve.wait_ge(s_tp, g + 1)
                        nc.vector.tensor_copy(
                            table[:, t * P * J:(t + 1) * P * J].rearrange("p (s j) -> p j s", j=J)[:, j, :],
                            banks[g % TPB][:, 0:P]).then_inc(s_tpc, 1)
                    dve.wait_ge(s_tpc, 2 * ST * J)
                    nc.vector.tensor_copy(steps_src[:, GATHERS:GATHERS + H], steps_src[:, 0:H])
                    with dve.Fori(HB // 4, 3 * HB // 8) as i:
                        for j in range(2):
                            bin_hots(i, j)
                    dve.wait_ge(s_insum, RT)
                    link(nc.vector.tensor_scalar(inrow[:], insum[:], 0.5, CE / 2, ALU.mult, ALU.add))
                    nc.vector.scalar_tensor_tensor(start_f[:], rowc_f[:], float(CE), inrow[:], ALU.mult,
                                                   ALU.add).then_inc(s_rs, 1)
                    with dve.Fori(3 * HB // 8, 7 * HB // 16) as i:
                        for j in range(2):
                            bin_hots(i, j)
                    dve.wait_ge(s_rs, 1)
                    dve.wait_ge(s_rb, 16)
                    link(nc.vector.tensor_tensor(norm_p[:], end_f[:], start_f[:, 0:NT], ALU.subtract))
                    link(nc.vector.tensor_scalar(norm_p[:], norm_p[:], 1.0, None, ALU.max))
                    nc.vector.reciprocal(norm_p[:], norm_p[:]).then_inc(s_recip_in, 1)
                    link(nc.vector.tensor_tensor(has_f[:], end_f[:], start_f[:, 0:NT], ALU.is_gt))
                    link(nc.vector.tensor_scalar(alt_f[:], has_f[:], float(-ONES_ROW), float(ONES_ROW),
                                                 ALU.mult, ALU.add))
                    link(nc.vector.scalar_tensor_tensor(end_f[:], end_f[:], -1.0, has_f[:], ALU.add, ALU.mult))
                    nc.vector.tensor_tensor(last_row[:], end_f[:], alt_f[:], ALU.add)
                    with dve.Fori(7 * HB // 16, HB // 2) as i:
                        for j in range(2):
                            bin_hots(i, j)
                    dve.wait_ge(s_hist, 2 + HB + 1)
                    nc.vector.tensor_copy(counts_sb[:], counts).then_inc(s_cnt, 1)
                    dve.wait_ge(s_nsrc, 1)
                    link(nc.vector.tensor_scalar(norm_src[:], by_node, 1.0, None, ALU.max))
                    nc.vector.reciprocal(norm_src[:], norm_src[:]).then_inc(s_recip, 1)

                @block.scalar
                def _(act):
                    def counted(t, values, sums, signal):
                        nc.scalar.activation(signs[:, 0:values.shape[1]], values, ACT.Sign,
                                             bias=number_less[:, t:t + 1], scale=-1.0,
                                             accum_out=sums[:, t:t + 1]).then_inc(signal, 1)
                        act.wait_ge(signal, t + 1)

                    act.wait_ge(s_bc, 1)
                    for t in range(RT):
                        counted(t, first_b[:, 0:CH], rowsum, s_rowsum)
                    act.wait_ge(s_nrows, 16 * RT)
                    for t in range(RT):
                        counted(t, nrows[:, t, :], insum, s_insum)
                    act.wait_ge(s_recip_in, 1)
                    nc.scalar.activation(norm_p[:], norm_p[:], ACT.Sqrt).then_inc(s_root, 1)
                    act.wait_ge(s_recip, 1)
                    nc.scalar.activation(norm_src[:], norm_src[:], ACT.Sqrt)

                @block.tensor
                def _(pe):
                    def bin_sums(i, j):
                        pe.wait_ge(s_bins, i * 2 + (j + 1))
                        for g in range(HG):
                            last = nc.tensor.matmul(counts, hot_low[:, j, g, :], hot_high[:, j, g, :],
                                                    start=False, stop=False)
                        last.then_inc(s_hist, 1)

                    pe.wait_ge(s_parts, 1)
                    nc.tensor.matmul(counts, zero_b[:, 0:LOW], zero_b[:, 0:HIGH], start=True, stop=False).then_inc(s_hist, 2)
                    with pe.Fori(0, HB // 4) as i:
                        for j in range(2):
                            bin_sums(i, j)
                    pe.wait_ge(s_rel, 1)
                    for g in range(2 * ST * J):
                        t, j, rows = g // (2 * J), g // 2 % J, (srows, drows)[g % 2]
                        if g >= TPB:
                            pe.wait_ge(s_tpc, g - TPB + 1)
                        nc.tensor.transpose(banks[g % TPB][:, 0:P], rows[:, t, j * P:(j + 1) * P].bitcast(F32),
                                            ident[:]).then_inc(s_tp, 1)
                    with pe.Fori(HB // 4, HB // 2) as i:
                        for j in range(2):
                            bin_sums(i, j)
                    nc.tensor.matmul(counts, zero_b[:, 0:LOW], zero_b[:, 0:HIGH], start=False, stop=True
                                     ).then_inc(s_hist, 1)
                    pe.wait_ge(s_cnt, 1)
                    by_half = counts_sb[:].rearrange("l (t h) -> l h t", h=2)
                    nc.tensor.matmul(by_node, ident[0:LOW, :], by_half[:, 0, :], start=True, stop=False)
                    nc.tensor.matmul(by_node, upper[:], by_half[:, 1, :], start=False, stop=True).then_inc(s_nsrc, 1)

        with ExitStack() as ph:
            sbt = sb_in(ph)
            agg = sbt("agg", [P, NW * P])
            xT = sbt("xT", [P, NP])
            ws = [sbt(f"w{k}", [D, D]) for k in range(3)]
            bs = [sbt(f"b{k}", [D, 1]) for k in range(3)]
            hs = x_sb
            idx = sbt("idx", [P, U], I32)
            msg = sbt("msg", [P, U, D])
            hot = sbt("hot", [P, U, P])
            v1_sb, v2_sb = sbt("v1_sb", [D, D]), sbt("v2_sb", [D, D])
            c1_sb = sbt("c1_sb", [D, 1])
            c1_less = sbt("c1_less", [D, 1])
            c2_row = sbt("c2_row", [3, C4, D])
            c2_parts = sbt("c2_parts", [3, C4, D], BF16)
            c2_rest = sbt("c2_rest", [3, C4, D])
            mask3 = sbt("mask3", [3, 3])
            c2_part = sbt("c2_part", [3, C4, D], BF16)
            s_parts3 = sem("s_c2_parts")
            ones_r = sbt("ones_r", [3, P], BF16)
            center = sbt("center", [P, 1])
            halves = sbt("halves", [P, 1])
            dist = sbt("dist", [P, BLK])
            sq = sbt("sq", [P, BLK])
            basis = sbt("basis", [P, BLK])
            t1, e1, s1 = sbt("t1", [P, BLK]), sbt("e1", [P, BLK]), sbt("s1", [P, BLK])
            t2, e2 = sbt("t2", [P, BLK]), sbt("e2", [P, BLK])
            y2 = sbt("y2", [P, C4, D])
            ef = sbt("ef", [P, C4, D])
            g_out = sbt("g_out", [P, C4, D])
            ps1, ps2 = banks[2], banks[3]
            slots = banks[0:2] + banks[4:8]

            s_x, s_w, s_cst, s_xt, s_xtc = (sem(n) for n in ("s_x", "s_w", "s_cst", "s_xt", "s_xtc"))
            s_hp, s_hc, s_hst = sem("s_h_in_psum"), sem("s_h_copied"), sem("s_h_stored")
            s_zero, s_scaled, s_relu = sem("s_agg_zeroed"), sem("s_agg_scaled"), sem("s_x_ready")
            s_idx, s_group = sem("s_idx_ready"), sem("s_group_begun")
            s_gat = [sem(f"s_gathered{u}") for u in range(U)]
            s_hot, s_mm, s_acc = sem("s_hot_ready"), sem("s_summed"), sem("s_accumulated")
            s_dist, s_sqr, s_bas, s_z1, s_t1, s_e1, s_l1, s_s1 = (sem(n) for n in (
                "s_dist_in", "s_squared", "s_basis", "s_z1", "s_t1", "s_e1", "s_l1", "s_s1"))
            s_z2, s_t2_, s_e2, s_l2_, s_y2, s_ef, s_g, s_gst = (sem(n) for n in (
                "s_z2", "s_t2_", "s_e2", "s_l2_", "s_y2", "s_ef_in", "s_g_ready", "s_g_stored"))
            s_ft, s_ln, s_bn, s_rv, s_sd, s_x1, s_x1d = (sem(n) for n in (
                "s_back", "s_resid", "s_moments", "s_recip", "s_rstd", "s_x1", "s_x1d"))
            mom = sbt("mom", [P, NT, 2])
            stat = sbt("stat", [P, NT, 6])
            rstd = sbt("rstd", [P, NT])

            HGRP = 4
            groups = [(a, min(a + HGRP, NT)) for a in range(0, NT, HGRP)]
            NG = len(groups)
            filters = [ITS, ITS, FULL // FB - 2 * ITS]
            assert FULL % FB == 0 and 0 < filters[2] < ITS
            XCH = 7
            XW = NP // XCH

            wt_row = wt_d.rearrange("(a b) -> a b", a=1)
            g_rows = g_d.rearrange("(b p c) d -> p b c d", c=C4, p=P)
            ef_rows = edge_attr[0:FULL * BLK, :].rearrange("(b p c) d -> p b c d", c=C4, p=P)
            h_rows = h_d.rearrange("(t p) d -> p t d", p=P)
            x1_rows = x1_d.rearrange("(t p) d -> p t d", p=P)

            with nc.Block() as block:
                @block.sync
                def _(sp):
                    col = lambda b: b.rearrange("(a b) -> a b", b=1)
                    row = lambda b: b.rearrange("(a b) -> a b", a=1)
                    for tile, ap in zip(ws + [v1_sb, v2_sb], (w1, w2, w3, v1, v2)):
                        sp.dma_start(tile[:], ap).then_inc(s_w, 16)
                    for tile, ap in zip(bs + [c1_sb], (b1, b2, b3, c1)):
                        sp.dma_start(tile[:], col(ap)).then_inc(s_w, 16)
                    for c in range(C4):
                        sp.dma_start(c2_row[:, c, :], row(c2).to_broadcast([3, D])).then_inc(s_w, 16)
                    sp.dma_start(dist[:], wt_row[:, 0:BLK].to_broadcast([P, BLK])).then_inc(s_dist, 16)
                    sp.dma_start(ef[:], ef_rows[:, 0]).then_inc(s_ef, 16)

                    with sp.Fori(0, FULL - 1) as b:
                        sp.wait_ge(s_sqr, b + 1)
                        sp.dma_start(dist[:], wt_row[:, bass.ds((b + 1) * BLK, BLK)].to_broadcast([P, BLK])
                                     ).then_inc(s_dist, 16)
                        sp.wait_ge(s_g, b + 1)
                        sp.dma_start(g_rows[:, bass.ds(b, 1)], g_out[:].unsqueeze(1)).then_inc(s_gst, 16)
                        sp.dma_start(ef[:].unsqueeze(1), ef_rows[:, bass.ds(b + 1, 1)]).then_inc(s_ef, 16)
                    sp.wait_ge(s_sqr, FULL)
                    sp.dma_start(dist[:], wt_row[:, FULL * BLK:EP].to_broadcast([P, BLK])).then_inc(s_dist, 16)
                    sp.wait_ge(s_g, FULL)
                    sp.dma_start(g_rows[:, FULL - 1], g_out[:]).then_inc(s_gst, 16)
                    sp.wait_ge(s_g, FULL + 1)
                    sp.dma_start(ef[0:TAIL // C4], edge_attr[FULL * BLK:E, :].rearrange("(p c) d -> p c d", c=C4)
                                 ).then_inc(s_ef, 16)
                    sp.wait_ge(s_g, FULL + 2)
                    sp.dma_start(g_rows[:, FULL], g_out[:]).then_inc(s_gst, 16)
                    sp.wait_ge(s_gst, 16 * (FULL + 2))

                @block.gpsimd
                def _(pool):
                    for k in range(3):
                        if k:
                            pool.wait_ge(s_relu, XCH * k)
                        nc.gpsimd.memset(agg[:], 0.0).then_inc(s_zero, 1)
                        pool.wait_ge(s_hst, 16 * XCH * (k + 1))
                        with pool.Fori(0, ITS) as it:
                            for g in range(G):
                                pool.wait_ge(s_idx, it * G + (G * ITS * k + g + 1))
                                pool.sem_inc(s_group, 1)
                                for u in range(g * H, (g + 1) * H):
                                    pool.indirect_dma_start(
                                        out=msg[:, u, :], out_offset=None, in_=h_d,
                                        in_offset=bass.IndirectOffsetOnAxis(ap=idx[:, u:u + 1], axis=0)
                                    ).then_inc(s_gat[u], 16)

                @block.scalar
                def _(act):
                    def basis_of(b):
                        act.wait_ge(s_dist, b * 16 + 16)
                        nc.scalar.activation(sq[:], dist[:], ACT.Square, bias=center[:]).then_inc(s_sqr, 1)
                        act.wait_ge(s_sqr, b + 1)
                        nc.scalar.activation(basis[:], sq[:], ACT.Exp, scale=COEFF).then_inc(s_bas, 1)

                    def soft(b, t, e, s_in, s_exp, s_out):
                        act.wait_ge(s_in, b + 1)
                        nc.scalar.activation(e[:], t[:], ACT.Exp).then_inc(s_exp, 1)
                        act.wait_ge(s_exp, b + 1)
                        nc.scalar.activation(t[:], e[:], ACT.Ln, bias=halves[:], scale=0.5).then_inc(s_out, 1)

                    nc.scalar.copy(idx[:, 0:H], steps_src[:, 0:H]).then_inc(s_idx, 1)
                    act.wait_ge(s_cst, 1)
                    for k in range(3):
                        for j in range(XCH):
                            a, b = j * NT // XCH, (j + 1) * NT // XCH
                            act.wait_ge(s_hc, NG * k + -(-b // HGRP))
                            act.dma_start(h_rows[:, a:b, :], hs[:, a:b, :]).then_inc(s_hst, 16)

                        if k == 2:
                            act.wait_ge(s_hst, 16 * XCH * 3)
                            act.dma_start(x_sb[:, 0:NT - 1, :], x[0:(NT - 1) * P, :].rearrange(
                                "(t p) d -> p t d", p=P)).then_inc(s_x, 16)
                            act.dma_start(x_sb[0:N - (NT - 1) * P, NT - 1, :], x[(NT - 1) * P:N, :]).then_inc(s_x, 16)

                        def copy_idx(it, g):
                            act.wait_ge(s_mm, it * U + (GATHERS * k + (g + 1) * H))
                            nc.scalar.copy(idx[:, g % G * H:(g % G + 1) * H],
                                           steps_src[:, bass.ds(it * U + g * H, H)]).then_inc(s_idx, 1)

                        nc.scalar.preload_act_table_set("natural_log_exp_and_others")
                        with act.Fori(0, filters[k]) as it:
                            b = [it * FB + (ITS * FB * k + f) for f in range(FB)]
                            copy_idx(it, 1)
                            basis_of(b[0])
                            soft(b[0], t1, e1, s_t1, s_e1, s_l1)
                            copy_idx(it, 2)
                            basis_of(b[1])
                            soft(b[0], t2, e2, s_t2_, s_e2, s_l2_)
                            soft(b[1], t1, e1, s_t1, s_e1, s_l1)
                            copy_idx(it, 3)
                            soft(b[1], t2, e2, s_t2_, s_e2, s_l2_)
                        if filters[k] < ITS:
                            basis_of(FULL)
                            soft(FULL, t1, e1, s_t1, s_e1, s_l1)
                            soft(FULL, t2, e2, s_t2_, s_e2, s_l2_)
                            with act.Fori(filters[k], ITS) as it:
                                for g in range(1, G + 1):
                                    copy_idx(it, g)
                        for j in range(XCH):
                            act.wait_ge(s_scaled, XCH * k + j + 1)
                            nc.scalar.activation(xT[:, j * XW:(j + 1) * XW], agg[:, j * XW:(j + 1) * XW],
                                                 ACT.Relu if k < 2 else ACT.Identity, bias=bs[k][:]
                                                 ).then_inc(s_relu, 1)
                    act.wait_ge(s_rv, 1)
                    nc.scalar.activation(rstd[:], rstd[:], ACT.Sqrt).then_inc(s_sd, 1)
                    for j in range(XCH):
                        act.wait_ge(s_x1, j + 1)
                        act.dma_start(x1_rows[:, 7 * j:7 * j + 7, :], x_sb[:, 7 * j:7 * j + 7, :]).then_inc(s_x1d, 16)
                    act.wait_ge(s_x1d, 16 * XCH)

                @block.tensor
                def _(pe):
                    def z1(b):
                        pe.wait_ge(s_bas, b + 1)
                        nc.tensor.matmul(ps1[:], v1_sb[:], basis[:], start=True, stop=True).then_inc(s_z1, 1)

                    def z2(b):
                        pe.wait_ge(s_s1, b + 1)
                        nc.tensor.matmul(ps2[:], ones_r[:], c2_parts[:].rearrange("p c d -> p (c d)"),
                                         start=True, stop=False)
                        s1_c = s1[:].rearrange("f (e c) -> f c e", c=C4)
                        for c in range(C4):
                            last = nc.tensor.matmul(ps2[:, c * D:(c + 1) * D], s1_c[:, c, :], v2_sb[:],
                                                    start=False, stop=(c == C4 - 1))
                        last.then_inc(s_z2, 1)

                    pe.wait_ge(s_cst, 1)
                    pe.sem_inc(s_mm, U)
                    for g, (a, b) in enumerate(groups):
                        if g >= 2:
                            pe.wait_ge(s_xtc, g - 1)
                        for t in range(a, b):
                            last = nc.tensor.transpose(banks[4 + g % 2][:, (t - a) * P:(t - a + 1) * P], x_sb[:, t, :],
                                                       ident[:])
                        last.then_inc(s_xt, 1)
                    pe.wait_ge(s_w, 16 * 13)
                    pe.wait_ge(s_xtc, NG)
                    for k in range(3):
                        for g, (a, b) in enumerate(groups):
                            if k:
                                pe.wait_ge(s_relu, XCH * (k - 1) + -(-b * P // XW))
                            if g >= 2:
                                pe.wait_ge(s_hc, NG * k + g - 1)
                            for t in range(a, b):
                                last = nc.tensor.matmul(banks[4 + g % 2][:, (t - a) * D:(t - a + 1) * D],
                                                        xT[:, t * P:(t + 1) * P], ws[k][:], start=True, stop=True)
                            last.then_inc(s_hp, 1)

                        beside = {step * J + J - 1: work for step, work in
                                  {0: (z1, 0), 2: (z2, 0), 4: (z1, 1), 8: (z2, 1)}.items()}

                        def iteration(it, filtered):
                            for u in range(U):
                                pe.wait_ge(s_gat[u], it * 16 + 16 * (ITS * k + 1))
                                if u % H == 0:
                                    pe.wait_ge(s_hot, it * G + (G * ITS * k + u // H + 1))
                                if u % J == 0:
                                    pe.wait_ge(s_acc, it * SU + (STEPS * k + u // J + 1))
                                nc.tensor.matmul(slots[u // J % SLOTS][:, 0:P], msg[:, u, :], hot[:, u, :],
                                                 start=(u % J == 0), stop=(u % J == J - 1)).then_inc(s_mm, 1)
                                if filtered and u in beside:
                                    work, f = beside[u]
                                    work(it * FB + (ITS * FB * k + f))

                        with pe.Fori(0, filters[k]) as it:
                            iteration(it, True)
                        if filters[k] < ITS:
                            z1(FULL)
                            z2(FULL)
                            with pe.Fori(filters[k], ITS) as it:
                                iteration(it, False)
                    for g, (a, b) in enumerate(groups):
                        pe.wait_ge(s_relu, XCH * 2 + -(-b * P // XW))
                        if g >= 2:
                            pe.wait_ge(s_ln, g - 1)
                        for t in range(a, b):
                            last = nc.tensor.transpose(banks[4 + g % 2][:, (t - a) * P:(t - a + 1) * P],
                                                       xT[:, t * P:(t + 1) * P], ident[:])
                        last.then_inc(s_ft, 1)

                @block.vector
                def _(dve):
                    nc.vector.memset(halves[:], 0.5)
                    nc.vector.memset(ones_r[:], 1.0)
                    nc.vector.tensor_scalar(center[:], pcol[:], -DELTA, None, ALU.mult).then_inc(s_cst, 1)
                    dve.sem_inc(s_acc, SLOTS)
                    dve.sem_inc(s_gst, 16)
                    for g, (a, b) in enumerate(groups):
                        dve.wait_ge(s_xt, g + 1)
                        nc.vector.tensor_copy(xT[:, a * P:b * P], banks[4 + g % 2][:, 0:(b - a) * P]).then_inc(s_xtc, 1)

                    def split_c2():
                        dve.wait_ge(s_w, 16 * 13)
                        parts = [0]

                        def then(ins):
                            parts[0] += 1
                            ins.then_inc(s_parts3, 1)
                            dve.wait_ge(s_parts3, parts[0])

                        for i in range(3):
                            nc.vector.tensor_scalar(mask3[:, i:i + 1], pcol[0:3, 0:1], float(i), None, ALU.is_equal)
                            then(nc.vector.tensor_copy(c2_part[:], c2_row[:]))
                            then(nc.vector.tensor_tensor(c2_row[:], c2_row[:], c2_part[:], ALU.subtract))
                            if i == 0:
                                then(nc.vector.tensor_scalar(c2_rest[:], c2_part[:], mask3[:, 0:1], None, ALU.mult))
                            else:
                                then(nc.vector.scalar_tensor_tensor(c2_rest[:], c2_part[:], mask3[:, i:i + 1], c2_rest[:],
                                                                    ALU.mult, ALU.add))
                        nc.vector.tensor_copy(c2_parts[:], c2_rest[:]).then_inc(s_parts3, 1)
                        nc.vector.tensor_scalar(c1_less[:], c1_sb[:], -LN2, None, ALU.add)

                    def min1(b):
                        dve.wait_ge(s_z1, b + 1)
                        nc.vector.tensor_scalar(t1[:], ps1[:], c1_sb[:], SOFT_MAX, ALU.add, ALU.min).then_inc(s_t1, 1)

                    def max1(b):
                        dve.wait_ge(s_l1, b + 1)
                        nc.vector.scalar_tensor_tensor(s1[:], ps1[:], c1_less[:], t1[:], ALU.add,
                                                       ALU.max).then_inc(s_s1, 1)

                    def min2(b):
                        dve.wait_ge(s_z2, b + 1)
                        nc.vector.tensor_scalar(t2[:], ps2[:], SOFT_MAX, None, ALU.min).then_inc(s_t2_, 1)

                    def max2(b):
                        dve.wait_ge(s_l2_, b + 1)
                        nc.vector.scalar_tensor_tensor(y2[:].rearrange("p c d -> p (c d)"), ps2[:], -LN2, t2[:],
                                                       ALU.add, ALU.max).then_inc(s_y2, 1)

                    def weigh(b):
                        dve.wait_ge(s_y2, b + 1)
                        dve.wait_ge(s_ef, b * 16 + 16)
                        dve.wait_ge(s_gst, b * 16 + 16)
                        nc.vector.tensor_tensor(g_out[:], y2[:], ef[:], ALU.mult).then_inc(s_g, 1)

                    def last_filter():
                        dve.wait_ge(s_gst, 16 * (FULL + 1))
                        nc.vector.memset(ef[:], 0.0).then_inc(s_g, 1)
                        min1(FULL)
                        max1(FULL)
                        min2(FULL)
                        max2(FULL)
                        dve.wait_ge(s_y2, FULL + 1)
                        dve.wait_ge(s_ef, 16 * (FULL + 1))
                        nc.vector.tensor_tensor(g_out[:], y2[:], ef[:], ALU.mult).then_inc(s_g, 1)

                    for k in range(3):
                        if k:
                            dve.wait_ge(s_hst, 16 * XCH * k)
                        for g, (a, b) in enumerate(groups):
                            dve.wait_ge(s_hp, NG * k + g + 1)
                            nc.vector.tensor_tensor(
                                hs[:, a:b, :], banks[4 + g % 2][:, 0:(b - a) * D].rearrange("p (t d) -> p t d", d=D),
                                norm_src[:, a:b].unsqueeze(2).to_broadcast([P, b - a, D]), ALU.mult).then_inc(s_hc, 1)

                        def one_hots(it, g):
                            dve.wait_ge(s_mm, it * U + (GATHERS * k + (g + 1) * H))
                            nc.vector.tensor_tensor(
                                hot[:, g * H:(g + 1) * H, :],
                                steps_dst[:, bass.ds(it * U + g * H, H)].unsqueeze(2).to_broadcast([P, H, P]),
                                iota_f[:].unsqueeze(1).to_broadcast([P, H, P]), ALU.is_equal).then_inc(s_hot, 1)

                        def iteration(it, filtered):
                            beside = {1: ((min1, 0),), 2: ((max1, 0),), 4: ((min2, 0),), 5: ((min1, 1),),
                                      6: ((max2, 0),), 7: ((weigh, 0), (max1, 1)), 9: ((min2, 1),),
                                      11: ((max2, 1), (weigh, 1))}
                            one_hots(it, 0)
                            wins = nc.values_load_multi_w_load_instructions(
                                windows[0:1, bass.ds(it * SU, SU)], engines=[mybir.EngineType.DVE],
                                min_val=0, max_val=NW - 1)[1]
                            for u in range(SU):
                                dve.wait_ge(s_mm, it * U + (GATHERS * k + U + (u + 1) * J))
                                dve.wait_ge(s_acc, it * SU + (STEPS * k + SLOTS + u))
                                into = agg[:, bass.ds(wins[u] * P, P)]
                                nc.vector.tensor_tensor(into, into, slots[u % SLOTS][:, 0:P], ALU.add
                                                        ).then_inc(s_acc, 1)
                                if u % (H // J) == 0 and u // (H // J) < G - 1:
                                    one_hots(it, u // (H // J) + 1)
                                if filtered:
                                    for work, f in beside.get(u, ()):
                                        work(it * FB + (ITS * FB * k + f))

                        if k == 0:
                            split_c2()
                        dve.wait_ge(s_zero, k + 1)
                        with dve.Fori(0, filters[k]) as it:
                            iteration(it, True)
                        if filters[k] < ITS:
                            last_filter()
                            with dve.Fori(filters[k], ITS) as it:
                                iteration(it, False)
                        dve.wait_ge(s_acc, STEPS * (k + 1) + SLOTS)
                        for j in range(XCH):
                            part = agg[:, j * XW:(j + 1) * XW]
                            nc.vector.tensor_tensor(part, part, norm_dst[:, j * XW:(j + 1) * XW],
                                                    ALU.mult).then_inc(s_scaled, 1)
                    dve.wait_ge(s_x, 32)
                    for g, (a, b) in enumerate(groups):
                        dve.wait_ge(s_ft, g + 1)
                        nc.vector.tensor_tensor(x_sb[:, a:b, :], x_sb[:, a:b, :],
                                                banks[4 + g % 2][:, 0:(b - a) * D].rearrange("p (t d) -> p t d", d=D),
                                                ALU.add).then_inc(s_ln, 1)
                        dve.wait_ge(s_ln, g + 1)
                        for t in range(a, b):
                            last = nc.vector.bn_stats(stat[:, t, :], x_sb[:, t, :])
                        last.then_inc(s_bn, 1)
                        dve.wait_ge(s_bn, 2 * g + 1)
                        for t in range(a, b):
                            last = nc.vector.bn_aggr(mom[:, t, :], stat[:, t, :])
                        last.then_inc(s_bn, 1)
                    dve.wait_ge(s_bn, 2 * NG)
                    nc.vector.tensor_scalar(rstd[:], mom[:, :, 1], EPS, None, ALU.add).then_inc(s_bn, 1)
                    dve.wait_ge(s_bn, 2 * NG + 1)
                    nc.vector.reciprocal(rstd[:], rstd[:]).then_inc(s_rv, 1)
                    dve.wait_ge(s_sd, 1)
                    for t in range(NT):
                        last = nc.vector.tensor_scalar(x_sb[:, t, :], x_sb[:, t, :], mom[:, t, 0:1], rstd[:, t:t + 1],
                                                       ALU.subtract, ALU.mult)
                        if t % 7 == 6:
                            last.then_inc(s_x1, 1)

        with ExitStack() as ph:
            sbt = sb_in(ph)
            R = AHEAD
            idx = sbt("idx4", [P, R, C4], I32)
            hgat = sbt("hgat", [P, R, C4, D])
            filt = sbt("filt", [P, R, C4, D])
            u_same = sbt("u_same", [P, R, C4, D])
            u_first = sbt("u_first", [P, R, C4, D])
            first_sb = sbt("first_sb", [P, R, BLK])
            run = sbt("run", [P, R, BLK])
            run_out = sbt("run_out", [P, R, C4, D])
            psame, pfirst = banks[0:R], banks[R:2 * R]
            prun = pfirst
            s_i, s_u, s_ts, s_fc, s_sc, s_tr, s_ro = (sem(n) for n in (
                "s_index4", "s_factors", "s_factors_T", "s_first_copied", "s_scanned", "s_run_T", "s_run_out"))
            s_turn = sem("s_gathers_begun")
            s_fi = [sem(f"s_filt_in{r}") for r in range(R)]
            s_gt = [[sem(f"s_hgat{r}_{c}") for c in range(C4)] for r in range(R)]
            s_rst = [sem(f"s_run_stored{r}") for r in range(R)]
            g_rows = g_d.rearrange("(b p c) d -> p b c d", c=C4, p=P)
            run_rows = run_d[0:EP, :].rearrange("(b p c) d -> p b c d", c=C4, p=P)
            LOOPS = (NB - 1) // R
            assert LOOPS * R == NB - 1 and R % 2
            with nc.Block() as block:
                @block.sync
                def _(sp):
                    def load(b, r):
                        sp.wait_ge(s_u, b + 1)
                        sp.dma_start(filt[:, r].unsqueeze(1), g_rows[:, bass.ds(b, 1)]).then_inc(s_fi[r], 16)

                    with sp.Fori(0, LOOPS) as i:
                        for r in range(R):
                            load(i * R + r, r)
                    load(NB - 1, 0)

                @block.gpsimd
                def _(pool):
                    def gather(b, r):
                        pool.wait_ge(s_i, b + 1)
                        pool.sem_inc(s_turn, 1)
                        for c in range(C4):
                            pool.indirect_dma_start(out=hgat[:, r, c, :], out_offset=None, in_=x1_d,
                                                    in_offset=bass.IndirectOffsetOnAxis(ap=idx[:, r, c:c + 1], axis=0)
                                                    ).then_inc(s_gt[r][c], 16)

                    with pool.Fori(0, LOOPS) as i:
                        for r in range(R):
                            gather(i * R + r, r)
                    gather(NB - 1, 0)

                @block.scalar
                def _(act):
                    def copy_idx(b, r):
                        act.wait_ge(s_u, b + 1)
                        nc.scalar.copy(idx[:, r:r + 1, :], edge_src[:, bass.ds(b, 1), :]).then_inc(s_i, 1)

                    def copy_first(b, r):
                        act.wait_ge(s_ts, b + (R + 1))
                        act.wait_ge(s_sc, b + 1)
                        nc.scalar.copy(first_sb[:, r, :], pfirst[r][:]).then_inc(s_fc, 1)

                    def store_run(b, r, stored):
                        act.wait_ge(s_tr, b + (R + 1))
                        act.wait_ge(s_rst[r], stored)
                        nc.scalar.copy(run_out[:, r].rearrange("p c d -> p (c d)"), prun[r][:]).then_inc(s_ro, 1)
                        act.wait_ge(s_ro, b + (R + 1))
                        act.dma_start(run_rows[:, bass.ds(b, 1)], run_out[:, r].unsqueeze(1)).then_inc(s_rst[r], 16)

                    act.sem_inc(s_ro, R)
                    for r in range(R):
                        act.sem_inc(s_rst[r], 16)
                        copy_idx(r, r)
                    copy_first(0, 0)
                    copy_idx(R, 0)
                    with act.Fori(0, LOOPS) as i:
                        for r in range(R):
                            b = i * R + r
                            copy_first(b + 1, (r + 1) % R)
                            copy_idx(b + 1 + R, (r + 1) % R)
                            store_run(b, r, i * 16 + 16)
                    store_run(NB - 1, 0, LOOPS * 16 + 16)
                    act.wait_ge(s_rst[0], LOOPS * 16 + 32)
                    for r in range(1, R):
                        act.wait_ge(s_rst[r], LOOPS * 16 + 16)

                @block.tensor
                def _(pe):
                    def turn(b, r):
                        pe.wait_ge(s_u, b + (R + 1))
                        pe.wait_ge(s_ro, b + 1)
                        for bank, fac in ((pfirst[r], u_first), (psame[r], u_same)):
                            view = bank[:].rearrange("p (e c) -> p c e", c=C4)
                            for c in range(C4):
                                last = nc.tensor.transpose(view[:, c, :], fac[:, r, c, :], ident[:])
                        last.then_inc(s_ts, 1)

                    def back(b, r):
                        pe.wait_ge(s_sc, b + (R + 1))
                        view = run[:, r, :].rearrange("p (e c) -> p c e", c=C4)
                        bank = prun[r]
                        for c in range(C4):
                            last = nc.tensor.transpose(bank[:, c * P:(c + 1) * P], view[:, c, :], ident[:])
                        last.then_inc(s_tr, 1)

                    pe.sem_inc(s_ts, R)
                    pe.sem_inc(s_tr, R)
                    turn(0, 0)
                    with pe.Fori(0, LOOPS) as i:
                        for r in range(R):
                            b = i * R + r
                            turn(b + 1, (r + 1) % R)
                            back(b, r)
                    back(NB - 1, 0)

                @block.vector
                def _(dve):
                    same = edge_same[:].rearrange("p b c -> p (b c)")
                    first = edge_first[:].rearrange("p b c -> p (b c)")

                    def factors(b, r, nth):
                        for c in range(C4):
                            dve.wait_ge(s_gt[r][c], nth)
                        dve.wait_ge(s_fi[r], nth)
                        dve.wait_ge(s_ts, b + 1)
                        for out_, mask in ((u_same, same), (u_first, first)):
                            for c in range(C4):
                                last = nc.vector.scalar_tensor_tensor(
                                    out_[:, r, c, :], hgat[:, r, c, :], mask[:, bass.ds(b * C4 + c, 1)],
                                    filt[:, r, c, :], ALU.mult, ALU.mult)
                        last.then_inc(s_u, 1)

                    def scan(b, r):
                        dve.wait_ge(s_fc, b + 1)
                        dve.wait_ge(s_tr, b + 1)
                        dve.wait_ge(s_sc, b + R)
                        nc.vector.tensor_tensor_scan(run[:, r, :], psame[r][:], first_sb[:, r, :],
                                                     run[:, (r - 1) % R, BLK - 1:BLK], ALU.mult, ALU.add
                                                     ).then_inc(s_sc, 1)

                    nc.vector.memset(run[:, R - 1, BLK - 1:BLK], 0.0).then_inc(s_sc, R)
                    dve.sem_inc(s_u, R)
                    factors(0, 0, 16)
                    with dve.Fori(0, LOOPS) as i:
                        for r in range(R):
                            b = i * R + r
                            factors(b + 1, (r + 1) % R, i * 16 + (32 if r == R - 1 else 16))
                            scan(b, r)
                    scan(NB - 1, 0)

        with ExitStack() as ph:
            sbt = sb_in(ph)
            prod = sbt("prod", [P, NT, D])
            prodT = sbt("prodT", [P, 2, HGRP * P])
            v3_sb = sbt("v3_sb", [D, D])
            c3_row = sbt("c3_row", [1, D])
            ones_r = sbt("ones_r5", [1, P])
            halves = sbt("halves5", [P, 1])
            zmin = sbt("zmin", [P, NT, D])
            ZB = 4
            zall = sbt("zall", [P, NT, D])
            mom = sbt("mom5", [P, NT, 2])
            stat = sbt("stat5", [P, NT, 6])
            rstd = sbt("rstd5", [P, NT])
            s_w5, s_pt, s_ptc, s_z, s_zc, s_ex, s_lg, s_l5, s_q5, s_r5, s_y, s_out = (sem(n) for n in (
                "s_w5", "s_prodT", "s_prodT_copied", "s_z3", "s_z3_copied", "s_exp3", "s_log3",
                "s_l5", "s_recip5", "s_rstd5", "s_out_ready", "s_out_stored"))
            PG = 2 * HGRP
            s_pg = [sem(f"s_prod_in{g}") for g in range(-(-NT // PG))]
            with nc.Block() as block:
                @block.sync
                def _(sp):
                    sp.dma_start(v3_sb[:], v3).then_inc(s_w5, 16)
                    sp.dma_start(c3_row[:], c3.rearrange("(a b) -> a b", a=1)).then_inc(s_w5, 16)
                    for j in range(7):
                        sp.wait_ge(s_y, j + 1)
                        a, b = 7 * j, 7 * j + 7
                        full = min(b, NT - 1)
                        sp.dma_start(out[a * P:full * P, :].rearrange("(t p) d -> p t d", p=P),
                                     x_sb[:, a:full, :]).then_inc(s_out, 16)
                    sp.dma_start(out[(NT - 1) * P:N, :], x_sb[0:N - (NT - 1) * P, NT - 1, :]).then_inc(s_out, 16)
                    sp.wait_ge(s_out, 16 * 8)

                @block.gpsimd
                def _(pool):
                    nc.gpsimd.memset(ones_r[:], 1.0)
                    nc.gpsimd.memset(halves[:], 0.5).then_inc(s_w5, 1)
                    for t in range(NT):
                        pool.indirect_dma_start(out=prod[:, t, :], out_offset=None, in_=run_d,
                                                in_offset=bass.IndirectOffsetOnAxis(ap=last_row[:, t:t + 1], axis=0)
                                                ).then_inc(s_pg[t // PG], 16)

                @block.tensor
                def _(pe):
                    def turn(g):
                        a, b = groups[g]
                        if g >= 2:
                            pe.wait_ge(s_ptc, g - 1)
                        pe.wait_ge(s_pg[a // PG], 16 * (min(NT, a // PG * PG + PG) - a // PG * PG))
                        for t in range(a, b):
                            last = nc.tensor.transpose(banks[g % 2][:, (t - a) * P:(t - a + 1) * P], prod[:, t, :],
                                                       ident[:])
                        last.then_inc(s_pt, 1)

                    pe.wait_ge(s_w5, 33)
                    turn(0)
                    for g, (a, b) in enumerate(groups):
                        if g + 1 < NG:
                            turn(g + 1)
                        pe.wait_ge(s_ptc, g + 1)
                        if g >= ZB:
                            pe.wait_ge(s_l5, 4 * (g - ZB) + 1)
                        for t in range(a, b):
                            z = banks[2 + g % ZB][:, (t - a) * D:(t - a + 1) * D]
                            nc.tensor.matmul(z, ones_r[:], c3_row[:], start=True, stop=False)
                            last = nc.tensor.matmul(z, prodT[:, g % 2, (t - a) * P:(t - a + 1) * P], v3_sb[:],
                                                    start=False, stop=True)
                        last.then_inc(s_z, 1)

                @block.scalar
                def _(act):
                    nc.scalar.preload_act_table_set("natural_log_exp_and_others")
                    for j, (a, b) in enumerate(groups):
                        act.wait_ge(s_zc, j + 1)
                        part = zmin[:, a:b, :]
                        nc.scalar.activation(part, part, ACT.Exp).then_inc(s_ex, 1)
                        act.wait_ge(s_ex, j + 1)
                        nc.scalar.activation(part, part, ACT.Ln, bias=halves[:], scale=0.5).then_inc(s_lg, 1)
                    act.wait_ge(s_q5, 1)
                    nc.scalar.activation(rstd[:], rstd[:], ACT.Sqrt).then_inc(s_r5, 1)

                @block.vector
                def _(dve):
                    z_of = lambda g: banks[2 + g % ZB][:, 0:(groups[g][1] - groups[g][0]) * D].rearrange(
                        "p (t d) -> p t d", d=D)

                    def copy_turned(g):
                        cols = (groups[g][1] - groups[g][0]) * P
                        dve.wait_ge(s_pt, g + 1)
                        if g >= 2:
                            dve.wait_ge(s_z, g - 1)
                        nc.vector.tensor_copy(prodT[:, g % 2, 0:cols], banks[g % 2][:, 0:cols]).then_inc(s_ptc, 1)

                    def soft_min(g):
                        dve.wait_ge(s_z, g + 1)
                        nc.vector.tensor_scalar(zmin[:, slice(*groups[g]), :], z_of(g), SOFT_MAX, None, ALU.min
                                                ).then_inc(s_zc, 1)

                    def residual(g):
                        sl = slice(*groups[g])
                        dve.wait_ge(s_lg, g + 1)
                        nc.vector.scalar_tensor_tensor(zall[:, sl, :], z_of(g), -LN2, zmin[:, sl, :], ALU.add,
                                                       ALU.max).then_inc(s_l5, 1)
                        dve.wait_ge(s_l5, 4 * g + 1)
                        nc.vector.tensor_tensor(x_sb[:, sl, :], x_sb[:, sl, :], zall[:, sl, :], ALU.add).then_inc(s_l5, 1)
                        dve.wait_ge(s_l5, 4 * g + 2)
                        for t in range(*groups[g]):
                            last = nc.vector.bn_stats(stat[:, t, :], x_sb[:, t, :])
                        last.then_inc(s_l5, 1)
                        dve.wait_ge(s_l5, 4 * g + 3)
                        for t in range(*groups[g]):
                            last = nc.vector.bn_aggr(mom[:, t, :], stat[:, t, :])
                        last.then_inc(s_l5, 1)

                    copy_turned(0)
                    for g in range(NG):
                        if g + 1 < NG:
                            copy_turned(g + 1)
                        if g:
                            residual(g - 1)
                        soft_min(g)
                    residual(NG - 1)
                    dve.wait_ge(s_l5, 4 * NG)
                    nc.vector.tensor_scalar(rstd[:], mom[:, :, 1], EPS, None, ALU.add).then_inc(s_l5, 1)
                    dve.wait_ge(s_l5, 4 * NG + 1)
                    nc.vector.reciprocal(rstd[:], rstd[:]).then_inc(s_q5, 1)
                    dve.wait_ge(s_r5, 1)
                    for t in range(NT):
                        last = nc.vector.tensor_scalar(x_sb[:, t, :], x_sb[:, t, :], mom[:, t, 0:1], rstd[:, t:t + 1],
                                                       ALU.subtract, ALU.mult)
                        if t % 7 == 6:
                            last.then_inc(s_y, 1)


_INS = ["x", "src", "dst", "edge_attr_128", "edge_weight",
        "L0_gnn_W1", "L0_gnn_b1", "L0_gnn_W2", "L0_gnn_b2", "L0_gnn_W3", "L0_gnn_b3",
        "L1_gnn_W1", "L1_gnn_b1", "L1_gnn_W2", "L1_gnn_b2", "L1_gnn_W3", "L1_gnn_b3"]


def kernel(**inputs):
    import concourse.bacc as bacc
    from concourse.bass_utils import run_bass_kernel_spmd

    nc = bacc.Bacc("TRN2", target_bir_lowering=False, num_devices=1)
    arrays, args = {}, []
    for name in _INS:
        a = np.ascontiguousarray(inputs[name])
        arrays[f"in_{name}"] = a
        args.append(nc.dram_tensor(f"in_{name}", a.shape, mybir.dt.from_np(a.dtype), kind="ExternalInput").ap())
    res = nc.dram_tensor("out_x", (N, D), F32, kind="ExternalOutput").ap()
    gnn(nc, *args, res)
    r = run_bass_kernel_spmd(nc, [arrays], core_ids=[0])
    return r.results[0]["out_x"]
```
